# Optimizing a Trainium2 kernel written in Bass

```python
import numpy as np
import jax
import jax.numpy as jnp

def _softmax(x, axis=-1):
    return jax.nn.softmax(x, axis=axis)
def _gelu(x):
    return jax.nn.gelu(x, approximate=True)
def _silu(x):
    return jax.nn.silu(x)
def _sigmoid(x):
    return jax.nn.sigmoid(x)
def _layernorm(x, axis=-1, eps=1e-5):
    m = jnp.mean(x, axis=axis, keepdims=True)
    v = jnp.var(x, axis=axis, keepdims=True)
    return (x - m) / jnp.sqrt(v + eps)
def _scatter_add(tgt, idx, src, axis=0):
    return tgt.at[idx].add(src)
def _segment_sum(src, seg, n):
    return jax.ops.segment_sum(src, seg, n)

kernel_name = 'mk_conv_preact_d4_conv_nchw32_ccf88e'

def setup_inputs(seed: int = 0):
    np.random.seed(seed)
    _w = jnp.asarray
    def _rec_inputs():
        import jax
        import jax.numpy as jnp
        _gk = jax.random.key(seed)
        x = -0.0005207 + 1.001 * jax.random.normal(jax.random.fold_in(_gk, 1), (4, 32, 128, 128), jnp.float32)
        return x
    x = _rec_inputs()
    def _L0_conv_setup():
        import jax, jax.numpy as jnp
        import numpy as np
        import math
        DIM, SCALES, ORIENTS, K = (32, 3, 8, 15)
        SIGMA, GAMMA = (5.0, 0.5)
        B, H, W = (4, 128, 128)

        def _make_gabor_filters():
            coords = np.arange(-(K // 2), K // 2 + 1, dtype=np.float32)
            y, x = np.meshgrid(coords, coords, indexing='ij')
            filts = []
            for s in range(SCALES):
                fu = 1.0 / 2 ** s
                for o in range(ORIENTS):
                    theta = o * math.pi / ORIENTS
                    xt = x * math.cos(theta) + y * math.sin(theta)
                    yt = -x * math.sin(theta) + y * math.cos(theta)
                    env = np.exp(-(xt ** 2 + GAMMA ** 2 * yt ** 2) / (2 * SIGMA ** 2))
                    amp = fu ** 2 / (math.pi * GAMMA ** 2)
                    real = amp * env * np.cos(2 * math.pi * fu * xt)
                    imag = amp * env * np.sin(2 * math.pi * fu * xt)
                    filts.append(np.stack([real, imag]))
            return jnp.asarray(np.stack(filts), dtype=jnp.float32)
        key = jax.random.key(seed)
        k1, k2, k3 = jax.random.split(key, 3)
        x = jax.random.normal(k1, (B, DIM, H, W), dtype=jnp.float32)
        filters = _make_gabor_filters()
        cin = DIM * SCALES * ORIENTS
        w1 = jax.random.normal(k2, (DIM, cin), dtype=jnp.float32) / np.sqrt(cin)
        b1 = jax.random.normal(k3, (DIM,), dtype=jnp.float32) * 0.01
        return {'x': x, 'filters': filters, 'w1': w1, 'b1': b1}
    _L0_conv_all = _L0_conv_setup()
    _L0_conv_in = {k: v for k, v in _L0_conv_all.items() if k in ('filters', 'w1', 'b1', )}
    del _L0_conv_all

    def _L1_conv_setup():
        import jax, jax.numpy as jnp
        import numpy as np
        key = jax.random.key(seed)
        k1, k2 = jax.random.split(key)
        x = jax.random.normal(k1, (8, 32, 252, 252), dtype=jnp.float32)
        weight = jax.random.normal(k2, (32, 32, 5, 5), dtype=jnp.float32)
        return {'x': x, 'weight': weight}
    _L1_conv_all = _L1_conv_setup()
    _L1_conv_in = {k: v for k, v in _L1_conv_all.items() if k in ('weight', )}
    del _L1_conv_all

    def _L2_conv_setup():
        import jax, jax.numpy as jnp
        import numpy as np
        from jax import lax
        B, C, H, W = (16, 32, 384, 384)
        NK = 32
        K = 3
        HID = 128
        key = jax.random.key(seed)
        ks = jax.random.split(key, 5)
        x = jax.random.normal(ks[0], (B, C, H, W), dtype=jnp.float32)
        w1 = jax.random.normal(ks[1], (C, HID), dtype=jnp.float32) * (1.0 / np.sqrt(C))
        b1 = jnp.zeros((HID,), dtype=jnp.float32)
        w2 = jax.random.normal(ks[2], (HID, NK * K * K), dtype=jnp.float32) * (1.0 / np.sqrt(HID))
        b2 = jnp.zeros((NK * K * K,), dtype=jnp.float32)
        return {'x': x, 'w1': w1, 'b1': b1, 'w2': w2, 'b2': b2}
    _L2_conv_all = _L2_conv_setup()
    _L2_conv_in = {k: v for k, v in _L2_conv_all.items() if k in ('w1', 'b1', 'w2', 'b2', )}
    del _L2_conv_all

    def _L3_conv_setup():
        import jax, jax.numpy as jnp
        import numpy as np

        def dht(x):
            X = jnp.fft.fftn(x, axes=(2, 3), norm='ortho')
            return X.real - X.imag

        def _neg_freq(a):
            return jnp.roll(jnp.flip(a, axis=(-2, -1)), shift=(1, 1), axis=(-2, -1))

        def compl_mul2d(x1, x2):
            x1n = _neg_freq(x1)
            x2n = _neg_freq(x2)
            return 0.5 * (jnp.einsum('bixy,ioxy->boxy', x1, x2) - jnp.einsum('bixy,ioxy->boxy', x1n, x2n) + jnp.einsum('bixy,ioxy->boxy', x1, x2n) + jnp.einsum('bixy,ioxy->boxy', x1n, x2))
        key = jax.random.key(seed)
        k1, k2 = jax.random.split(key)
        B, Ci, Co, S, M = (16, 32, 32, 256, 16)
        x = jax.random.normal(k1, (B, Ci, S, S), dtype=jnp.float32)
        scale = 1.0 / (Ci * Co)
        weights1 = scale * jax.random.uniform(k2, (Ci, Co, M, M), dtype=jnp.float32)
        return {'x': x, 'weights1': weights1}
    _L3_conv_all = _L3_conv_setup()
    _L3_conv_in = {k: v for k, v in _L3_conv_all.items() if k in ('weights1', )}
    del _L3_conv_all

    return {
        "x": x,
        "L0_conv_filters": _L0_conv_in["filters"],
        "L0_conv_w1": _L0_conv_in["w1"],
        "L0_conv_b1": _L0_conv_in["b1"],
        "L1_conv_weight": _L1_conv_in["weight"],
        "L2_conv_w1": _L2_conv_in["w1"],
        "L2_conv_b1": _L2_conv_in["b1"],
        "L2_conv_w2": _L2_conv_in["w2"],
        "L2_conv_b2": _L2_conv_in["b2"],
        "L3_conv_weights1": _L3_conv_in["weights1"],
    }

def reference(x, L0_conv_filters, L0_conv_w1, L0_conv_b1, L1_conv_weight, L2_conv_w1, L2_conv_b1, L2_conv_w2, L2_conv_b2, L3_conv_weights1):
    import jax
    import jax.numpy as jnp
    def _L0_conv_ref(x, filters, w1, b1):
        import jax, jax.numpy as jnp
        import numpy as np
        import math
        DIM, SCALES, ORIENTS, K = (32, 3, 8, 15)
        SIGMA, GAMMA = (5.0, 0.5)
        B, H, W = (4, 128, 128)

        def _make_gabor_filters():
            coords = np.arange(-(K // 2), K // 2 + 1, dtype=np.float32)
            y, x = np.meshgrid(coords, coords, indexing='ij')
            filts = []
            for s in range(SCALES):
                fu = 1.0 / 2 ** s
                for o in range(ORIENTS):
                    theta = o * math.pi / ORIENTS
                    xt = x * math.cos(theta) + y * math.sin(theta)
                    yt = -x * math.sin(theta) + y * math.cos(theta)
                    env = np.exp(-(xt ** 2 + GAMMA ** 2 * yt ** 2) / (2 * SIGMA ** 2))
                    amp = fu ** 2 / (math.pi * GAMMA ** 2)
                    real = amp * env * np.cos(2 * math.pi * fu * xt)
                    imag = amp * env * np.sin(2 * math.pi * fu * xt)
                    filts.append(np.stack([real, imag]))
            return jnp.asarray(np.stack(filts), dtype=jnp.float32)
        Bb, C, Hh, Ww = x.shape
        SO = filters.shape[0]
        pad = K // 2
        xr = x.reshape(Bb * C, 1, Hh, Ww)
        kern = filters.reshape(SO * 2, 1, K, K)
        feat = jax.lax.conv_general_dilated(xr, kern, window_strides=(1, 1), padding=[(pad, pad), (pad, pad)], dimension_numbers=('NCHW', 'OIHW', 'NCHW'))
        feat = feat.reshape(Bb, C, SO, 2, Hh, Ww)
        mag = jnp.sqrt(feat[:, :, :, 0] ** 2 + feat[:, :, :, 1] ** 2)
        mag = jnp.swapaxes(mag, -1, -2)
        mag = mag.reshape(Bb, C * SO, Hh, Ww)
        y = jnp.einsum('oc,bchw->bohw', w1, mag) + b1[None, :, None, None]
        mean = y.mean(axis=(2, 3), keepdims=True)
        var = y.var(axis=(2, 3), keepdims=True)
        return (y - mean) / jnp.sqrt(var + 1e-05)

    def _L1_conv_ref(x, weight):
        import jax, jax.numpy as jnp
        import numpy as np
        k = weight.shape[-1]
        p = k // 2
        xp = jnp.pad(x, ((0, 0), (0, 0), (p, p), (p, p)), mode='reflect')
        H, W = (xp.shape[-2], xp.shape[-1])
        wp = jnp.zeros((weight.shape[0], weight.shape[1], H, W), dtype=x.dtype)
        wp = wp.at[:, :, :k, :k].set(weight)
        shift = -k // 2
        wp = jnp.roll(wp, shift=(shift, shift), axis=(-2, -1))
        x_fft = jnp.fft.fft2(xp)
        w_fft = jnp.fft.fft2(wp)
        out_fft = jnp.einsum('bihw,oihw->bohw', x_fft, w_fft)
        out = jnp.fft.ifft2(out_fft).real
        return out[:, :, p:-p, p:-p]

    def _L2_conv_ref(x, w1, b1, w2, b2):
        import jax, jax.numpy as jnp
        import numpy as np
        from jax import lax
        B, C, H, W = (16, 32, 384, 384)
        NK = 32
        K = 3
        HID = 128
        b, c, h, w = x.shape
        pooled = x.mean(axis=(2, 3))
        hdn = jax.nn.relu(pooled @ w1 + b1)
        kernels = (hdn @ w2 + b2).reshape(b, NK, K, K)
        xg = x[:, :NK].reshape(1, b * NK, h, w)
        wgt = kernels.reshape(b * NK, 1, K, K)
        pad = K // 2
        out = lax.conv_general_dilated(xg, wgt, window_strides=(1, 1), padding=[(pad, pad), (pad, pad)], feature_group_count=b * NK, dimension_numbers=('NCHW', 'OIHW', 'NCHW'))
        return out.reshape(b, NK, h, w)

    def _L3_conv_ref(x, weights1):
        import jax, jax.numpy as jnp
        import numpy as np

        def dht(x):
            X = jnp.fft.fftn(x, axes=(2, 3), norm='ortho')
            return X.real - X.imag

        def _neg_freq(a):
            return jnp.roll(jnp.flip(a, axis=(-2, -1)), shift=(1, 1), axis=(-2, -1))

        def compl_mul2d(x1, x2):
            x1n = _neg_freq(x1)
            x2n = _neg_freq(x2)
            return 0.5 * (jnp.einsum('bixy,ioxy->boxy', x1, x2) - jnp.einsum('bixy,ioxy->boxy', x1n, x2n) + jnp.einsum('bixy,ioxy->boxy', x1, x2n) + jnp.einsum('bixy,ioxy->boxy', x1n, x2))
        B = x.shape[0]
        S1, S2 = (x.shape[-2], x.shape[-1])
        Co = weights1.shape[1]
        m1, m2 = (weights1.shape[2], weights1.shape[3])
        x_ht = dht(x)
        res = compl_mul2d(x_ht[:, :, :m1, :m2], weights1)
        out_ht = jnp.zeros((B, Co, S1, S2), dtype=x.dtype).at[:, :, :m1, :m2].set(res)
        return dht(out_ht)

    def _gn(v, G=16, eps=1e-5):
        B_, C_, H_, W_ = v.shape
        g = v.reshape(B_, G, C_ // G, H_, W_)
        m = jnp.mean(g, axis=(2, 3, 4), keepdims=True)
        s = jnp.var(g, axis=(2, 3, 4), keepdims=True)
        return ((g - m) / jnp.sqrt(s + eps)).reshape(v.shape)

    def _ln_c(v, eps=1e-6):
        m = jnp.mean(v, axis=1, keepdims=True)
        s = jnp.var(v, axis=1, keepdims=True)
        return (v - m) / jnp.sqrt(s + eps)

    def _ln_t(v, eps=1e-5):
        m = jnp.mean(v, axis=-1, keepdims=True)
        s = jnp.var(v, axis=-1, keepdims=True)
        return (v - m) / jnp.sqrt(s + eps)

    def _to_tokens(v):
        B_, C_, H_, W_ = v.shape
        return v.reshape(B_, C_, H_ * W_).transpose(0, 2, 1)
    def _from_tokens(t, like):
        B_, C_, H_, W_ = like.shape
        return t.transpose(0, 2, 1).reshape(B_, C_, H_, W_)

    x = x + _L0_conv_ref(_gn(x), L0_conv_filters, L0_conv_w1, L0_conv_b1)
    x = x + _L1_conv_ref(_gn(x), L1_conv_weight)
    x = x + _L2_conv_ref(_gn(x), L2_conv_w1, L2_conv_b1, L2_conv_w2, L2_conv_b2)
    x = x + _L3_conv_ref(_gn(x), L3_conv_weights1)
    return x


_drawn_inputs = setup_inputs


def setup_inputs(seed=0):
    import zlib

    import numpy as np

    out = dict(_drawn_inputs(seed))
    spreads = {'L2_conv_b1': (0.0, 0.8), 'L2_conv_b2': (0.0, 0.8)}
    factors = {'L0_conv_b1': 64.0, 'L2_conv_w1': 29.893, 'L2_conv_w2': 7.686, 'L3_conv_weights1': 64.0}
    for name, (base, spread) in spreads.items():
        noise = np.random.default_rng([zlib.crc32(name.encode()), seed]).standard_normal(out[name].shape)
        drawn = base * np.exp(spread * noise) if base else spread * noise
        out[name] = jnp.asarray(drawn.astype(out[name].dtype))
    for name, factor in factors.items():
        out[name] = (out[name] * factor).astype(out[name].dtype)
    return out
```

```python
import math
from contextlib import ExitStack

import numpy as np

import concourse.bass as bass
from concourse import mybir
from concourse.alu_op_type import AluOpType as ALU

F32 = mybir.dt.float32
F16 = mybir.dt.float16
ACT = mybir.ActivationFunctionType
AX = mybir.AxisListType
ABSMAX = bass.bass_isa.ReduceOp.absmax

B, C, H, W = 4, 32, 128, 128
P = 128
HR, WR = H // 2, W // 2
NPIX = HR * WR
SO = 24
KF = 15
M0 = 4 * SO
TINY = 1e-30
EPS = 1e-5

PADW = WR + 8
ROW = 2 * PADW
PROWS = HR + 7
IMG_RUN = HR * ROW
PLANE = PROWS * ROW + 8
QR = 16
QRUN = QR * ROW
NQ = HR // QR
NG = B * NQ
SLOTS = 4
CQ = C // SLOTS
CHUNK = 512
NCH = NPIX // CHUNK

K1 = 16
K2 = 9
PR1, PC1 = HR + 3, WR + 4
MODES = 16
NPAIR = C // 2
STEPS = 3 * NPAIR
BODY = 3 * SLOTS // 2
AHEAD = BODY
BANKS = 4
TT = NPIX // P


def build(nc, xt, xn, fw, w1, lw, v1, v2, w3, w3n, const, basis, ibasis, out):
    es = ExitStack()
    with es:
        def sb(name, shape, dt=F32, stack=es):
            return stack.enter_context(nc.sbuf_tensor(name, shape, dt))

        def sem(name):
            return es.enter_context(nc.semaphore(name))

        X = sb("X", [P, B * NPIX])
        cst = sb("cst", [P, CONST_COLS])
        yscale = sb("yscale", [P, 1])
        lwh = sb("lwh", [P, K1, P], F16)
        lwl = sb("lwl", [P, K1, P], F16)
        lscale = sb("lscale", [P, 1])
        bst = sb("bst", [P, B * NCH, 6])
        mv = sb("mv", [P, B, 2])
        mom = sb("mom", [P, B, 2])
        red = sb("red", [P, B, 2])
        var = sb("var", [P, B])
        std = sb("std", [P, B])
        rstd = sb("rstd", [P, B])
        shift = sb("shift", [P, B])
        fmax = sb("fmax", [P, SO])
        fall = sb("fall", [P, SO])
        frec = sb("frec", [P, SO])
        frow = sb("frow", [1, 4 * SO])
        frows = sb("frows", [1, 3, P])
        fcol = sb("fcol", [P, 3])
        wmax = sb("wmax", [P, 2])
        wall = sb("wall", [P, 2])
        wrec = sb("wrec", [P, 2])
        wload = sb("wload", [P, NPAIR * 3 * P])
        mv3 = sb("mv3", [P, B, 2])
        zero16 = sb("zero16", [P, P], F16)
        zero32 = sb("zero32", [P, P])
        s0 = ExitStack()
        patch = sb("patch", [P, SLOTS, QR, 2, PADW], F16, s0)
        fws = sb("fws", [P, 4, M0], F32, s0)
        fwh = sb("fwh", [P, 4, M0], F16, s0)
        fwl = sb("fwl", [P, 4, M0], F16, s0)
        w1h = sb("w1h", [P, NPAIR, 3, P], F16, s0)
        w1l = sb("w1l", [P, NPAIR, 3, P], F16, s0)
        w1x = sb("w1x", [P, 2, 2, P], F16, s0)
        HL = sb("HL", [P, HR, 2, PADW], F16, s0)
        sq = sb("sq", [P, 2, 2, CHUNK], F32, s0)
        power = sb("power", [P, 2, CHUNK], F32, s0)
        mag = sb("mag", [P, 2, CHUNK], F32, s0)
        mhl = sb("mhl", [P, 3, 2, CHUNK], F16, s0)
        s0.close()
        s1 = ExitStack()
        xin = sb("xin", [P, 2, NPIX], F32, s1)
        t32 = sb("t32", [P, NPIX], F32, s1)
        PH = sb("PH", [P, 2, 2, PR1, PC1], F16, s1)
        s1.close()
        s2 = ExitStack()
        v1s = sb("v1s", [C, P], F32, s2)
        v2s = sb("v2s", [P, K2, P], F32, s2)
        hid = sb("hid", [P, 1], F32, s2)
        pool = sb("pool", [P, 2], F32, s2)
        k9 = sb("k9", [P, K2], F32, s2)
        kk = sb("kk", [P, K2 * 4], F32, s2)
        kmax = sb("kmax", [P, 1], F32, s2)
        kall = sb("kall", [P, 1], F32, s2)
        krec = sb("krec", [P, 1], F32, s2)
        kscale = sb("kscale", [P, B], F32, s2)
        W2 = sb("W2", [P, K2 * 4, C], F32, s2)
        W2h = sb("W2h", [P, 2, K2, P], F16, s2)
        W2l = sb("W2l", [P, 2, K2, P], F16, s2)
        s2.close()
        s3 = ExitStack()
        bas = sb("bas", [P, 4, 4 * P], F32, s3)
        ibas = sb("ibas", [P, 2, 4, CHUNK], F32, s3)
        xg = sb("xg", [P, 2, B, P], F32, s3)
        xT = sb("xT", [P, 2, B * P], F32, s3)
        G = sb("G", [P, 2, B * C], F32, s3)
        XX = sb("XX", [P, 2, B, 2, C], F32, s3)
        WW = sb("WW", [P, 2, C, 2, C], F32, s3)
        R = sb("R", [P, 2, B, C], F32, s3)
        LL = sb("LL", [P, 4, B, 4, C], F32, s3)
        s4 = ExitStack()
        WL = sb("WL", [P, 2, 2, C * C], F32, s4)
        s4.close()
        prod = sb("prod", [P, 4, C, 2 * C], F32, s3)
        s3.close()

        pc = es.enter_context(nc.psum_tensor("pc", [P, 4, CHUNK], F32))
        py = es.enter_context(nc.psum_tensor("py", [P, 2, CHUNK], F32))
        pn = es.enter_context(nc.psum_tensor("pn", [P, CHUNK], F32))
        pw = es.enter_context(nc.psum_tensor("pw", [P, CHUNK], F32))

        planes = nc.dram_tensor("planes", [P, 4, PLANE], F16)
        planes_ap = planes.ap()

        def cc(name):
            at, n = CONST_AT[name]
            return cst[:, at:at + n]

        const_in = sem("const_in")
        xt_in = [sem(f"xt_in{b}") for b in range(B)]
        fw_in = sem("fw_in")
        w1_in = sem("w1_in")
        lw_in = sem("lw_in")
        zeros_set = sem("zeros_set")
        zeros_out = sem("zeros_out")
        planes_out = sem("planes_out")
        fmax_ready = sem("fmax_ready")
        fall_ready = sem("fall_ready")
        frow_ready = sem("frow_ready")
        fcol_ready = sem("fcol_ready")
        fw_split = sem("fw_split")
        wmax_ready = sem("wmax_ready")
        wall_ready = sem("wall_ready")
        w1_split = sem("w1_split")
        lw_split = sem("lw_split")
        staged = sem("staged")
        patch_in = [sem(f"patch_in{i}") for i in range(SLOTS)]
        conv_done = sem("conv_done")
        square_done = sem("square_done")
        power_done = sem("power_done")
        mag_done = sem("mag_done")
        maghl_done = sem("maghl_done")
        w1x_ready = sem("w1x_ready")
        w1x_free = sem("w1x_free")
        y_ready = sem("y_ready")
        group_stat = sem("group_stat")
        mag_hi = sem("mag_hi")
        filters_ready = sem("filters_ready")
        y_out = sem("y_out")
        moments = sem("moments")
        group_sums = sem("group_sums")
        var_ready = sem("var_ready")
        std_ready = sem("std_ready")
        xn_in = [sem(f"xn_in{i}") for i in range(2)]
        in_done = sem("in_done")
        x1_done = sem("x1_done")
        norm_ready = sem("norm_ready")
        border_clear = sem("border_clear")
        hi_done = sem("hi_done")
        padded = sem("padded")
        chunk_done = sem("chunk_done")
        chunk_out = sem("chunk_out")
        v_in = sem("v_in")
        pool_ready = sem("pool_ready")
        hid_sum = sem("hid_sum")
        hid_ready = sem("hid_ready")
        k_sum = sem("k_sum")
        kmax_ready = sem("kmax_ready")
        kall_ready = sem("kall_ready")
        w3_in = sem("w3_in")
        ww_ready = sem("ww_ready")
        bas_in = [sem(f"bas_in{i}") for i in range(4)]
        ibas_in = [sem(f"ibas_in{i}") for i in range(2)]
        xg_ready = sem("xg_ready")
        xT_done = sem("xT_done")
        xT_out = sem("xT_out")
        spec_tile = sem("spec_tile")
        spec_done = sem("spec_done")
        G_ready = sem("G_ready")
        Gn_ready = sem("Gn_ready")
        XX_ready = sem("XX_ready")
        prod_ready = sem("prod_ready")
        LL_ready = sem("LL_ready")
        inv_done = sem("inv_done")
        inv_out = sem("inv_out")
        saved = sem("saved")
        v_chain = sem("v_chain")
        p_chain = sem("p_chain")

        LASTJOB = 2 + 2 * B
        JOBS = [(1, b) for b in range(B)] + [(2, b) for b in range(B)]

        block = es.enter_context(nc.Block())

        @block.sync
        def _(sp):
            sp.dma_start(cst[:, :], const).then_inc(const_in, 16)
            sp.dma_start(fws[:, :, :].rearrange("p g m -> p (g m)"), fw).then_inc(fw_in, 16)
            for b in range(B):
                sp.dma_start(X[:, b * NPIX:(b + 1) * NPIX], xt[:, b * NPIX:(b + 1) * NPIX]).then_inc(xt_in[b], 16)
                if b == 0:
                    sp.dma_start(wload[:, :], w1).then_inc(w1_in, 16)
            sp.wait_ge(zeros_set, 1)
            for pr in range(2):
                for pcol in range(2):
                    plane = 2 * pr + pcol
                    top = (4 - pr) * ROW - pcol
                    end = top + IMG_RUN
                    flat = HL[:, :, :, :].rearrange("p r h w -> p (r h w)")
                    sp.dma_start(planes_ap[:, plane, 0:top], flat[:, 0:top]).then_inc(zeros_out, 16)
                    sp.dma_start(planes_ap[:, plane, end:PLANE], flat[:, 0:PLANE - end]).then_inc(zeros_out, 16)
            sp.wait_ge(zeros_out, 16 * 8)
            sp.wait_ge(w1_split, 1)
            sp.dma_start(wload[:, 0:K1 * P], lw).then_inc(lw_in, 16)
            for b in range(B):
                sp.wait_ge(planes_out, (b + 1) * 64)
                with sp.Fori(0, NQ) as q:
                    with sp.Fori(0, CQ) as cq:
                        for s in range(SLOTS):
                            sp.wait_ge(conv_done, q * STEPS + cq * BODY
                                       + (b * NQ * STEPS + 3 * (s // 2 - 1) + AHEAD))
                            for plane in range(4):
                                src = bass.AP(planes, cq * (SLOTS * 4 * PLANE) + q * QRUN
                                              + ((b * C + s) * 4 * PLANE + plane * PLANE),
                                              [[ROW, 8], [1, 4], [1, QRUN]])
                                dst = patch[32 * plane:32 * plane + 32, s, :, :, :].rearrange("p r h w -> p (r h w)")
                                sp.dma_start(dst, src).then_inc(patch_in[s], 16)
            sp.wait_ge(y_out, 1 + NG)
            for b in range(B):
                if b >= 2:
                    sp.wait_ge(x1_done, b - 1)
                sp.dma_start(xin[:, b % 2, :], xn[:, b * NPIX:(b + 1) * NPIX]).then_inc(xn_in[b % 2], 16)
            sp.wait_ge(x1_done, B)
            sp.dma_start(v1s[:, :], v1).then_inc(v_in, 16)
            sp.dma_start(v2s[:, :, :].rearrange("p t m -> p (t m)"), v2).then_inc(v_in, 16)
            sp.wait_ge(chunk_out, BANKS + 2 * B * NCH)
            for kt in range(2):
                sp.dma_start(WL[:, kt, 0, :], w3[kt]).then_inc(w3_in, 16)
                sp.dma_start(WL[:, kt, 1, :], w3n[kt]).then_inc(w3_in, 16)
            for s in range(4):
                sp.dma_start(bas[:, s, :], basis[s]).then_inc(bas_in[s], 16)
            for s in range(2):
                sp.dma_start(ibas[:, s, :, :], ibasis[s]).then_inc(ibas_in[s], 16)
            with sp.Fori(1, TT // 4) as t4:
                for s in range(4):
                    sp.wait_ge(spec_tile, 4 * t4 + (s - 3))
                    sp.dma_start(bas[:, s, :], basis[bass.ds(4 * t4 + s, 1)].rearrange("o p n -> (o p) n")
                                 ).then_inc(bas_in[s], 16)
            for n in range(NCH):
                sp.wait_ge(inv_out, B * (n + 1))
                sp.dma_start(out.rearrange("p (b n) -> p b n", b=B)[:, :, n * CHUNK:(n + 1) * CHUNK],
                             X[:, :].rearrange("p (b n) -> p b n", b=B)[:, :, n * CHUNK:(n + 1) * CHUNK]
                             ).then_inc(saved, 16)
                if n + 2 < NCH:
                    sp.dma_start(ibas[:, n % 2, :, :], ibasis[n + 2]).then_inc(ibas_in[n % 2], 16)
            sp.wait_ge(saved, 16 * NCH)

        @block.gpsimd
        def _(gp):
            steps = [0]

            def link(ins):
                steps[0] += 1
                ins.then_inc(p_chain, 1)
                gp.wait_ge(p_chain, steps[0])

            nc.gpsimd.memset(HL[:, :, :, :], 0.0).then_inc(zeros_set, 1)
            nc.gpsimd.memset(zero16[:, :], 0.0)
            nc.gpsimd.memset(zero32[:, :], 0.0).then_inc(zeros_set, 1)
            gp.wait_ge(fmax_ready, 1)
            nc.gpsimd.partition_all_reduce(fall[:, :], fmax[:, :], P, ABSMAX).then_inc(fall_ready, 1)
            gp.wait_ge(wmax_ready, 1)
            nc.gpsimd.partition_all_reduce(wall[:, 0:1], wmax[:, 0:1], P, ABSMAX).then_inc(wall_ready, 1)

            for b in range(B):
                xb = X[:, b * NPIX:(b + 1) * NPIX]
                xb3 = xb.rearrange("p (r w) -> p r w", w=WR)
                hi = HL[:, :, 0, 4:4 + WR]
                lo = HL[:, :, 1, 4:4 + WR]
                if b == 0:
                    gp.wait_ge(staged, 1)
                    gp.wait_ge(zeros_out, 16 * 8)
                else:
                    link(nc.gpsimd.tensor_scalar(xb, xb, rstd[:, b:b + 1], shift[:, b:b + 1], ALU.mult, ALU.add))
                    gp.wait_ge(planes_out, 64 * b)
                    link(nc.gpsimd.tensor_copy(hi, xb3))
                    link(nc.gpsimd.tensor_tensor(lo, xb3, hi, ALU.subtract))
                for a in range(2):
                    for e in range(2):
                        plane = 2 * (1 - a) + (1 - e)
                        at = (3 + a) * ROW - (1 - e)
                        g = 2 * a + e
                        gp.dma_start(planes_ap[b * C:(b + 1) * C, plane, at:at + IMG_RUN],
                                     HL[32 * g:32 * g + 32, :, :, :].rearrange("p r h w -> p (r h w)")
                                     ).then_inc(planes_out, 16)
            gp.wait_ge(wmax_ready, 2)
            nc.gpsimd.partition_all_reduce(wall[:, 1:2], wmax[:, 1:2], P, ABSMAX).then_inc(wall_ready, 1)
            gp.wait_ge(y_out, 1 + NG)
            nc.gpsimd.memset(PH[:, :, :, :, :].rearrange("p k h r w -> p (k h r w)"), 0.0).then_inc(border_clear, 1)
            for b in range(B):
                gp.wait_ge(kmax_ready, b + 1)
                nc.gpsimd.partition_all_reduce(kall[:, :], kmax[:, :], P, ABSMAX).then_inc(kall_ready, 1)
            gp.wait_ge(w3_in, 64)
            for kt in range(2):
                a = WL[:, kt, 0, :].rearrange("p (o i) -> p o i", i=C)
                n = WL[:, kt, 1, :].rearrange("p (o i) -> p o i", i=C)
                link(nc.gpsimd.tensor_tensor(WW[:, kt, :, 0, :], a, n, ALU.add))
                link(nc.gpsimd.tensor_tensor(WW[:, kt, :, 1, :], a, n, ALU.subtract))
            nc.gpsimd.tensor_scalar(WW[:, :, :, :, :].rearrange("p k o t i -> p (k o t i)"),
                                    WW[:, :, :, :, :].rearrange("p k o t i -> p (k o t i)"),
                                    0.5, None, ALU.mult).then_inc(ww_ready, 1)
            gp.wait_ge(ww_ready, 1)
            gp.wait_ge(XX_ready, 2)
            for b in range(B):
                nc.gpsimd.tensor_tensor(
                    prod[:, b, :, :], WW[:, 1, :, :, :].rearrange("p o t i -> p o (t i)"),
                    XX[:, 1, b, :, :].rearrange("p t i -> p (t i)").unsqueeze(1).broadcast_to([P, C, 2 * C]),
                    ALU.mult).then_inc(prod_ready, 1)

        @block.scalar
        def _(act):
            def root(j, n):
                act.wait_ge(var_ready, j + 1)
                nc.scalar.activation(std[:, 0:n], var[:, 0:n], ACT.Sqrt).then_inc(std_ready, 1)

            root(0, B)

            def step(t, k, n=None):
                act.wait_ge(conv_done, t + (1 + AHEAD))
                nc.scalar.activation(sq[:, k % 2, :, :], pc[:, 2 * (k % 2):2 * (k % 2) + 2, :],
                                     ACT.Square).then_inc(square_done, 1)
                act.wait_ge(power_done, t + 1)
                nc.scalar.activation(mag[:, k % 2, :], power[:, k % 2, :], ACT.Sqrt).then_inc(mag_done, 1)

            def group_out(g):
                act.wait_ge(y_ready, g + 1)
                nc.scalar.activation(X[:, bass.ds(g * (2 * CHUNK), 2 * CHUNK)],
                                     py[:, :, :].rearrange("p h n -> p (h n)"), ACT.Identity,
                                     bias=cc("b1"), scale=yscale[:, 0:1]).then_inc(y_out, 1)

            act.wait_ge(const_in, 16)
            act.wait_ge(w1_split, 1)
            step(0, 0)
            step(1, 1)
            with act.Fori(0, NG - 1) as g:
                with act.Fori(0, CQ) as cq:
                    for s in range(BODY):
                        step(g * STEPS + cq * BODY + (s + 2), s + 2)
                group_out(g)
            g = NG - 1
            with act.Fori(0, CQ - 1) as cq:
                for s in range(BODY):
                    step(cq * BODY + (g * STEPS + s + 2), s + 2)
            for s in range(BODY - 2):
                step(g * STEPS + (CQ - 1) * BODY + s + 2, s + 2)
            group_out(g)

            root(1, B)
            act.wait_ge(norm_ready, 1)
            for b in range(B):
                xb = X[:, b * NPIX:(b + 1) * NPIX]
                nc.scalar.activation(xb, xb, ACT.Identity, bias=shift[:, b:b + 1],
                                     scale=rstd[:, b:b + 1]).then_inc(in_done, 1)

            for k, (layer, b) in enumerate(JOBS):
                root(2 + k, 1)
                act.wait_ge(norm_ready, 2 + k)
                if k < 2:
                    act.wait_ge(border_clear, 1)
                else:
                    act.wait_ge(chunk_done, NCH * (k - 1))
                nc.scalar.activation(PH[:, k % 2, 0, 1:1 + HR, 1:1 + WR],
                                     X[:, b * NPIX:(b + 1) * NPIX].rearrange("p (r w) -> p r w", w=WR),
                                     ACT.Identity, bias=shift[:, 0:1], scale=rstd[:, 0:1]).then_inc(hi_done, 1)
            root(LASTJOB, B)
            with act.Fori(0, TT // 2) as t2:
                for s in range(2):
                    act.wait_ge(xT_done, 2 * t2 + (s + 1 + 2))
                    nc.scalar.activation(xT[:, s, :], py[:, s, :], ACT.Identity).then_inc(xT_out, 1)

        @block.vector
        def _(ve):
            steps = [0]

            def link(ins):
                steps[0] += 1
                ins.then_inc(v_chain, 1)
                ve.wait_ge(v_chain, steps[0])

            def batch_stats(b):
                for i in range(NCH):
                    last = nc.vector.bn_stats(bst[:, i, :], X[:, b * NPIX + i * CHUNK:b * NPIX + (i + 1) * CHUNK])
                link(last)

            def aggregate(to, n):
                for i in range(n):
                    last = nc.vector.bn_aggr(to[:, i, :], bst[:, i * NCH:(i + 1) * NCH, :].rearrange("p n s -> p (n s)"))
                link(last)

            def moments_of(mv, n):
                nc.vector.tensor_copy(mom[:, 0:n, 0], mv[:, 0:n, 0])
                link(nc.vector.tensor_tensor(mom[:, 0:n, 1], mv[:, 0:n, 0], mv[:, 0:n, 0], ALU.mult))
                nc.vector.tensor_tensor(mom[:, 0:n, 1], mom[:, 0:n, 1], mv[:, 0:n, 1], ALU.add).then_inc(moments, 1)

            def finish_norm(j, n, done=None):
                ve.wait_ge(group_sums, j + 1)
                link(nc.vector.tensor_copy(red[:, 0:n, :].rearrange("p n s -> p (n s)"), pn[:, 0:2 * n]))
                link(nc.vector.tensor_tensor(var[:, 0:n], red[:, 0:n, 0], red[:, 0:n, 0], ALU.mult))
                link(nc.vector.tensor_tensor(var[:, 0:n], red[:, 0:n, 1], var[:, 0:n], ALU.subtract))
                nc.vector.tensor_scalar(var[:, 0:n], var[:, 0:n], 0.0, EPS, ALU.max, ALU.add).then_inc(var_ready, 1)
                ve.wait_ge(std_ready, j + 1)
                link(nc.vector.reciprocal(rstd[:, 0:n], std[:, 0:n]))
                ins = nc.vector.scalar_tensor_tensor(shift[:, 0:n], red[:, 0:n, 0], -1.0, rstd[:, 0:n],
                                                     ALU.mult, ALU.mult)
                if done is None:
                    link(ins)
                else:
                    ins.then_inc(done, 1)

            ve.wait_ge(fw_in, 16)
            nc.vector.tensor_reduce(fmax[:, :], fws[:, :, :].rearrange("p g (x s) -> p s (g x)", s=SO),
                                    AX.X, ALU.max, apply_absolute_value=True).then_inc(fmax_ready, 1)
            for b in range(B):
                ve.wait_ge(xt_in[b], 16)
                for i in range(NCH):
                    last = nc.vector.bn_stats(bst[:, b * NCH + i, :],
                                              X[:, b * NPIX + i * CHUNK:b * NPIX + (i + 1) * CHUNK])
            link(last)
            aggregate(mv, B)
            moments_of(mv, B)
            ve.wait_ge(fall_ready, 1)
            link(nc.vector.tensor_scalar(fall[:, :], fall[:, :], TINY, None, ALU.max))
            link(nc.vector.reciprocal(frec[:, :], fall[:, :]))
            for i in range(4):
                last = nc.vector.tensor_copy(frow[0:1, i * SO:(i + 1) * SO], fall[0:1, :])
            link(last)
            for j in range(2):
                nc.vector.tensor_copy(frows[0:1, 0, j * 64:(j + 1) * 64], frow[0:1, 0:64])
                nc.vector.tensor_copy(frows[0:1, 1, j * 64:(j + 1) * 64], frow[0:1, 32:M0])
                nc.vector.tensor_copy(frows[0:1, 2, j * 32:(j + 1) * 32], frow[0:1, 64:M0])
                last = nc.vector.tensor_copy(frows[0:1, 2, 64 + j * 32:96 + j * 32], frow[0:1, 0:32])
            last.then_inc(frow_ready, 1)
            link(nc.vector.tensor_tensor(
                fws[:, :, :].rearrange("p g (x s) -> p (g x) s", s=SO),
                fws[:, :, :].rearrange("p g (x s) -> p (g x) s", s=SO),
                frec[:, :].unsqueeze(1).broadcast_to([P, 16, SO]), ALU.mult))
            link(nc.vector.tensor_copy(fwh[:, :, :], fws[:, :, :]))
            nc.vector.tensor_tensor(fwl[:, :, :], fws[:, :, :], fwh[:, :, :], ALU.subtract).then_inc(fw_split, 1)

            finish_norm(0, B)
            xb = X[:, 0:NPIX]
            xb3 = xb.rearrange("p (r w) -> p r w", w=WR)
            link(nc.vector.tensor_scalar(xb, xb, rstd[:, 0:1], shift[:, 0:1], ALU.mult, ALU.add))
            ve.wait_ge(zeros_out, 16 * 8)
            link(nc.vector.tensor_copy(HL[:, :, 0, 4:4 + WR], xb3))
            nc.vector.tensor_tensor(HL[:, :, 1, 4:4 + WR], xb3, HL[:, :, 0, 4:4 + WR], ALU.subtract).then_inc(staged, 1)

            ve.wait_ge(fcol_ready, 1)
            link(nc.vector.tensor_copy(fcol[:, :], pw[:, 0:3]))
            ve.wait_ge(w1_in, 16)
            w1s = wload[:, :].rearrange("p (n t m) -> p n t m", n=NPAIR, t=3)
            for i in range(3):
                last = nc.vector.tensor_scalar(w1s[:, :, i, :], w1s[:, :, i, :], fcol[:, i:i + 1], None, ALU.mult)
            link(last)
            nc.vector.tensor_reduce(wmax[:, 0:1], wload[:, :], AX.X, ALU.max,
                                    apply_absolute_value=True).then_inc(wmax_ready, 1)
            ve.wait_ge(wall_ready, 1)
            link(nc.vector.tensor_scalar(yscale[:, :], wall[:, 0:1], TINY, None, ALU.max))
            link(nc.vector.reciprocal(wrec[:, 0:1], yscale[:, :]))
            link(nc.vector.tensor_scalar(wload[:, :], wload[:, :], wrec[:, 0:1], None, ALU.mult))
            flat_h = w1h[:, :, :, :].rearrange("p n t m -> p (n t m)")
            link(nc.vector.tensor_copy(flat_h, wload[:, :]))
            nc.vector.tensor_tensor(w1l[:, :, :, :].rearrange("p n t m -> p (n t m)"), wload[:, :], flat_h,
                                    ALU.subtract).then_inc(w1_split, 1)
            ve.wait_ge(lw_in, 16)
            wl = wload[:, 0:K1 * P]
            nc.vector.tensor_reduce(wmax[:, 1:2], wl, AX.X, ALU.max, apply_absolute_value=True).then_inc(wmax_ready, 1)

            def step(g, cq, k):
                t = g * STEPS + cq * BODY + k
                if k % 3 == 2:
                    pair = k // 3
                    ve.wait_ge(w1x_free, g * NPAIR + cq * 2 + (pair + 1))
                    for i, wt in enumerate((w1h, w1l)):
                        nc.vector.tensor_copy(w1x[:, pair, i, :],
                                              wt[:, bass.ds(cq * 2 + pair, 1), 2, :].rearrange("p o m -> p (o m)")
                                              ).then_inc(w1x_ready, 1)
                ve.wait_ge(square_done, t + 1)
                nc.vector.tensor_tensor(power[:, k % 2, :], sq[:, k % 2, 0, :], sq[:, k % 2, 1, :],
                                        ALU.add).then_inc(power_done, 1)
                ve.wait_ge(mag_done, t + 1)
                nc.vector.tensor_copy(mhl[:, k % 3, 0, :], mag[:, k % 2, :]).then_inc(mag_hi, 1)
                ve.wait_ge(mag_hi, t + 1)
                nc.vector.tensor_tensor(mhl[:, k % 3, 1, :], mag[:, k % 2, :], mhl[:, k % 3, 0, :],
                                        ALU.subtract).then_inc(maghl_done, 1)

            def group_stats(g):
                ve.wait_ge(y_out, g + 2)
                for i in range(2):
                    nc.vector.bn_stats(bst[:, bass.ds(g * 2 + i, 1), :].rearrange("p o s -> p (o s)"),
                                       X[:, bass.ds(g * (2 * CHUNK) + i * CHUNK, CHUNK)]).then_inc(group_stat, 1)

            step(0, 0, 0)
            step(0, 0, 1)
            with ve.Fori(0, NG - 1) as g:
                with ve.Fori(0, CQ) as cq:
                    for s in range(BODY):
                        step(g, cq, s + 2)
                group_stats(g)
            g = NG - 1
            with ve.Fori(0, CQ - 1) as cq:
                for s in range(BODY):
                    step(g, cq, s + 2)
            for s in range(BODY - 2):
                step(g, CQ - 1, s + 2)
            group_stats(g)
            ve.wait_ge(group_stat, 2 * NG)

            ve.wait_ge(wall_ready, 2)
            link(nc.vector.tensor_scalar(lscale[:, :], wall[:, 1:2], TINY, None, ALU.max))
            link(nc.vector.reciprocal(wrec[:, 1:2], lscale[:, :]))
            link(nc.vector.tensor_scalar(wl, wl, wrec[:, 1:2], None, ALU.mult))
            link(nc.vector.tensor_copy(lwh[:, :, :].rearrange("p s m -> p (s m)"), wl))
            nc.vector.tensor_tensor(lwl[:, :, :].rearrange("p s m -> p (s m)"), wl,
                                    lwh[:, :, :].rearrange("p s m -> p (s m)"), ALU.subtract).then_inc(lw_split, 1)
            aggregate(mv, B)
            moments_of(mv, B)
            finish_norm(1, B, norm_ready)

            for b in range(B):
                ve.wait_ge(xn_in[b % 2], 16 * (b // 2 + 1))
                ve.wait_ge(in_done, b + 1)
                xb = X[:, b * NPIX:(b + 1) * NPIX]
                nc.vector.tensor_tensor(xb, xb, xin[:, b % 2, :], ALU.add).then_inc(x1_done, 1)
            ve.wait_ge(x1_done, B)

            def prepare(k):
                layer, b = JOBS[k]
                s = k % 2
                if layer == 2:
                    ve.wait_ge(chunk_out, BANKS + NCH * (b + 1))
                batch_stats(b)
                aggregate(mv, 1)
                moments_of(mv, 1)
                finish_norm(2 + k, 1, norm_ready)
                ve.wait_ge(norm_ready, 2 + k)
                if layer == 2:
                    nc.vector.tensor_scalar(pool[:, 0:1], pn[:, 2:3], rstd[:, 0:1], shift[:, 0:1],
                                            ALU.mult, ALU.add).then_inc(pool_ready, 1)
                    filters(k)
                if k < 2:
                    ve.wait_ge(border_clear, 1)
                else:
                    ve.wait_ge(chunk_done, NCH * (k - 1))
                    if k in (B, B + 1):
                        for r0, r1 in ((0, 1), (1 + HR, PR1)):
                            link(nc.vector.memset(PH[:, s, :, r0:r1, :], 0.0))
                        for c0, c1 in ((0, 1), (1 + WR, PC1)):
                            link(nc.vector.memset(PH[:, s, :, :, c0:c1], 0.0))
                xb = X[:, b * NPIX:(b + 1) * NPIX]
                link(nc.vector.tensor_scalar(t32[:, :], xb, rstd[:, 0:1], shift[:, 0:1], ALU.mult, ALU.add))
                ve.wait_ge(hi_done, k + 1)
                hi = PH[:, s, 0, 1:1 + HR, 1:1 + WR]
                lo = PH[:, s, 1, 1:1 + HR, 1:1 + WR]
                ins = nc.vector.tensor_tensor(lo, t32[:, :].rearrange("p (r w) -> p r w", w=WR), hi, ALU.subtract)
                if layer == 2:
                    ins.then_inc(padded, 1)
                    return
                link(ins)
                rows = PH[:, s, :, :, :]
                nc.vector.tensor_copy(rows[:, :, 0, 1:1 + WR], rows[:, :, 1, 1:1 + WR])
                nc.vector.tensor_copy(rows[0:64, :, HR + 1, 1:1 + WR], rows[0:64, :, HR, 1:1 + WR])
                nc.vector.tensor_copy(rows[64:128, :, HR + 1, 1:1 + WR], rows[64:128, :, HR - 1, 1:1 + WR])
                link(nc.vector.tensor_copy(rows[:, :, HR + 2, 1:1 + WR], rows[:, :, 2, 1:1 + WR]))
                nc.vector.tensor_copy(rows[:, :, :, 0], rows[:, :, :, 1])
                for g in range(4):
                    q = rows[32 * g:32 * g + 32]
                    nc.vector.tensor_copy(q[:, :, :, WR + 1], q[:, :, :, WR - g % 2])
                nc.vector.tensor_copy(rows[:, :, :, WR + 2], rows[:, :, :, 2]).then_inc(padded, 1)

            def filters(k):
                b = JOBS[k][1]
                if b == 0:
                    ve.wait_ge(v_in, 32)
                ve.wait_ge(hid_sum, b + 1)
                nc.vector.tensor_scalar(hid[:, :], pw[:, 8:9], cc("vb1"), 0.0, ALU.add, ALU.max).then_inc(hid_ready, 1)
                ve.wait_ge(k_sum, b + 1)
                link(nc.vector.tensor_tensor(k9[:, :], pw[:, 16:16 + K2], cc("vb2"), ALU.add))
                nc.vector.tensor_reduce(kmax[:, :], k9[:, :], AX.X, ALU.max,
                                        apply_absolute_value=True).then_inc(kmax_ready, 1)
                ve.wait_ge(kall_ready, b + 1)
                link(nc.vector.tensor_scalar(kscale[:, b:b + 1], kall[:, :], TINY, None, ALU.max))
                link(nc.vector.reciprocal(krec[:, :], kscale[:, b:b + 1]))
                link(nc.vector.tensor_scalar(k9[:, :], k9[:, :], krec[:, 0:1], None, ALU.mult))
                masks = cc("taps").rearrange("p (t n) -> p t n", t=K2)
                link(nc.vector.tensor_scalar(kk[:, :], masks[:, 0, :], k9[:, 0:1], None, ALU.mult))
                for t in range(1, K2):
                    link(nc.vector.scalar_tensor_tensor(kk[:, :], masks[:, t, :], k9[:, t:t + 1], kk[:, :],
                                                        ALU.mult, ALU.add))
                link(nc.vector.tensor_tensor(
                    W2[:, :, :], kk[:, :].unsqueeze(2).broadcast_to([P, 4 * K2, C]),
                    cc("chan").unsqueeze(1).broadcast_to([P, 4 * K2, C]), ALU.mult))
                flat = W2[:, :, :].rearrange("p n c -> p (n c)")
                fh = W2h[:, b % 2, :, :].rearrange("p s m -> p (s m)")
                link(nc.vector.tensor_copy(fh, flat))
                nc.vector.tensor_tensor(W2l[:, b % 2, :, :].rearrange("p s m -> p (s m)"), flat, fh,
                                        ALU.subtract).then_inc(filters_ready, 1)

            def evict(k):
                layer, b = JOBS[k]
                scale = lscale[:, 0:1] if layer == 1 else kscale[:, b:b + 1]
                for n in range(NCH):
                    ve.wait_ge(chunk_done, NCH * k + n + 1)
                    xc = X[:, b * NPIX + n * CHUNK:b * NPIX + (n + 1) * CHUNK]
                    nc.vector.scalar_tensor_tensor(xc, pc[:, n % 4, :], scale, xc, ALU.mult,
                                                   ALU.add).then_inc(chunk_out, 1)

            prepare(0)
            prepare(1)
            evict(0)
            for k in range(2, 2 * B + 1):
                if k < 2 * B:
                    prepare(k)
                evict(k - 1)
                if k > B:
                    b = k - 1 - B
                    ve.wait_ge(chunk_out, BANKS + NCH * k)
                    batch_stats(b)
                    link(nc.vector.bn_aggr(mv3[:, b, :], bst[:, 0:NCH, :].rearrange("p n s -> p (n s)")))

            moments_of(mv3, B)
            finish_norm(LASTJOB, B)
            with ve.Fori(0, TT // 2) as t2:
                for s in range(2):
                    ve.wait_ge(xT_done, 2 * t2 + (s + 1))
                    for b in range(B):
                        last = nc.vector.tensor_scalar(xg[:, s, b, :], X[:, bass.ds(t2 * (2 * P) + (b * NPIX + s * P), P)],
                                                       rstd[:, b:b + 1], shift[:, b:b + 1], ALU.mult, ALU.add)
                    last.then_inc(xg_ready, 1)
            ve.wait_ge(spec_done, 1)
            cosw = cc("cosw").rearrange("p (k g) -> p k g", k=2)
            sinw = cc("sinw").rearrange("p (k g) -> p k g", k=2)
            for kt in range(2):
                gk = G[:, kt, :].rearrange("p (b c) -> p b c", b=B)
                for sgn in range(2):
                    tab = sinw if sgn else cosw
                    acc = pc[:, 2 * sgn + kt, :].rearrange("p (b g c) -> p b g c", b=B, g=4)
                    for g in range(4):
                        if sgn == 0 and g == 0:
                            ins = nc.vector.tensor_scalar(gk, acc[:, :, g, :], tab[:, kt, g:g + 1], None, ALU.mult)
                        else:
                            ins = nc.vector.scalar_tensor_tensor(gk, acc[:, :, g, :], tab[:, kt, g:g + 1], gk,
                                                                 ALU.mult, ALU.add)
                        if sgn == 1 and g == 3:
                            ins.then_inc(G_ready, 1)
                        else:
                            link(ins)
            ve.wait_ge(G_ready, 2)
            ve.wait_ge(Gn_ready, 1)
            for kt in (1, 0):
                nc.vector.tensor_copy(XX[:, kt, :, 0, :], G[:, kt, :].rearrange("p (b c) -> p b c", b=B))
                nc.vector.tensor_copy(XX[:, kt, :, 1, :],
                                      pn[:, kt * P:(kt + 1) * P].rearrange("p (b c) -> p b c", b=B)
                                      ).then_inc(XX_ready, 1)
            ve.wait_ge(XX_ready, 2)
            ve.wait_ge(ww_ready, 1)
            for b in range(B):
                ve.wait_ge(prod_ready, b + 1)
                link(nc.vector.tensor_reduce(R[:, 1, b, :], prod[:, b, :, :], AX.X, ALU.add))
                link(nc.vector.tensor_tensor(
                    prod[:, b, :, :], WW[:, 0, :, :, :].rearrange("p o t i -> p o (t i)"),
                    XX[:, 0, b, :, :].rearrange("p t i -> p (t i)").unsqueeze(1).broadcast_to([P, C, 2 * C]),
                    ALU.mult))
                link(nc.vector.tensor_reduce(R[:, 0, b, :], prod[:, b, :, :], AX.X, ALU.add))
            for sgn in range(2):
                tab = sinw if sgn else cosw
                for kt in range(2):
                    for g in range(4):
                        last = nc.vector.tensor_scalar(LL[:, 2 * sgn + kt, :, g, :], R[:, kt, :, :],
                                                       tab[:, kt, g:g + 1], None, ALU.mult)
            last.then_inc(LL_ready, 1)
            for n in range(NCH):
                for b in range(B):
                    i = n * B + b
                    ve.wait_ge(inv_done, i + 1)
                    xc = X[:, b * NPIX + n * CHUNK:b * NPIX + (n + 1) * CHUNK]
                    nc.vector.tensor_tensor(xc, xc, pc[:, i % 4, :], ALU.add).then_inc(inv_out, 1)

        @block.tensor
        def _(pe):
            nc.tensor.sem_inc(conv_done, AHEAD)
            nc.tensor.sem_inc(chunk_out, BANKS)
            nc.tensor.sem_inc(w1x_free, 2)
            nc.tensor.sem_inc(y_out, 1)
            nc.tensor.sem_inc(xT_done, 2)

            def stats(j, n, pooled=False):
                pe.wait_ge(moments, j + 1)
                ins = nc.tensor.matmul(pn[:, 0:2 * n], cc("channel" if j == 1 else "group"),
                                       mom[:, 0:n, :].rearrange("p n s -> p (n s)"), start=True, stop=True)
                if pooled:
                    ins = nc.tensor.matmul(pn[:, 2:4], cc("channel"), mom[:, 0:1, :].rearrange("p n s -> p (n s)"),
                                           start=True, stop=True)
                ins.then_inc(group_sums, 1)

            pe.wait_ge(const_in, 16)
            stats(0, B)
            pe.wait_ge(frow_ready, 1)
            for i in range(3):
                last = nc.tensor.matmul(pw[:, i:i + 1], frows[0:1, i, :], cc("one")[0:1, :], start=True, stop=True)
            last.then_inc(fcol_ready, 1)
            pe.wait_ge(fw_split, 1)
            pe.wait_ge(w1_split, 1)
            pe.wait_ge(zeros_set, 2)

            def conv(k, quad):
                pair, kind = k // 3, k % 3
                slot = [(2 * pair + j) % SLOTS for j in range(2)]
                if kind == 0:
                    for j in range(2):
                        pe.wait_ge(patch_in[slot[j]], quad * 64 + 64)
                if kind < 2:
                    tiles = [(64 * j, 32 * kind, 64, slot[j], kind) for j in range(2)]
                else:
                    tiles = [(32 * j, (64, 0)[j // 2], 32, slot[j % 2], j // 2) for j in range(4)]
                for ri in range(2):
                    mm = 0
                    for kt in range(2):
                        for wt, h in ((fwh, 0), (fwh, 1), (fwl, 0)):
                            for at, first, n, sl, half in tiles:
                                last = nc.tensor.matmul(
                                    pc[at:at + n, 2 * (k % 2) + ri, :], wt[:, 2 * kt + ri, first:first + n],
                                    patch[:, sl, 8 * half:8 * half + 8, h, 4 * kt:4 * kt + WR],
                                    start=(mm == 0), stop=(mm == 5))
                            mm += 1
                last.then_inc(conv_done, 1)

            def mix(g, cq, k):
                pe.wait_ge(maghl_done, g * STEPS + cq * BODY + (k + 1))
                pair, kind = k // 3, k % 3
                if kind < 2:
                    for wt, h in ((w1h, 0), (w1h, 1), (w1l, 0)):
                        lhs = wt[:, bass.ds(cq * 2 + pair, 1), kind, :].rearrange("p o m -> p (o m)")
                        nc.tensor.matmul(py[:, kind, :], lhs, mhl[:, k % 3, h, :], start=False, stop=False)
                else:
                    pe.wait_ge(w1x_ready, g * (2 * NPAIR) + cq * 4 + (2 * pair + 2))
                    for i, h in ((0, 0), (0, 1), (1, 0)):
                        for half, to in ((0, slice(64, 128)), (1, slice(0, 64))):
                            last = nc.tensor.matmul(py[to, half, :], w1x[:, pair, i, to], mhl[:, k % 3, h, :],
                                                    start=False, stop=False)
                    last.then_inc(w1x_free, 1)

            def zeros(to, start, stop):
                return nc.tensor.matmul(to, zero16[:, :], zero16[:, :].unsqueeze(1).broadcast_to([P, 4, P]),
                                        start=start, stop=stop)

            def step(g, cq, s, ahead=True):
                if ahead:
                    pe.wait_ge(square_done, g * STEPS + cq * BODY + (s + 1))
                    conv(s + 2, g * CQ + cq + (s + 2) // BODY)
                mix(g, cq, s)

            def open_sum(g):
                pe.wait_ge(y_out, g + 1)
                for h in range(2):
                    zeros(py[:, h, :], True, False)

            def close_sum():
                for h in range(2):
                    last = zeros(py[:, h, :], False, True)
                last.then_inc(y_ready, 1)

            conv(0, 0)
            conv(1, 0)
            with pe.Fori(0, NG - 1) as g:
                open_sum(g)
                with pe.Fori(0, CQ) as cq:
                    for s in range(BODY):
                        step(g, cq, s)
                close_sum()
            g = NG - 1
            open_sum(g)
            with pe.Fori(0, CQ - 1) as cq:
                for s in range(BODY):
                    step(g, cq, s)
            for s in range(BODY):
                step(g, CQ - 1, s, ahead=s < BODY - 2)
            close_sum()
            stats(1, B)

            pe.wait_ge(lw_split, 1)

            def block_conv(k, half):
                layer, b = JOBS[k]
                side = 4 if layer == 1 else 3
                if half == 0:
                    pe.wait_ge(padded, k + 1)
                    if layer == 2:
                        pe.wait_ge(filters_ready, b + 1)
                with pe.Fori(0, BANKS) as i:
                    pe.wait_ge(chunk_out, i + (NCH * k + BANKS * half + 1))
                    mm, total = 0, 3 * side * side
                    for s in range(side * side):
                        sy, sx = s // side - 1, s % side - 1
                        if layer == 1:
                            hi, lo = lwh[:, s, :], lwl[:, s, :]
                        else:
                            hi, lo = W2h[:, b % 2, s, :], W2l[:, b % 2, s, :]
                        for wt, h in ((hi, 0), (hi, 1), (lo, 0)):
                            last = nc.tensor.matmul(
                                pc[:, bass.ds(i, 1), :].rearrange("p o n -> p (o n)"), wt,
                                PH[:, k % 2, h, bass.ds(i * 8 + (half * 32 + 1 + sy), 8), 1 + sx:1 + sx + WR],
                                start=(mm == 0), stop=(mm == total - 1))
                            mm += 1
                    last.then_inc(chunk_done, 1)

            def filter_net(k):
                b = JOBS[k][1]
                if b == 0:
                    pe.wait_ge(v_in, 32)
                pe.wait_ge(pool_ready, b + 1)
                nc.tensor.matmul(pw[:, 8:9], v1s[:, :], pool[0:C, 0:1], start=True, stop=True).then_inc(hid_sum, 1)
                pe.wait_ge(hid_ready, b + 1)
                for t in range(K2):
                    last = nc.tensor.matmul(pw[:, 16 + t:17 + t], v2s[:, t, :], hid[:, :], start=True, stop=True)
                last.then_inc(k_sum, 1)

            stats(2, 1)
            for k in range(2 * B):
                block_conv(k, 0)
                if k + 1 < 2 * B:
                    stats(3 + k, 1, pooled=k + 1 >= B)
                    if k + 1 >= B:
                        filter_net(k + 1)
                block_conv(k, 1)
            stats(LASTJOB, B)

            pe.wait_ge(chunk_out, BANKS + 2 * B * NCH)
            for m in range(4):
                zeros(pc[:, m, :], True, False)

            def transposes(t, s):
                pe.wait_ge(xg_ready, t + 1)
                for b in range(B):
                    last = nc.tensor.transpose(py[:, s % 2, b * P:(b + 1) * P], xg[:, s % 2, b, :], cc("ident"))
                last.then_inc(xT_done, 1)

            def spectrum(t, s, t4):
                pe.wait_ge(xT_out, t + 1)
                pe.wait_ge(bas_in[s], t4 * 16 + 16)
                for m in range(4):
                    last = nc.tensor.matmul(pc[:, m, :], bas[:, s, m * P:(m + 1) * P], xT[:, s % 2, :],
                                            start=False, stop=False)
                last.then_inc(spec_tile, 1)

            transposes(0, 0)
            with pe.Fori(0, TT // 4 - 1) as t4:
                for s in range(4):
                    transposes(t4 * 4 + (s + 1), (s + 1) % 4)
                    spectrum(t4 * 4 + s, s, t4)
            t4 = TT // 4 - 1
            for s in range(4):
                if s < 3:
                    transposes(t4 * 4 + s + 1, s + 1)
                spectrum(t4 * 4 + s, s, t4)
            for m in range(4):
                last = zeros(pc[:, m, :], False, True)
            last.then_inc(spec_done, 1)
            pe.wait_ge(G_ready, 2)
            perm = cc("mirror").rearrange("p (i o m) -> p i o m", i=2, o=2)
            for o in range(2):
                for i in range(2):
                    last = nc.tensor.matmul(pn[:, o * P:(o + 1) * P], perm[:, i, o, :], G[:, i, :],
                                            start=(i == 0), stop=(i == 1))
            last.then_inc(Gn_ready, 1)
            pe.wait_ge(LL_ready, 1)
            for n in range(NCH):
                pe.wait_ge(ibas_in[n % 2], 16 * (n // 2 + 1))
                for b in range(B):
                    i = n * B + b
                    if i >= 4:
                        pe.wait_ge(inv_out, i - 3)
                    for m in range(4):
                        last = nc.tensor.matmul(pc[:, i % 4, :], LL[:, m, b, :, :].rearrange("p g o -> p (g o)"),
                                                ibas[:, n % 2, m, :], start=(m == 0), stop=(m == 3))
                    last.then_inc(inv_done, 1)


def _const_columns():
    widths = [("group", P), ("channel", P), ("ident", P), ("mirror", 4 * P), ("taps", K2 * 4 * K2), ("chan", C),
              ("cosw", 8), ("sinw", 8), ("one", 1), ("b1", 1), ("vb1", 1), ("vb2", K2)]
    at, where = 0, {}
    for name, n in widths:
        where[name] = (at, n)
        at += n
    return where, at


CONST_AT, CONST_COLS = _const_columns()


def _shape_constants():
    p = np.arange(P)
    chan, ph = p % C, p // C
    parts = {}
    parts["group"] = (chan[:, None] // 2 == chan[None, :] // 2) / 8.0
    parts["channel"] = (chan[:, None] == chan[None, :]) / 4.0
    parts["ident"] = np.eye(P)
    parts["chan"] = (chan[:, None] == np.arange(C)[None, :]) * 1.0
    parts["one"] = np.ones((P, 1))
    m = np.arange(MODES * MODES)
    minus = (-(m // MODES)) % MODES * MODES + (-(m % MODES)) % MODES
    full = np.zeros((2 * P, 2 * P))
    full[minus, m] = 1.0
    parts["mirror"] = full.reshape(2, P, 2, P).transpose(1, 0, 2, 3).reshape(P, 4 * P)
    taps = np.zeros((P, K2, K2, 2, 2))
    for q in range(4):
        for s in range(K2):
            for a in range(2):
                for e in range(2):
                    dy = 2 * (s // 3 - 1) + q // 2 - a + 1
                    dx = 2 * (s % 3 - 1) + q % 2 - e + 1
                    if 0 <= dy < 3 and 0 <= dx < 3:
                        taps[ph == q, 3 * dy + dx, s, a, e] = 1.0
    parts["taps"] = taps.reshape(P, -1)
    k1, k2 = (m // MODES).reshape(2, P), (m % MODES).reshape(2, P)
    for name, f in (("cosw", np.cos), ("sinw", np.sin)):
        table = [[f(2 * math.pi * (k1[kt] * (g // 2) + k2[kt] * (g % 2)) / H) / H for g in range(4)] for kt in range(2)]
        parts[name] = np.array(table).transpose(2, 0, 1).reshape(P, 8)
    return parts


def _bases():
    m = np.arange(MODES * MODES)
    pos = np.arange(NPIX)
    turns = (m[:, None] // MODES * (pos[None, :] // WR) + m[:, None] % MODES * (pos[None, :] % WR)) % HR
    angle = 2 * math.pi * turns / HR
    cas = np.stack([np.cos(angle) + np.sin(angle), np.cos(angle) - np.sin(angle)]).reshape(4, P, NPIX)
    basis = cas.reshape(4 * P, TT, P).transpose(1, 2, 0)
    ibasis = cas.reshape(4, P, NCH, CHUNK).transpose(2, 1, 0, 3).reshape(NCH, P, 4 * CHUNK)
    return np.ascontiguousarray(basis, np.float32), np.ascontiguousarray(ibasis, np.float32)


def _phases(v):
    v = v.reshape(B, C, HR, 2, WR, 2).transpose(3, 5, 1, 0, 2, 4)
    return np.ascontiguousarray(v).reshape(P, B * NPIX)


def _filters(f):
    out = np.zeros((P, 2, 2, 2, 2, SO), f.dtype)
    for p in range(P):
        i2, plane, j2 = p // 4 % 8, p // 32, p % 4
        i, j = 2 * i2 + plane // 2, 2 * j2 + plane % 2
        for kt in range(2):
            for a in range(2):
                for e in range(2):
                    dx, dy = i - a, 8 * kt + j - e
                    if 0 <= dx < KF and 0 <= dy < KF:
                        out[p, kt, :, a, e, :] = f[:, :, dy, dx].T
    return out.reshape(P, 4 * M0)


def _mix(w):
    one = np.zeros((C, 4, SO, 4, C), w.dtype)
    for g in range(4):
        one[:, g, :, g, :] = w.reshape(C, C, SO).transpose(1, 2, 0)
    rows = one.reshape(NPAIR, 2, M0, P).transpose(1, 2, 0, 3)
    out = np.empty((P, NPAIR, 3, P), w.dtype)
    out[:, :, 0] = rows[:, :64].reshape(P, NPAIR, P)
    out[:, :, 1] = rows[:, 32:].reshape(P, NPAIR, P)
    out[:64, :, 2] = rows[:, 64:].reshape(64, NPAIR, P)
    out[64:, :, 2] = rows[:, :32].reshape(64, NPAIR, P)
    return out.reshape(P, NPAIR * 3 * P)


def _blocks(w):
    out = np.zeros((2, 2, C, 4, 4, 2, 2, C), w.dtype)
    for a in range(2):
        for e in range(2):
            for sy in range(4):
                for sx in range(4):
                    for oa in range(2):
                        for oe in range(2):
                            i = 3 - (2 * (sy - 1) + a - oa)
                            j = 3 - (2 * (sx - 1) + e - oe)
                            if 0 <= i < 5 and 0 <= j < 5:
                                out[a, e, :, sy, sx, oa, oe, :] = w[:, :, i, j].T
    return out.reshape(P, K1 * P)


def _modes(w):
    n = np.roll(np.flip(w, (-2, -1)), (1, 1), (-2, -1))
    return [np.ascontiguousarray(v.transpose(2, 3, 1, 0)).reshape(2, P, C * C) for v in (w, n)]


def kernel(x, L0_conv_filters, L0_conv_w1, L0_conv_b1, L1_conv_weight, L2_conv_w1, L2_conv_b1, L2_conv_w2,
           L2_conv_b2, L3_conv_weights1):
    import concourse.bacc as bacc
    from concourse.bass_utils import run_bass_kernel_spmd

    x = np.asarray(x)
    parts = _shape_constants()
    parts["b1"] = np.tile(np.asarray(L0_conv_b1), 4)[:, None]
    parts["vb1"] = np.asarray(L2_conv_b1)[:, None]
    parts["vb2"] = np.tile(np.asarray(L2_conv_b2).reshape(C, K2), (4, 1))
    const = np.zeros((P, CONST_COLS), np.float32)
    for name, (at, n) in CONST_AT.items():
        const[:, at:at + n] = parts[name]
    basis, ibasis = _bases()
    w3, w3n = _modes(np.asarray(L3_conv_weights1))
    arrays = {
        "xt": _phases(x.transpose(0, 1, 3, 2)),
        "xn": _phases(x),
        "fw": _filters(np.asarray(L0_conv_filters)),
        "w1": _mix(np.asarray(L0_conv_w1)),
        "lw": _blocks(np.asarray(L1_conv_weight)),
        "v1": np.ascontiguousarray(L2_conv_w1),
        "v2": np.ascontiguousarray(np.tile(np.asarray(L2_conv_w2).reshape(P, C, K2).transpose(0, 2, 1),
                                           (1, 1, 4))).reshape(P, K2 * P),
        "w3": w3,
        "w3n": w3n,
        "const": const,
        "basis": basis,
        "ibasis": ibasis,
    }
    nc = bacc.Bacc("TRN2", target_bir_lowering=False, num_devices=1)
    t = {n: nc.dram_tensor(n, a.shape, F32, kind="ExternalInput").ap() for n, a in arrays.items()}
    out = nc.dram_tensor("out", (P, B * NPIX), F32, kind="ExternalOutput").ap()
    build(nc, t["xt"], t["xn"], t["fw"], t["w1"], t["lw"], t["v1"], t["v2"], t["w3"], t["w3n"],
          t["const"], t["basis"], t["ibasis"], out)
    r = run_bass_kernel_spmd(nc, [arrays], core_ids=[0])
    got = r.results[0]["out"].reshape(2, 2, C, B, HR, WR).transpose(3, 2, 4, 0, 5, 1)
    return np.ascontiguousarray(got).reshape(B, C, H, W)
```

```python
import math
from contextlib import ExitStack

import numpy as np

import concourse.bass as bass
from concourse import mybir
from concourse.alu_op_type import AluOpType as ALU

F32 = mybir.dt.float32
F16 = mybir.dt.float16
ACT = mybir.ActivationFunctionType
AX = mybir.AxisListType
ABSMAX = bass.bass_isa.ReduceOp.absmax

B, C, H, W = 4, 32, 128, 128
P = 128
HR, WR = H // 2, W // 2
NPIX = HR * WR
SO = 24
KF = 15
M0 = 4 * SO
TINY = 1e-30
EPS = 1e-5

PADW = WR + 8
ROW = 2 * PADW
PROWS = HR + 7
IMG_RUN = HR * ROW
PLANE = PROWS * ROW + 8
QR = 16
QRUN = QR * ROW
NQ = HR // QR
NG = B * NQ
SLOTS = 4
CQ = C // SLOTS
CHUNK = 512
NCH = NPIX // CHUNK

K1 = 9
K2 = 6
TAPS = 9
TILES = {1: [(i, 7) for i in range(0, 63, 7)] + [(63, 2)],
         2: [(i, 8) for i in range(0, 64, 8)] + [(64, 1)]}
PR1, PC1 = HR + 3, WR + 4
MODES = 16
NPAIR = C // 2
STEPS = 3 * NPAIR
BODY = 3 * SLOTS // 2
HALVES = 2
AHEAD = HALVES * BODY
FREE = 10
TT = NPIX // P
IBAS = 5
INVERSE = [(b, n) for n0, n1 in ((0, IBAS), (IBAS, NCH)) for b in range(B) for n in range(n0, n1)]


def build(nc, xt, xn, fw, w1, lw, v1, v2, w3, w3n, const, basis, ibasis, out):
    es = ExitStack()
    with es:
        def sb(name, shape, dt=F32, stack=es):
            return stack.enter_context(nc.sbuf_tensor(name, shape, dt))

        def sem(name):
            return es.enter_context(nc.semaphore(name))

        X = sb("X", [P, B * NPIX])
        cst = sb("cst", [P, CONST_COLS])
        yscale = sb("yscale", [P, 1])
        lwh = sb("lwh", [P, K1, P], F16)
        lwl = sb("lwl", [P, K1, P], F16)
        lscale = sb("lscale", [P, 1])
        bst = sb("bst", [P, B * NCH, 6])
        mv = sb("mv", [P, B, 2])
        mom = sb("mom", [P, B, 2])
        red = sb("red", [P, B, 2])
        var = sb("var", [P, B])
        std = sb("std", [P, B])
        rstd = sb("rstd", [P, B])
        shift = sb("shift", [P, B])
        fmax = sb("fmax", [P, SO])
        fall = sb("fall", [P, SO])
        frec = sb("frec", [P, SO])
        frow = sb("frow", [1, 4 * SO])
        frows = sb("frows", [1, 3, P])
        fcol = sb("fcol", [P, 3])
        wmax = sb("wmax", [P, 2])
        wall = sb("wall", [P, 2])
        wrec = sb("wrec", [P, 2])
        wload = sb("wload", [P, NPAIR * 3 * P])
        HL = sb("HL", [P, HR, 2, PADW], F16)
        mv3 = sb("mv3", [P, B, 2])
        zero16 = sb("zero16", [P, P], F16)
        zero32 = sb("zero32", [P, P])
        s0 = ExitStack()
        norm0 = sb("norm0", [P, NPIX], F32, s0)
        s0.close()
        sq = sb("sq", [P, 2, 2, CHUNK], F32, s0)
        power = sb("power", [P, 2, CHUNK], F32, s0)
        mag = sb("mag", [P, 2, CHUNK], F32, s0)
        mhl = sb("mhl", [P, BODY, 2, CHUNK], F16, s0)
        patch = sb("patch", [P, SLOTS, QR, 2, PADW], F16, s0)
        fws = sb("fws", [P, 4, M0], F32, s0)
        fwx = sb("fwx", [P, 2, 2, 384], F16, s0)
        w1h = sb("w1h", [P, NPAIR, 3, P], F16, s0)
        w1l = sb("w1l", [P, NPAIR, 3, P], F16, s0)
        w1x = sb("w1x", [P, 2, 2, P], F16, s0)
        zpad = sb("zpad", [P, PLANE - IMG_RUN - 3 * ROW + 8], F16, s0)
        s0.close()
        s1 = ExitStack()
        t32 = sb("t32", [P, NPIX], F32, s1)
        PH = sb("PH", [P, 2, 2, PR1, PC1], F16, s1)
        s2 = ExitStack()
        v1s = sb("v1s", [C, P], F32, s2)
        v2s = sb("v2s", [P, TAPS, P], F32, s2)
        hid = sb("hid", [P, 1], F32, s2)
        pool = sb("pool", [P, 2], F32, s2)
        k9 = sb("k9", [P, TAPS], F32, s2)
        kk = sb("kk", [P, K2 * 4], F32, s2)
        kmax = sb("kmax", [P, 1], F32, s2)
        kall = sb("kall", [P, 1], F32, s2)
        krec = sb("krec", [P, 1], F32, s2)
        kscale = sb("kscale", [P, B], F32, s2)
        W2 = sb("W2", [P, K2 * 4, C], F32, s2)
        W2h = sb("W2h", [P, 2, K2, P], F16, s2)
        W2l = sb("W2l", [P, 2, K2, P], F16, s2)
        s2.close()
        s1.close()
        s3 = ExitStack()
        G = sb("G", [P, 2, B * C], F32, s3)
        XX = sb("XX", [P, 2, B, 2, C], F32, s3)
        WW = sb("WW", [P, 2, C, 2, C], F32, s3)
        R = sb("R", [P, 2, B, C], F32, s3)
        LL = sb("LL", [P, 2, 2, 4, C], F32, s3)
        LLhl = sb("LLhl", [P, B, 2, 4, 4 * C], F16, s3)
        w3max = sb("w3max", [P, 1], F32, s3)
        w3all = sb("w3all", [P, 1], F32, s3)
        w3rec = sb("w3rec", [P, 1], F32, s3)
        oscale = sb("oscale", [P, 1], F32, s3)
        ident16 = sb("ident16", [P, P], F16, s3)
        s4 = ExitStack()
        WL = sb("WL", [P, 2, 2, C * C], F32, s4)
        bas = sb("bas", [P, 4, 2, 4 * P], F16, s4)
        xg = sb("xg", [P, 2, B, P], F32, s4)
        xhl = sb("xhl", [P, 2, 2, B * P], F16, s4)
        xT = sb("xT", [P, 2, 2 * B * P], F16, s4)
        s4.close()
        prod = sb("prod", [P, B, C, 2 * C], F32, s3)
        prod0 = sb("prod0", [P, C, 2 * C], F32, s3)
        s3.close()

        hl_flat = HL[:, :, :, :].rearrange("p r h w -> p (r h w)").bitcast(F32)
        xin = [hl_flat[:, 0:NPIX], wload[:, 0:NPIX]]
        ibas = [v.bitcast(F16).rearrange("p (h m n) -> p h m n", h=2, m=4)
                for v in [hl_flat[:, i * 4 * CHUNK:(i + 1) * 4 * CHUNK] for i in range(2)]
                + [wload[:, i * 4 * CHUNK:(i + 1) * 4 * CHUNK] for i in range(IBAS - 2)]]

        pc = es.enter_context(nc.psum_tensor("pc", [P, 4, CHUNK], F32))
        py = es.enter_context(nc.psum_tensor("py", [P, 2, CHUNK], F32))
        pn = es.enter_context(nc.psum_tensor("pn", [P, CHUNK], F32))
        pw = es.enter_context(nc.psum_tensor("pw", [P, CHUNK], F32))

        py16 = py[:, :, :].bitcast(F16)

        planes = nc.dram_tensor("planes", [P, 4, PLANE], F16)
        planes_ap = planes.ap()

        def bank(i):
            return pc[:, i % 4, :] if i < 8 else py[:, i - 8, :]

        def cc(name):
            at, n = CONST_AT[name]
            return cst[:, at:at + n]

        const_in = sem("const_in")
        xt_in = [sem(f"xt_in{b}") for b in range(B)]
        fw_in = sem("fw_in")
        w1_in = sem("w1_in")
        lw_in = sem("lw_in")
        zeros_set = sem("zeros_set")
        zeros_out = sem("zeros_out")
        first_planes = [sem(f"first_planes{i}") for i in range(2)]
        planes_out = sem("planes_out")
        fmax_ready = sem("fmax_ready")
        fall_ready = sem("fall_ready")
        frow_ready = sem("frow_ready")
        fcol_ready = sem("fcol_ready")
        fw_split = sem("fw_split")
        wmax_ready = sem("wmax_ready")
        wall_ready = sem("wall_ready")
        wrec_ready = sem("wrec_ready")
        w1_hi = sem("w1_hi")
        w1_split = sem("w1_split")
        lw_split = sem("lw_split")
        first_hi = sem("first_hi")
        staged = sem("staged")
        patch_in = [sem(f"patch_in{i}") for i in range(SLOTS)]
        conv_done = sem("conv_done")
        square_done = sem("square_done")
        power_done = sem("power_done")
        mag_done = sem("mag_done")
        maghl_done = sem("maghl_done")
        w1x_ready = sem("w1x_ready")
        w1x_free = sem("w1x_free")
        y_ready = sem("y_ready")
        group_stat = sem("group_stat")
        mag_hi = sem("mag_hi")
        filters_ready = sem("filters_ready")
        y_out = sem("y_out")
        moments = sem("moments")
        group_sums = sem("group_sums")
        var_ready = sem("var_ready")
        std_ready = sem("std_ready")
        xn_in = [sem(f"xn_in{i}") for i in range(2)]
        in_done = sem("in_done")
        x1_done = sem("x1_done")
        norm_ready = sem("norm_ready")
        hi_done = sem("hi_done")
        bordered = sem("bordered")
        tile_done = sem("tile_done")
        tile_out = sem("tile_out")
        lo_done = sem("lo_done")
        lw_scale = sem("lw_scale")
        v_in = sem("v_in")
        pool_ready = sem("pool_ready")
        hid_sum = sem("hid_sum")
        hid_ready = sem("hid_ready")
        k_sum = sem("k_sum")
        kmax_ready = sem("kmax_ready")
        kall_ready = sem("kall_ready")
        w3_in = sem("w3_in")
        ww_ready = sem("ww_ready")
        bas_in = [sem(f"bas_in{i}") for i in range(4)]
        ibas_in = [sem(f"ibas_in{i}") for i in range(IBAS)]
        w3max_ready = sem("w3max_ready")
        w3all_ready = sem("w3all_ready")
        w3rec_ready = sem("w3rec_ready")
        ident_ready = sem("ident_ready")
        xg_norm = sem("xg_norm")
        xg_hi = sem("xg_hi")
        xg_ready = sem("xg_ready")
        xT_done = sem("xT_done")
        xT_out = sem("xT_out")
        spec_tile = sem("spec_tile")
        spec_done = sem("spec_done")
        G_ready = sem("G_ready")
        Gn_ready = sem("Gn_ready")
        XX_ready = sem("XX_ready")
        prod_ready = sem("prod_ready")
        LL_ready = sem("LL_ready")
        inv_done = sem("inv_done")
        inv_out = sem("inv_out")
        saved = sem("saved")
        v_chain = sem("v_chain")
        p_chain = sem("p_chain")

        INJOB = 4
        LASTJOB = INJOB + 2 * B

        def job(k):
            return INJOB - 1 if k == 0 else INJOB + k

        RUNS = [(0, NG - NQ), (NG - NQ, NG - NQ + 1), (NG - NQ + 1, NG - NQ + 2), (NG - NQ + 2, NG - 1)]
        JOBS = [(1, b) for b in range(B)] + [(2, b) for b in range(B)]

        TILES_BEFORE = [sum(len(TILES[layer]) for layer, _ in JOBS[:k]) for k in range(2 * B + 1)]

        block = es.enter_context(nc.Block())

        @block.sync
        def _(sp):
            sp.dma_start(fws[:, :, :].rearrange("p g m -> p (g m)"), fw).then_inc(fw_in, 16)
            sp.dma_start(X[:, 0:NPIX], xt[:, 0:NPIX]).then_inc(xt_in[0], 16)
            sp.dma_start(cst[:, :], const).then_inc(const_in, 16)
            sp.dma_start(wload[:, :], w1).then_inc(w1_in, 16)
            for b in range(1, B):
                sp.dma_start(X[:, b * NPIX:(b + 1) * NPIX], xt[:, b * NPIX:(b + 1) * NPIX]).then_inc(xt_in[b], 16)
            sp.wait_ge(zeros_set, 2)
            for pr in range(2):
                for pcol in range(2):
                    plane = 2 * pr + pcol
                    top = (4 - pr) * ROW - pcol
                    end = top + IMG_RUN
                    sp.dma_start(planes_ap[:, plane, 0:top], zpad[:, 0:top]).then_inc(zeros_out, 16)
                    sp.dma_start(planes_ap[:, plane, end:PLANE], zpad[:, 0:PLANE - end]).then_inc(zeros_out, 16)
            for half in range(2):
                sp.wait_ge(staged, half + 1)
                rows = slice(half * HR // 2, (half + 1) * HR // 2)
                for a in range(2):
                    for e in range(2):
                        plane = 2 * (1 - a) + (1 - e)
                        at = (3 + a) * ROW - (1 - e) + half * IMG_RUN // 2
                        g = 2 * a + e
                        sp.dma_start(planes_ap[0:C, plane, at:at + IMG_RUN // 2],
                                     HL[32 * g:32 * g + 32, rows, :, :].rearrange("p r h w -> p (r h w)")
                                     ).then_inc(first_planes[half], 16)
            sp.wait_ge(zeros_out, 16 * 8)
            sp.wait_ge(w1_split, 1)
            sp.dma_start(wload[:, 0:K1 * P], lw).then_inc(lw_in, 16)
            for b, q0, q1 in [(0, 0, 1), (0, 1, NQ)] + [(b, 0, NQ) for b in range(1, B)]:
                if b == 0:
                    sp.wait_ge(first_planes[q0], 64)
                else:
                    sp.wait_ge(planes_out, b * 64)
                if b == B - 1:
                    sp.dma_start(xin[0], xn[:, 0:NPIX]).then_inc(xn_in[0], 16)
                    sp.wait_ge(lw_split, 1)
                    sp.dma_start(xin[1], xn[:, NPIX:2 * NPIX]).then_inc(xn_in[1], 16)
                with sp.Fori(q0, q1) as q:
                    with sp.Fori(0, CQ) as cq:
                        for s in range(SLOTS):
                            sp.wait_ge(conv_done, q * (HALVES * STEPS) + cq * (HALVES * BODY)
                                       + (HALVES * (b * NQ * STEPS + 3 * (s // 2 - 1)) + AHEAD))
                            for plane in range(4):
                                src = bass.AP(planes, cq * (SLOTS * 4 * PLANE) + q * QRUN
                                              + ((b * C + s) * 4 * PLANE + plane * PLANE),
                                              [[ROW, 8], [1, 4], [1, QRUN]])
                                dst = patch[32 * plane:32 * plane + 32, s, :, :, :].rearrange("p r h w -> p (r h w)")
                                sp.dma_start(dst, src).then_inc(patch_in[s], 16)
            for b in range(2, B):
                sp.wait_ge(x1_done, b - 1)
                sp.dma_start(xin[b % 2], xn[:, b * NPIX:(b + 1) * NPIX]).then_inc(xn_in[b % 2], 16)
            sp.wait_ge(y_out, NG + 1)
            sp.dma_start(v1s[:, :], v1).then_inc(v_in, 16)
            sp.dma_start(v2s[:, :, :].rearrange("p t m -> p (t m)"), v2).then_inc(v_in, 16)
            sp.wait_ge(tile_out, FREE + TILES_BEFORE[2 * B])
            for kt in range(2):
                sp.dma_start(WL[:, kt, 0, :], w3[kt]).then_inc(w3_in, 16)
                sp.dma_start(WL[:, kt, 1, :], w3n[kt]).then_inc(w3_in, 16)
            for s in range(4):
                sp.dma_start(bas[:, s, :, :].rearrange("p h n -> p (h n)"), basis[s]).then_inc(bas_in[s], 16)
            for s in range(IBAS):
                sp.dma_start(ibas[s].rearrange("p h m n -> p (h m n)"), ibasis[s]).then_inc(ibas_in[s], 16)
            with sp.Fori(1, TT // 4) as t4:
                for s in range(4):
                    sp.wait_ge(spec_tile, 4 * t4 + (s - 3))
                    sp.dma_start(bas[:, s, :, :].rearrange("p h n -> p (h n)"),
                                 basis[bass.ds(4 * t4 + s, 1)].rearrange("o p n -> (o p) n")
                                 ).then_inc(bas_in[s], 16)
            for i, (b, n) in enumerate(INVERSE):
                sp.wait_ge(inv_out, i + 1)
                if b == B - 1 and n + IBAS < NCH:
                    sp.dma_start(ibas[n].rearrange("p h m n -> p (h m n)"), ibasis[n + IBAS]
                                 ).then_inc(ibas_in[n], 16)
                cols = slice(b * NPIX + n * CHUNK, b * NPIX + (n + 1) * CHUNK)
                sp.dma_start(out[:, cols], X[:, cols]).then_inc(saved, 16)
            sp.wait_ge(saved, 16 * len(INVERSE))

        @block.gpsimd
        def _(gp):
            steps = [0]

            def link(ins):
                steps[0] += 1
                ins.then_inc(p_chain, 1)
                gp.wait_ge(p_chain, steps[0])

            nc.gpsimd.memset(zero16[:, :], 0.0).then_inc(zeros_set, 1)
            gp.wait_ge(fmax_ready, 1)
            nc.gpsimd.partition_all_reduce(fall[:, :], fmax[:, :], P, ABSMAX).then_inc(fall_ready, 1)
            for i in range(2):
                gp.wait_ge(wmax_ready, i + 1)
                nc.gpsimd.partition_all_reduce(wall[:, i:i + 1], wmax[:, i:i + 1], P, ABSMAX).then_inc(wall_ready, 1)
            gp.wait_ge(norm_ready, 2)
            for b in range(1, B):
                xb = X[:, b * NPIX:(b + 1) * NPIX]
                xb3 = xb.rearrange("p (r w) -> p r w", w=WR)
                hi = HL[:, :, 0, 4:4 + WR]
                lo = HL[:, :, 1, 4:4 + WR]
                link(nc.gpsimd.tensor_scalar(xb, xb, rstd[:, b:b + 1], shift[:, b:b + 1], ALU.mult, ALU.add))
                if b == 1:
                    for half in range(2):
                        gp.wait_ge(first_planes[half], 64)
                else:
                    gp.wait_ge(planes_out, 64 * (b - 1))
                link(nc.gpsimd.tensor_copy(hi, xb3))
                link(nc.gpsimd.tensor_tensor(lo, xb3, hi, ALU.subtract))
                for a in range(2):
                    for e in range(2):
                        plane = 2 * (1 - a) + (1 - e)
                        at = (3 + a) * ROW - (1 - e)
                        g = 2 * a + e
                        gp.dma_start(planes_ap[b * C:(b + 1) * C, plane, at:at + IMG_RUN],
                                     HL[32 * g:32 * g + 32, :, :, :].rearrange("p r h w -> p (r h w)")
                                     ).then_inc(planes_out, 16)
            gp.wait_ge(lw_scale, 1)
            wl = wload[:, 0:K1 * P]
            flat_h = lwh[:, :, :].rearrange("p s m -> p (s m)")
            link(nc.gpsimd.tensor_scalar(wl, wl, wrec[:, 1:2], None, ALU.mult))
            link(nc.gpsimd.tensor_copy(flat_h, wl))
            nc.gpsimd.tensor_tensor(lwl[:, :, :].rearrange("p s m -> p (s m)"), wl, flat_h,
                                    ALU.subtract).then_inc(lw_split, 1)
            gp.wait_ge(norm_ready, 3)
            for b in range(2):
                xb = X[:, b * NPIX:(b + 1) * NPIX]
                gp.wait_ge(xn_in[b], 16)
                link(nc.gpsimd.tensor_scalar(xb, xb, rstd[:, b:b + 1], shift[:, b:b + 1], ALU.mult, ALU.add))
                nc.gpsimd.tensor_tensor(xb, xb, xin[b], ALU.add).then_inc(x1_done, 1)

            def low_part(k):
                layer, b = JOBS[k]
                s = k % 2
                if k > 0:
                    gp.wait_ge(hi_done, 2 * (k + 1))
                    nc.gpsimd.tensor_tensor(PH[:, s, 1, 1:1 + HR, 1:1 + WR],
                                            t32[:, :].rearrange("p (r w) -> p r w", w=WR),
                                            PH[:, s, 0, 1:1 + HR, 1:1 + WR], ALU.subtract).then_inc(lo_done, 1)
                rows = PH[:, s, :, :, :]
                if k >= B + 2:
                    return
                if layer == 2:
                    link(nc.gpsimd.memset(rows[:, :, 0:1, :], 0.0))
                    link(nc.gpsimd.memset(rows[:, :, 1 + HR:PR1, :], 0.0))
                    link(nc.gpsimd.memset(rows[:, :, :, 0:1], 0.0))
                    nc.gpsimd.memset(rows[:, :, :, 1 + WR:PC1], 0.0).then_inc(bordered, 1)
                    return
                gp.wait_ge(lo_done, k + 1)
                link(nc.gpsimd.tensor_copy(rows[:, :, 0, 1:1 + WR], rows[:, :, 1, 1:1 + WR]))
                link(nc.gpsimd.tensor_copy(rows[0:64, :, HR + 1, 1:1 + WR], rows[0:64, :, HR, 1:1 + WR]))
                link(nc.gpsimd.tensor_copy(rows[64:128, :, HR + 1, 1:1 + WR], rows[64:128, :, HR - 1, 1:1 + WR]))
                link(nc.gpsimd.tensor_copy(rows[:, :, HR + 2, 1:1 + WR], rows[:, :, 2, 1:1 + WR]))
                link(nc.gpsimd.tensor_copy(rows[:, :, :, 0], rows[:, :, :, 1]))
                for g in range(4):
                    q = rows[32 * g:32 * g + 32]
                    link(nc.gpsimd.tensor_copy(q[:, :, :, WR + 1], q[:, :, :, WR - g % 2]))
                nc.gpsimd.tensor_copy(rows[:, :, :, WR + 2], rows[:, :, :, 2]).then_inc(bordered, 1)

            for k in range(2 * B):
                if k >= B:
                    gp.wait_ge(kmax_ready, k - B + 1)
                    nc.gpsimd.partition_all_reduce(kall[:, :], kmax[:, :], P, ABSMAX).then_inc(kall_ready, 1)
                low_part(k)
            gp.wait_ge(w3_in, 64)
            for kt in range(2):
                a = WL[:, kt, 0, :].rearrange("p (o i) -> p o i", i=C)
                n = WL[:, kt, 1, :].rearrange("p (o i) -> p o i", i=C)
                link(nc.gpsimd.tensor_tensor(WW[:, kt, :, 0, :], a, n, ALU.add))
                link(nc.gpsimd.tensor_tensor(WW[:, kt, :, 1, :], a, n, ALU.subtract))
            gp.wait_ge(w3max_ready, 1)
            nc.gpsimd.partition_all_reduce(w3all[:, :], w3max[:, :], P, ABSMAX).then_inc(w3all_ready, 1)
            gp.wait_ge(w3rec_ready, 1)
            flat = WW[:, :, :, :, :].rearrange("p k o t i -> p (k o t i)")
            nc.gpsimd.tensor_scalar(flat, flat, w3rec[:, 0:1], 0.5, ALU.mult, ALU.mult).then_inc(ww_ready, 1)
            gp.wait_ge(ww_ready, 1)
            gp.wait_ge(XX_ready, 1)
            for b in range(B):
                nc.gpsimd.tensor_tensor(
                    prod[:, b, :, :], WW[:, 1, :, :, :].rearrange("p o t i -> p o (t i)"),
                    XX[:, 1, b, :, :].rearrange("p t i -> p (t i)").unsqueeze(1).broadcast_to([P, C, 2 * C]),
                    ALU.mult).then_inc(prod_ready, 1)

        @block.scalar
        def _(act):
            def root(j, n):
                act.wait_ge(var_ready, j + 1)
                nc.scalar.activation(std[:, 0:n], var[:, 0:n], ACT.Sqrt).then_inc(std_ready, 1)

            root(0, 1)
            act.wait_ge(norm_ready, 1)
            for half in range(2):
                rows = slice(half * HR // 2, (half + 1) * HR // 2)
                nc.scalar.activation(HL[:, rows, 0, 4:4 + WR],
                                     X[:, 0:NPIX].rearrange("p (r w) -> p r w", w=WR)[:, rows, :], ACT.Identity,
                                     bias=shift[:, 0:1], scale=rstd[:, 0:1]).then_inc(first_hi, 1)
            act.wait_ge(wrec_ready, 1)
            nc.scalar.activation(w1h[:, :, :, :].rearrange("p n t m -> p (n t m)"), wload[:, :], ACT.Identity,
                                 scale=wrec[:, 0:1]).then_inc(w1_hi, 1)
            root(1, B - 1)

            def square(t, k):
                for i in range(HALVES):
                    act.wait_ge(conv_done, t * HALVES + (i + 1 + AHEAD))
                    acc = pc[:, 2 * (k % 2) + i, :]
                    nc.scalar.activation(sq[:, k % 2, i, :], acc, ACT.Square)
                    nc.scalar.activation(acc, acc, ACT.Square).then_inc(square_done, 1)

            def root_of(t, k):
                act.wait_ge(power_done, t * HALVES + HALVES)
                nc.scalar.activation(mag[:, k % 2, :], power[:, k % 2, :], ACT.Sqrt).then_inc(mag_done, 1)

            def group_out(g):
                act.wait_ge(y_ready, g + 1)
                nc.scalar.activation(X[:, bass.ds(g * (2 * CHUNK), 2 * CHUNK)],
                                     py[:, :, :].rearrange("p h n -> p (h n)"), ACT.Identity,
                                     bias=cc("b1"), scale=yscale[:, 0:1]).then_inc(y_out, 1)

            act.wait_ge(const_in, 16)
            act.wait_ge(w1_split, 1)
            square(0, 0)
            square(1, 1)
            root_of(0, 0)
            square(2, 2)
            for run, (g0, g1) in enumerate(RUNS):
                with act.Fori(g0, g1) as g:
                    with act.Fori(0, CQ) as cq:
                        for s in range(BODY):
                            root_of(g * STEPS + cq * BODY + (s + 1), s + 1)
                            square(g * STEPS + cq * BODY + (s + 3), s + 3)
                    group_out(g)
                if run == 1:
                    root(2, B - 1)
                if run == 3:
                    root(3, 1)
            g = NG - 1
            with act.Fori(0, CQ - 1) as cq:
                for s in range(BODY):
                    root_of(cq * BODY + (g * STEPS + s + 1), s + 1)
                    square(cq * BODY + (g * STEPS + s + 3), s + 3)
            for s in range(BODY - 1):
                root_of(g * STEPS + (CQ - 1) * BODY + s + 1, s + 1)
                if s < BODY - 3:
                    square(g * STEPS + (CQ - 1) * BODY + s + 3, s + 3)
            group_out(g)

            def high_part(k):
                b = JOBS[k][1]
                if k:
                    root(job(k), 1)
                act.wait_ge(norm_ready, job(k) + 1)
                if k >= 2:
                    act.wait_ge(tile_done, TILES_BEFORE[k - 1])
                if k >= 1:
                    act.wait_ge(lo_done, k)
                xb = X[:, b * NPIX:(b + 1) * NPIX]
                nc.scalar.activation(PH[:, k % 2, 0, 1:1 + HR, 1:1 + WR], xb.rearrange("p (r w) -> p r w", w=WR),
                                     ACT.Identity, bias=shift[:, 0:1], scale=rstd[:, 0:1]).then_inc(hi_done, 1)
                nc.scalar.activation(t32[:, :], xb, ACT.Identity, bias=shift[:, 0:1],
                                     scale=rstd[:, 0:1]).then_inc(hi_done, 1)

            high_part(0)
            root(INJOB, 1)
            act.wait_ge(norm_ready, INJOB + 1)
            for b in range(2, B):
                xb = X[:, b * NPIX:(b + 1) * NPIX]
                nc.scalar.activation(xb, xb, ACT.Identity, bias=shift[:, b:b + 1],
                                     scale=rstd[:, b:b + 1]).then_inc(in_done, 1)
            for k in range(1, 2 * B):
                high_part(k)
            root(LASTJOB, B)
            with act.Fori(0, TT // 2) as t2:
                for s in range(2):
                    act.wait_ge(xT_done, 2 * t2 + (s + 1 + 2))
                    nc.scalar.activation(xT[:, s, :], py16[:, s, :], ACT.Identity).then_inc(xT_out, 1)

        @block.vector
        def _(ve):
            steps = [0]

            def link(ins):
                steps[0] += 1
                ins.then_inc(v_chain, 1)
                ve.wait_ge(v_chain, steps[0])

            def batch_stats(b):
                for i in range(NCH):
                    last = nc.vector.bn_stats(bst[:, i, :], X[:, b * NPIX + i * CHUNK:b * NPIX + (i + 1) * CHUNK])
                link(last)

            def aggregate(to, n):
                for i in range(n):
                    last = nc.vector.bn_aggr(to[:, i, :], bst[:, i * NCH:(i + 1) * NCH, :].rearrange("p n s -> p (n s)"))
                link(last)

            def moments_of(mv, n):
                nc.vector.tensor_copy(mom[:, 0:n, 0], mv[:, 0:n, 0])
                link(nc.vector.tensor_tensor(mom[:, 0:n, 1], mv[:, 0:n, 0], mv[:, 0:n, 0], ALU.mult))
                nc.vector.tensor_tensor(mom[:, 0:n, 1], mom[:, 0:n, 1], mv[:, 0:n, 1], ALU.add).then_inc(moments, 1)

            def finish_norm(j, n, done=None, first=0):
                r, sh = rstd[:, first:first + n], shift[:, first:first + n]
                ve.wait_ge(group_sums, j + 1)
                link(nc.vector.tensor_copy(red[:, 0:n, :].rearrange("p n s -> p (n s)"), pn[:, 0:2 * n]))
                link(nc.vector.tensor_tensor(var[:, 0:n], red[:, 0:n, 0], red[:, 0:n, 0], ALU.mult))
                link(nc.vector.tensor_tensor(var[:, 0:n], red[:, 0:n, 1], var[:, 0:n], ALU.subtract))
                nc.vector.tensor_scalar(var[:, 0:n], var[:, 0:n], 0.0, EPS, ALU.max, ALU.add).then_inc(var_ready, 1)
                ve.wait_ge(std_ready, j + 1)
                link(nc.vector.reciprocal(r, std[:, 0:n]))
                ins = nc.vector.scalar_tensor_tensor(sh, red[:, 0:n, 0], -1.0, r, ALU.mult, ALU.mult)
                if done is None:
                    link(ins)
                else:
                    ins.then_inc(done, 1)

            nc.vector.memset(zpad[:, :], 0.0).then_inc(zeros_set, 1)
            link(nc.vector.memset(HL[:, :, :, :].rearrange("p r h w -> p (r h w)").bitcast(F32), 0.0))
            ve.wait_ge(fw_in, 16)
            nc.vector.tensor_reduce(fmax[:, :], fws[:, :, :].rearrange("p g (x s) -> p s (g x)", s=SO),
                                    AX.X, ALU.max, apply_absolute_value=True).then_inc(fmax_ready, 1)
            ve.wait_ge(xt_in[0], 16)
            batch_stats(0)
            aggregate(mv, 1)
            moments_of(mv, 1)
            ve.wait_ge(fall_ready, 1)
            link(nc.vector.tensor_scalar(fall[:, :], fall[:, :], TINY, None, ALU.max))
            link(nc.vector.reciprocal(frec[:, :], fall[:, :]))
            for i in range(4):
                last = nc.vector.tensor_copy(frow[0:1, i * SO:(i + 1) * SO], fall[0:1, :])
            link(last)
            for j in range(2):
                nc.vector.tensor_copy(frows[0:1, 0, j * 64:(j + 1) * 64], frow[0:1, 0:64])
                nc.vector.tensor_copy(frows[0:1, 1, j * 64:(j + 1) * 64], frow[0:1, 32:M0])
                nc.vector.tensor_copy(frows[0:1, 2, j * 32:(j + 1) * 32], frow[0:1, 64:M0])
                last = nc.vector.tensor_copy(frows[0:1, 2, 64 + j * 32:96 + j * 32], frow[0:1, 0:32])
            last.then_inc(frow_ready, 1)
            link(nc.vector.tensor_tensor(
                fws[:, :, :].rearrange("p g (x s) -> p (g x) s", s=SO),
                fws[:, :, :].rearrange("p g (x s) -> p (g x) s", s=SO),
                frec[:, :].unsqueeze(1).broadcast_to([P, 16, SO]), ALU.mult))
            fw4 = fws[:, :, :].rearrange("p (k r) m -> p k r m", k=2)
            places = [(0, 0, 64), (128, 32, 64), (256, 64, 32), (320, 0, 32)]
            for at, first, n in places:
                for kt in range(2):
                    last = nc.vector.tensor_copy(
                        fwx[:, 0, kt, at:at + 2 * n].rearrange("p (r m) -> p r m", r=2), fw4[:, kt, :, first:first + n])
            link(last)
            for at, first, n in places:
                for kt in range(2):
                    last = nc.vector.tensor_tensor(
                        fwx[:, 1, kt, at:at + 2 * n].rearrange("p (r m) -> p r m", r=2), fw4[:, kt, :, first:first + n],
                        fwx[:, 0, kt, at:at + 2 * n].rearrange("p (r m) -> p r m", r=2), ALU.subtract)
            last.then_inc(fw_split, 1)

            finish_norm(0, 1, norm_ready)
            ve.wait_ge(norm_ready, 1)
            for half in range(2):
                rows = slice(half * HR // 2, (half + 1) * HR // 2)
                part = slice(half * NPIX // 2, (half + 1) * NPIX // 2)
                link(nc.vector.tensor_scalar(norm0[:, part], X[:, part], rstd[:, 0:1], shift[:, 0:1],
                                             ALU.mult, ALU.add))
                ve.wait_ge(first_hi, half + 1)
                nc.vector.tensor_tensor(HL[:, rows, 1, 4:4 + WR],
                                        norm0[:, part].rearrange("p (r w) -> p r w", w=WR),
                                        HL[:, rows, 0, 4:4 + WR], ALU.subtract).then_inc(staged, 1)

            ve.wait_ge(fcol_ready, 1)
            link(nc.vector.tensor_copy(fcol[:, :], pw[:, 0:3]))
            ve.wait_ge(w1_in, 16)
            w1s = wload[:, :].rearrange("p (n t m) -> p n t m", n=NPAIR, t=3)
            for i in range(3):
                last = nc.vector.tensor_scalar(w1s[:, :, i, :], w1s[:, :, i, :], fcol[:, i:i + 1], None, ALU.mult)
            link(last)
            nc.vector.tensor_reduce(wmax[:, 0:1], wload[:, :], AX.X, ALU.max,
                                    apply_absolute_value=True).then_inc(wmax_ready, 1)
            ve.wait_ge(wall_ready, 1)
            link(nc.vector.tensor_scalar(yscale[:, :], wall[:, 0:1], TINY, None, ALU.max))
            nc.vector.reciprocal(wrec[:, 0:1], yscale[:, :]).then_inc(wrec_ready, 1)
            for b in range(1, B):
                ve.wait_ge(xt_in[b], 16)
                for i in range(NCH):
                    last = nc.vector.bn_stats(bst[:, (b - 1) * NCH + i, :],
                                              X[:, b * NPIX + i * CHUNK:b * NPIX + (i + 1) * CHUNK])
                if b == 1:
                    ve.wait_ge(w1_hi, 1)
                    nc.vector.scalar_tensor_tensor(w1l[:, :, :, :].rearrange("p n t m -> p (n t m)"), wload[:, :],
                                                   wrec[:, 0:1], w1h[:, :, :, :].rearrange("p n t m -> p (n t m)"),
                                                   ALU.mult, ALU.subtract).then_inc(w1_split, 1)
            link(last)
            aggregate(mv, B - 1)
            moments_of(mv, B - 1)
            finish_norm(1, B - 1, norm_ready, first=1)
            ve.wait_ge(lw_in, 16)
            nc.vector.tensor_reduce(wmax[:, 1:2], wload[:, 0:K1 * P], AX.X, ALU.max,
                                    apply_absolute_value=True).then_inc(wmax_ready, 1)
            ve.wait_ge(wall_ready, 2)
            link(nc.vector.tensor_scalar(lscale[:, :], wall[:, 1:2], TINY, None, ALU.max))
            nc.vector.reciprocal(wrec[:, 1:2], lscale[:, :]).then_inc(lw_scale, 1)

            def powers(g, cq, k):
                for i in range(HALVES):
                    ve.wait_ge(square_done, g * (HALVES * STEPS) + cq * (HALVES * BODY) + (HALVES * k + i + 1))
                    acc = pc[:, 2 * (k % 2) + i, :]
                    n = 64 if k % 3 < 2 else 32
                    for j in range(64 // n):
                        last = nc.vector.tensor_tensor(
                            power[64 * i + n * j:64 * i + n * j + n, k % 2, :], acc[2 * n * j:2 * n * j + n, :],
                            sq[2 * n * j + n:2 * n * j + 2 * n, k % 2, i, :], ALU.add)
                    last.then_inc(power_done, 1)

            def split(g, cq, k):
                t = g * STEPS + cq * BODY + k
                if k % 3 == 2:
                    pair = k // 3
                    ve.wait_ge(w1x_free, g * NPAIR + cq * 2 + (pair + 1))
                    for i, wt in enumerate((w1h, w1l)):
                        nc.vector.tensor_copy(w1x[:, pair, i, :],
                                              wt[:, bass.ds(cq * 2 + pair, 1), 2, :].rearrange("p o m -> p (o m)")
                                              ).then_inc(w1x_ready, 1)
                ve.wait_ge(mag_done, t + 1)
                nc.vector.tensor_copy(mhl[:, k % BODY, 0, :], mag[:, k % 2, :]).then_inc(mag_hi, 1)
                ve.wait_ge(mag_hi, t + 1)
                nc.vector.tensor_tensor(mhl[:, k % BODY, 1, :], mag[:, k % 2, :], mhl[:, k % BODY, 0, :],
                                        ALU.subtract).then_inc(maghl_done, 1)

            def group_stats(g):
                ve.wait_ge(y_out, g + 2)
                for i in range(2):
                    nc.vector.bn_stats(bst[:, bass.ds(g * 2 + i, 1), :].rearrange("p o s -> p (o s)"),
                                       X[:, bass.ds(g * (2 * CHUNK) + i * CHUNK, CHUNK)]).then_inc(group_stat, 1)

            powers(0, 0, 0)
            powers(0, 0, 1)
            split(0, 0, 0)
            powers(0, 0, 2)
            for run, (g0, g1) in enumerate(RUNS):
                with ve.Fori(g0, g1) as g:
                    with ve.Fori(0, CQ) as cq:
                        for s in range(BODY):
                            split(g, cq, s + 1)
                            powers(g, cq, s + 3)
                    group_stats(g)
                if run == 0:
                    ve.wait_ge(group_stat, 2 * g1)
                    aggregate(mv, B - 1)
                    moments_of(mv, B - 1)
                elif run == 1:
                    finish_norm(2, B - 1, norm_ready)
                elif run == 2:
                    ve.wait_ge(x1_done, 1)
                    batch_stats(0)
                    aggregate(mv, 1)
                    moments_of(mv, 1)
                else:
                    finish_norm(job(0), 1, norm_ready)
            g = NG - 1
            with ve.Fori(0, CQ - 1) as cq:
                for s in range(BODY):
                    split(g, cq, s + 1)
                    powers(g, cq, s + 3)
            for s in range(BODY - 1):
                split(g, CQ - 1, s + 1)
                if s < BODY - 3:
                    powers(g, CQ - 1, s + 3)
            group_stats(g)
            ve.wait_ge(group_stat, 2 * NG)
            link(nc.vector.bn_aggr(mv[:, 0, :], bst[:, (B - 1) * NCH:B * NCH, :].rearrange("p n s -> p (n s)")))
            moments_of(mv, 1)
            finish_norm(INJOB, 1, norm_ready, first=B - 1)

            def x1(b):
                ve.wait_ge(xn_in[b % 2], 32)
                ve.wait_ge(in_done, b - 1)
                xb = X[:, b * NPIX:(b + 1) * NPIX]
                nc.vector.tensor_tensor(xb, xb, xin[b % 2], ALU.add).then_inc(x1_done, 1)

            def prepare(k):
                layer, b = JOBS[k]
                if layer == 2:
                    ve.wait_ge(tile_out, FREE + TILES_BEFORE[b + 1])
                elif k >= 1:
                    ve.wait_ge(x1_done, b + 1)
                batch_stats(b)
                aggregate(mv, 1)
                moments_of(mv, 1)
                if k >= 1:
                    ve.wait_ge(hi_done, 2 * k)
                finish_norm(job(k), 1, norm_ready)
                if layer == 2:
                    ve.wait_ge(norm_ready, job(k) + 1)
                    nc.vector.tensor_scalar(pool[:, 0:1], pn[:, 2:3], rstd[:, 0:1], shift[:, 0:1],
                                            ALU.mult, ALU.add).then_inc(pool_ready, 1)
                    filters(k)

            def filters(k):
                b = JOBS[k][1]
                if b == 0:
                    ve.wait_ge(v_in, 32)
                ve.wait_ge(hid_sum, b + 1)
                nc.vector.tensor_scalar(hid[:, :], pw[:, 8:9], cc("vb1"), 0.0, ALU.add, ALU.max).then_inc(hid_ready, 1)
                ve.wait_ge(k_sum, b + 1)
                link(nc.vector.tensor_tensor(k9[:, :], pw[:, 16:16 + TAPS], cc("vb2"), ALU.add))
                nc.vector.tensor_reduce(kmax[:, :], k9[:, :], AX.X, ALU.max,
                                        apply_absolute_value=True).then_inc(kmax_ready, 1)
                ve.wait_ge(kall_ready, b + 1)
                link(nc.vector.tensor_scalar(kscale[:, b:b + 1], kall[:, :], TINY, None, ALU.max))
                link(nc.vector.reciprocal(krec[:, :], kscale[:, b:b + 1]))
                link(nc.vector.tensor_scalar(k9[:, :], k9[:, :], krec[:, 0:1], None, ALU.mult))
                masks = cc("taps").rearrange("p (t n) -> p t n", t=TAPS)
                link(nc.vector.tensor_scalar(kk[:, :], masks[:, 0, :], k9[:, 0:1], None, ALU.mult))
                for t in range(1, TAPS):
                    link(nc.vector.scalar_tensor_tensor(kk[:, :], masks[:, t, :], k9[:, t:t + 1], kk[:, :],
                                                        ALU.mult, ALU.add))
                link(nc.vector.tensor_tensor(
                    W2[:, :, :], kk[:, :].unsqueeze(2).broadcast_to([P, 4 * K2, C]),
                    cc("chan").unsqueeze(1).broadcast_to([P, 4 * K2, C]), ALU.mult))
                flat = W2[:, :, :].rearrange("p n c -> p (n c)")
                fh = W2h[:, b % 2, :, :].rearrange("p s m -> p (s m)")
                link(nc.vector.tensor_copy(fh, flat))
                nc.vector.tensor_tensor(W2l[:, b % 2, :, :].rearrange("p s m -> p (s m)"), flat, fh,
                                        ALU.subtract).then_inc(filters_ready, 1)

            def evict(k):
                layer, b = JOBS[k]
                scale = lscale[:, 0:1] if layer == 1 else kscale[:, b:b + 1]
                xb = X[:, b * NPIX:(b + 1) * NPIX].rearrange("p (r w) -> p r w", w=WR)
                for i, (w0, n) in enumerate(TILES[layer]):
                    ve.wait_ge(tile_done, TILES_BEFORE[k] + i + 1)
                    parts = [(32 * g, 32, g // 2, g % 2) for g in range(4)] if layer == 1 else \
                        [(64 * a, 64, a, 0) for a in range(2)]
                    cols = WR + 1 if layer == 1 else WR
                    acc = bank(i)[:, 0:n * cols].rearrange("p (r w) -> p r w", w=cols)
                    todo = []
                    for at, size, a, e in parts:
                        lo, hi = max(w0 - a, 0), min(w0 + n - a, HR)
                        if lo < hi:
                            todo.append((slice(at, at + size), lo, hi, lo + a - w0, e))
                    for ps, lo, hi, r, e in todo:
                        last = nc.vector.scalar_tensor_tensor(xb[ps, lo:hi, :], acc[ps, r:r + hi - lo, e:e + WR],
                                                              scale[ps], xb[ps, lo:hi, :], ALU.mult, ALU.add)
                    last.then_inc(tile_out, 1)

            ve.wait_ge(hi_done, 2)
            nc.vector.tensor_tensor(PH[:, 0, 1, 1:1 + HR, 1:1 + WR], t32[:, :].rearrange("p (r w) -> p r w", w=WR),
                                    PH[:, 0, 0, 1:1 + HR, 1:1 + WR], ALU.subtract).then_inc(lo_done, 1)
            prepare(1)
            x1(2)
            x1(3)
            evict(0)
            for k in range(2, 2 * B + 1):
                if k < 2 * B:
                    prepare(k)
                evict(k - 1)
                if k > B:
                    b = k - 1 - B
                    ve.wait_ge(tile_out, FREE + TILES_BEFORE[k])
                    batch_stats(b)
                    link(nc.vector.bn_aggr(mv3[:, b, :], bst[:, 0:NCH, :].rearrange("p n s -> p (n s)")))

            moments_of(mv3, B)
            finish_norm(LASTJOB, B)
            nc.vector.tensor_copy(ident16[:, :], cc("ident")).then_inc(ident_ready, 1)
            for part, (t0, t1) in enumerate([(0, 4), (4, 8), (8, TT // 2)]):
                with ve.Fori(t0, t1) as t2:
                    for s in range(2):
                        ve.wait_ge(xT_done, 2 * t2 + (s + 1))
                        for b in range(B):
                            last = nc.vector.tensor_scalar(
                                xg[:, s, b, :], X[:, bass.ds(t2 * (2 * P) + (b * NPIX + s * P), P)],
                                rstd[:, b:b + 1], shift[:, b:b + 1], ALU.mult, ALU.add)
                        last.then_inc(xg_norm, 1)
                        ve.wait_ge(xg_norm, 2 * t2 + (s + 1))
                        tile = xg[:, s, :, :].rearrange("p b n -> p (b n)")
                        nc.vector.tensor_copy(xhl[:, s, 0, :], tile).then_inc(xg_hi, 1)
                        ve.wait_ge(xg_hi, 2 * t2 + (s + 1))
                        nc.vector.tensor_tensor(xhl[:, s, 1, :], tile, xhl[:, s, 0, :],
                                                ALU.subtract).then_inc(xg_ready, 1)
                if part == 0:
                    ve.wait_ge(w3_in, 64)
                    nc.vector.tensor_reduce(w3max[:, :], WL[:, :, :, :].rearrange("p k t n -> p (k t n)"), AX.X,
                                            ALU.max, apply_absolute_value=True).then_inc(w3max_ready, 1)
                elif part == 1:
                    ve.wait_ge(w3all_ready, 1)
                    link(nc.vector.tensor_scalar(w3all[:, :], w3all[:, :], TINY, None, ALU.max))
                    nc.vector.tensor_scalar(oscale[:, :], w3all[:, :], 1.0 / H, None, ALU.mult)
                    nc.vector.reciprocal(w3rec[:, :], w3all[:, :]).then_inc(w3rec_ready, 1)
            ve.wait_ge(spec_done, 1)
            cosw = cc("cosw").rearrange("p (k g) -> p k g", k=2)
            sinw = cc("sinw").rearrange("p (k g) -> p k g", k=2)
            for kt in range(2):
                gk = G[:, kt, :].rearrange("p (b c) -> p b c", b=B)
                for sgn in range(2):
                    tab = sinw if sgn else cosw
                    acc = pc[:, 2 * sgn + kt, :].rearrange("p (b g c) -> p b g c", b=B, g=4)
                    for g in range(4):
                        if sgn == 0 and g == 0:
                            ins = nc.vector.tensor_scalar(gk, acc[:, :, g, :], tab[:, kt, g:g + 1], None, ALU.mult)
                        else:
                            ins = nc.vector.scalar_tensor_tensor(gk, acc[:, :, g, :], tab[:, kt, g:g + 1], gk,
                                                                 ALU.mult, ALU.add)
                        if sgn == 1 and g == 3:
                            ins.then_inc(G_ready, 1)
                        else:
                            link(ins)
            ve.wait_ge(G_ready, 2)
            ve.wait_ge(Gn_ready, 1)
            for kt in (1, 0):
                nc.vector.tensor_copy(XX[:, kt, :, 0, :], G[:, kt, :].rearrange("p (b c) -> p b c", b=B))
                nc.vector.tensor_copy(XX[:, kt, :, 1, :],
                                      pn[:, kt * P:(kt + 1) * P].rearrange("p (b c) -> p b c", b=B)
                                      ).then_inc(XX_ready, 1)
            ve.wait_ge(XX_ready, 2)
            ve.wait_ge(ww_ready, 1)

            def mixed(b):
                ve.wait_ge(XX_ready, 2)
                link(nc.vector.tensor_tensor(
                    prod0[:, :, :], WW[:, 0, :, :, :].rearrange("p o t i -> p o (t i)"),
                    XX[:, 0, b, :, :].rearrange("p t i -> p (t i)").unsqueeze(1).broadcast_to([P, C, 2 * C]),
                    ALU.mult))
                link(nc.vector.tensor_reduce(R[:, 0, b, :], prod0[:, :, :], AX.X, ALU.add))
                ve.wait_ge(prod_ready, b + 1)
                link(nc.vector.tensor_reduce(R[:, 1, b, :], prod[:, b, :, :], AX.X, ALU.add))
                for sgn in range(2):
                    tab = cc("sin" if sgn else "cos").rearrange("p (k g) -> p k g", k=2)
                    for kt in range(2):
                        last = nc.vector.tensor_tensor(
                            LL[:, sgn, kt, :, :], R[:, kt, b, :].unsqueeze(1).broadcast_to([P, 4, C]),
                            tab[:, kt, :].unsqueeze(2).broadcast_to([P, 4, C]), ALU.mult)
                link(last)
                flat = LL[:, :, :, :, :].rearrange("p s k g o -> p (s k g o)")
                parts = LLhl[:, b, :, :, :].rearrange("p h m n -> p h (m n)")
                link(nc.vector.tensor_copy(parts[:, 0, :], flat))
                ins = nc.vector.tensor_tensor(parts[:, 1, :], flat, parts[:, 0, :], ALU.subtract)
                ins.then_inc(LL_ready, 1)

            def add(i):
                b, n = INVERSE[i]
                ve.wait_ge(inv_done, i + 1)
                xc = X[:, b * NPIX + n * CHUNK:b * NPIX + (n + 1) * CHUNK]
                nc.vector.scalar_tensor_tensor(xc, pc[:, i % 4, :], oscale[:, 0:1], xc,
                                               ALU.mult, ALU.add).then_inc(inv_out, 1)

            mixed(0)
            for b in range(1, B):
                mixed(b)
                for i in range((b - 1) * IBAS, b * IBAS):
                    add(i)
            for i in range((B - 1) * IBAS, len(INVERSE)):
                add(i)

        @block.tensor
        def _(pe):
            nc.tensor.sem_inc(conv_done, AHEAD)
            nc.tensor.sem_inc(tile_out, FREE)
            nc.tensor.sem_inc(w1x_free, 2)
            nc.tensor.sem_inc(y_out, 1)
            nc.tensor.sem_inc(xT_done, 2)

            def stats(j, n, pooled=False):
                pe.wait_ge(moments, j + 1)
                ins = nc.tensor.matmul(pn[:, 0:2 * n], cc("channel" if j in (2, INJOB) else "group"),
                                       mom[:, 0:n, :].rearrange("p n s -> p (n s)"), start=True, stop=True)
                if pooled:
                    ins = nc.tensor.matmul(pn[:, 2:4], cc("channel"), mom[:, 0:1, :].rearrange("p n s -> p (n s)"),
                                           start=True, stop=True)
                ins.then_inc(group_sums, 1)

            pe.wait_ge(const_in, 16)
            stats(0, 1)
            pe.wait_ge(frow_ready, 1)
            for i in range(3):
                last = nc.tensor.matmul(pw[:, i:i + 1], frows[0:1, i, :], cc("one")[0:1, :], start=True, stop=True)
            last.then_inc(fcol_ready, 1)
            pe.wait_ge(fw_split, 1)
            pe.wait_ge(zeros_set, 2)

            def conv(k, quad, freed=None):
                pair, kind = k // 3, k % 3
                slot = [(2 * pair + j) % SLOTS for j in range(2)]
                if kind == 0:
                    for j in range(2):
                        pe.wait_ge(patch_in[slot[j]], quad * 64 + 64)
                for i in range(HALVES):
                    if freed is not None:
                        pe.wait_ge(power_done, freed + (i + 1))
                    if kind < 2:
                        tiles = [(0, P, slot[i], kind, 128 * kind)]
                    else:
                        tiles = [(64 * j, 64, slot[j], i, 256 + 64 * i) for j in range(2)]
                    mm = 0
                    for kt in range(2):
                        for wt, h in ((0, 0), (0, 1), (1, 0)):
                            for at, n, sl, half, w in tiles:
                                last = nc.tensor.matmul(
                                    pc[at:at + n, 2 * (k % 2) + i, :], fwx[:, wt, kt, w:w + n],
                                    patch[:, sl, 8 * half:8 * half + 8, h, 4 * kt:4 * kt + WR],
                                    start=(mm == 0), stop=(mm == 5))
                            mm += 1
                    last.then_inc(conv_done, 1)

            def mix(g, cq, k, first=False):
                pe.wait_ge(maghl_done, g * STEPS + cq * BODY + (k + 1))
                pair, kind = k // 3, k % 3
                if first and k == 0:
                    pe.wait_ge(y_out, g + 1)
                if kind < 2:
                    for wt, h in ((w1h, 0), (w1h, 1), (w1l, 0)):
                        lhs = wt[:, bass.ds(cq * 2 + pair, 1), kind, :].rearrange("p o m -> p (o m)")
                        nc.tensor.matmul(py[:, kind, :], lhs, mhl[:, k % BODY, h, :],
                                         start=first and k < 2 and wt is w1h and h == 0, stop=False)
                else:
                    pe.wait_ge(w1x_ready, g * (2 * NPAIR) + cq * 4 + (2 * pair + 2))
                    for i, h in ((0, 0), (0, 1), (1, 0)):
                        for half, to in ((0, slice(64, 128)), (1, slice(0, 64))):
                            last = nc.tensor.matmul(py[to, half, :], w1x[:, pair, i, to], mhl[:, k % BODY, h, :],
                                                    start=False, stop=False)
                    last.then_inc(w1x_free, 1)

            def zeros(to, start, stop):
                return nc.tensor.matmul(to, zero16[:, :], zero16[:, :].unsqueeze(1).broadcast_to([P, 4, P]),
                                        start=start, stop=stop)

            def step(g, cq, s, ahead=True, first=False):
                if ahead:
                    conv(s + 3, g * CQ + cq + (s + 3) // BODY,
                         g * (HALVES * STEPS) + cq * (HALVES * BODY) + HALVES * (s + 1))
                mix(g, cq, s, first)

            def close_sum():
                for h in range(2):
                    last = zeros(py[:, h, :], False, True)
                last.then_inc(y_ready, 1)

            conv(0, 0)
            conv(1, 0)
            pe.wait_ge(w1_split, 1)
            stats(1, B - 1)
            conv(2, 0, 0)
            for run, (g0, g1) in enumerate(RUNS):
                with pe.Fori(g0, g1) as g:
                    for s in range(BODY):
                        step(g, 0, s, first=True)
                    with pe.Fori(1, CQ) as cq:
                        for s in range(BODY):
                            step(g, cq, s)
                    close_sum()
                if run == 1:
                    stats(2, B - 1)
                elif run == 3:
                    stats(job(0), 1)
            g = NG - 1
            for s in range(BODY):
                step(g, 0, s, first=True)
            with pe.Fori(1, CQ - 1) as cq:
                for s in range(BODY):
                    step(g, cq, s)
            for s in range(BODY):
                step(g, CQ - 1, s, ahead=s < BODY - 3)
            close_sum()
            stats(INJOB, 1)

            pe.wait_ge(lw_split, 1)

            def window_sum(k, to, row, rows, done=True):
                layer, b = JOBS[k]
                nx, cols = (3, WR + 1) if layer == 1 else (3, WR)
                total, mm = 3 * (K1 if layer == 1 else K2), 0
                for s in range(total // 3):
                    sy, sx = s // nx, s % nx
                    if layer == 1:
                        hi, lo = lwh[:, s, :], lwl[:, s, :]
                    else:
                        hi, lo = W2h[:, b % 2, s, :], W2l[:, b % 2, s, :]
                    for wt, h in ((hi, 0), (hi, 1), (lo, 0)):
                        last = nc.tensor.matmul(to, wt, PH[:, k % 2, h, bass.ds(row + sy, rows), sx:sx + cols],
                                                start=(mm == 0), stop=(mm == total - 1))
                        mm += 1
                last.then_inc(tile_done, 1)

            def block_conv(k, half):
                layer, b = JOBS[k]
                if half == 0:
                    pe.wait_ge(lo_done, k + 1)
                    pe.wait_ge(bordered, min(k + 1, B + 2))
                    if layer == 2:
                        pe.wait_ge(filters_ready, b + 1)
                rows, cols = (7, WR + 1) if layer == 1 else (8, WR)
                before = TILES_BEFORE[k]
                freed = FREE + ((TILES_BEFORE[k - 1] + 4 if k else -6) if half == 0 else before) + 1
                with pe.Fori(0, 4) as i:
                    pe.wait_ge(tile_out, i + freed)
                    window_sum(k, pc[:, bass.ds(i, 1), 0:rows * cols].rearrange("p o n -> p (o n)"),
                               i * rows + half * 4 * rows, rows)
                if half == 1:
                    for i in range(8, len(TILES[layer])):
                        row, n = TILES[layer][i]
                        if k:
                            pe.wait_ge(tile_out, FREE + before)
                        window_sum(k, bank(i)[:, 0:n * cols], row, n)

            def filter_net(k):
                b = JOBS[k][1]
                if b == 0:
                    pe.wait_ge(v_in, 32)
                pe.wait_ge(pool_ready, b + 1)
                nc.tensor.matmul(pw[:, 8:9], v1s[:, :], pool[0:C, 0:1], start=True, stop=True).then_inc(hid_sum, 1)
                pe.wait_ge(hid_ready, b + 1)
                for t in range(TAPS):
                    last = nc.tensor.matmul(pw[:, 16 + t:17 + t], v2s[:, t, :], hid[:, :], start=True, stop=True)
                last.then_inc(k_sum, 1)

            for k in range(2 * B):
                block_conv(k, 0)
                if k + 1 < 2 * B:
                    stats(job(k + 1), 1, pooled=k + 1 >= B)
                    if k + 1 >= B:
                        filter_net(k + 1)
                block_conv(k, 1)
            stats(LASTJOB, B)

            pe.wait_ge(tile_out, FREE + TILES_BEFORE[2 * B])
            for m in range(4):
                zeros(pc[:, m, :], True, False)

            def transposes(t, s):
                pe.wait_ge(xg_ready, t + 1)
                for i in range(2 * B):
                    last = nc.tensor.transpose(py16[:, s % 2, i * P:(i + 1) * P],
                                               xhl[:, s % 2, i // B, i % B * P:(i % B + 1) * P], ident16[:, :])
                last.then_inc(xT_done, 1)

            def spectrum(t, s, t4):
                pe.wait_ge(xT_out, t + 1)
                pe.wait_ge(bas_in[s], t4 * 16 + 16)
                for m in range(4):
                    for wt, h in ((0, 0), (0, 1), (1, 0)):
                        last = nc.tensor.matmul(pc[:, m, :], bas[:, s, wt, m * P:(m + 1) * P],
                                                xT[:, s % 2, h * B * P:(h + 1) * B * P], start=False, stop=False)
                last.then_inc(spec_tile, 1)

            pe.wait_ge(ident_ready, 1)
            transposes(0, 0)
            with pe.Fori(0, TT // 4 - 1) as t4:
                for s in range(4):
                    transposes(t4 * 4 + (s + 1), (s + 1) % 4)
                    spectrum(t4 * 4 + s, s, t4)
            t4 = TT // 4 - 1
            for s in range(4):
                if s < 3:
                    transposes(t4 * 4 + s + 1, s + 1)
                spectrum(t4 * 4 + s, s, t4)
            for m in range(4):
                last = zeros(pc[:, m, :], False, True)
            last.then_inc(spec_done, 1)
            pe.wait_ge(G_ready, 2)
            perm = cc("mirror").rearrange("p (i o m) -> p i o m", i=2, o=2)
            for o in range(2):
                for i in range(2):
                    last = nc.tensor.matmul(pn[:, o * P:(o + 1) * P], perm[:, i, o, :], G[:, i, :],
                                            start=(i == 0), stop=(i == 1))
            last.then_inc(Gn_ready, 1)
            for i, (b, n) in enumerate(INVERSE):
                pe.wait_ge(LL_ready, b + 1)
                pe.wait_ge(ibas_in[n % IBAS], 16 * (n // IBAS + 1))
                if i >= 4:
                    pe.wait_ge(inv_out, i - 3)
                mm = 0
                for m in range(4):
                    for wt, h in ((0, 0), (0, 1), (1, 0)):
                        last = nc.tensor.matmul(pc[:, i % 4, :], LLhl[:, b, wt, m, :], ibas[n % IBAS][:, h, m, :],
                                                start=(mm == 0), stop=(mm == 11))
                        mm += 1
                last.then_inc(inv_done, 1)


def _const_columns():
    widths = [("group", P), ("channel", P), ("ident", P), ("mirror", 4 * P), ("taps", TAPS * 4 * K2), ("chan", C),
              ("cosw", 8), ("sinw", 8), ("cos", 8), ("sin", 8), ("one", 1), ("b1", 1), ("vb1", 1), ("vb2", TAPS)]
    at, where = 0, {}
    for name, n in widths:
        where[name] = (at, n)
        at += n
    return where, at


CONST_AT, CONST_COLS = _const_columns()


def _shape_constants():
    p = np.arange(P)
    chan, ph = p % C, p // C
    parts = {}
    parts["group"] = (chan[:, None] // 2 == chan[None, :] // 2) / 8.0
    parts["channel"] = (chan[:, None] == chan[None, :]) / 4.0
    parts["ident"] = np.eye(P)
    parts["chan"] = (chan[:, None] == np.arange(C)[None, :]) * 1.0
    parts["one"] = np.ones((P, 1))
    m = np.arange(MODES * MODES)
    minus = (-(m // MODES)) % MODES * MODES + (-(m % MODES)) % MODES
    full = np.zeros((2 * P, 2 * P))
    full[minus, m] = 1.0
    parts["mirror"] = full.reshape(2, P, 2, P).transpose(1, 0, 2, 3).reshape(P, 4 * P)
    taps = np.zeros((P, TAPS, K2, 2, 2))
    for q in range(4):
        for s in range(K2):
            for a in range(2):
                for e in range(2):
                    dy = 2 * (s // 3) + q // 2 - (2 - a) + 1
                    dx = 2 * (s % 3 - 1) + q % 2 - e + 1
                    if 0 <= dy < 3 and 0 <= dx < 3:
                        taps[ph == q, 3 * dy + dx, s, a, e] = 1.0
    parts["taps"] = taps.reshape(P, -1)
    k1, k2 = (m // MODES).reshape(2, P), (m % MODES).reshape(2, P)
    for name, f in (("cos", np.cos), ("sin", np.sin)):
        table = [[f(2 * math.pi * (k1[kt] * (g // 2) + k2[kt] * (g % 2)) / H) for g in range(4)] for kt in range(2)]
        parts[name] = np.array(table).transpose(2, 0, 1).reshape(P, 8)
        parts[name + "w"] = parts[name] / H
    return parts


def _bases():
    m = np.arange(MODES * MODES)
    pos = np.arange(NPIX)
    turns = (m[:, None] // MODES * (pos[None, :] // WR) + m[:, None] % MODES * (pos[None, :] % WR)) % HR
    angle = 2 * math.pi * turns / HR
    cas = np.stack([np.cos(angle) + np.sin(angle), np.cos(angle) - np.sin(angle)]).reshape(4, P, NPIX)
    high = cas.astype(np.float16)
    parts = np.stack([high, (cas - high).astype(np.float16)])
    basis = parts.reshape(2, 4 * P, TT, P).transpose(2, 3, 0, 1).reshape(TT, P, 2 * 4 * P)
    ibasis = parts.reshape(2, 4, P, NCH, CHUNK).transpose(3, 2, 0, 1, 4).reshape(NCH, P, 2 * 4 * CHUNK)
    return np.ascontiguousarray(basis), np.ascontiguousarray(ibasis)


def _phases(v):
    v = v.reshape(B, C, HR, 2, WR, 2).transpose(3, 5, 1, 0, 2, 4)
    return np.ascontiguousarray(v).reshape(P, B * NPIX)


def _filters(f):
    out = np.zeros((P, 2, 2, 2, 2, SO), f.dtype)
    for p in range(P):
        i2, plane, j2 = p // 4 % 8, p // 32, p % 4
        i, j = 2 * i2 + plane // 2, 2 * j2 + plane % 2
        for kt in range(2):
            for a in range(2):
                for e in range(2):
                    dx, dy = i - a, 8 * kt + j - e
                    if 0 <= dx < KF and 0 <= dy < KF:
                        out[p, kt, :, a, e, :] = f[:, :, dy, dx].T
    return out.reshape(P, 4 * M0)


def _mix(w):
    one = np.zeros((C, 4, SO, 4, C), w.dtype)
    for g in range(4):
        one[:, g, :, g, :] = w.reshape(C, C, SO).transpose(1, 2, 0)
    rows = one.reshape(NPAIR, 2, M0, P).transpose(1, 2, 0, 3)
    out = np.empty((P, NPAIR, 3, P), w.dtype)
    out[:, :, 0] = rows[:, :64].reshape(P, NPAIR, P)
    out[:, :, 1] = rows[:, 32:].reshape(P, NPAIR, P)
    out[:64, :, 2] = rows[:, 64:].reshape(64, NPAIR, P)
    out[64:, :, 2] = rows[:, :32].reshape(64, NPAIR, P)
    return out.reshape(P, NPAIR * 3 * P)


def _blocks(w):
    out = np.zeros((2, 2, C, 3, 3, 2, 2, C), w.dtype)
    for a in range(2):
        for e in range(2):
            for sy in range(3):
                for sx in range(3):
                    for oa in range(2):
                        for oe in range(2):
                            i = 3 - (2 * sy + a - (2 - oa))
                            j = 3 - (2 * sx + e - (2 - oe))
                            if 0 <= i < 5 and 0 <= j < 5:
                                out[a, e, :, sy, sx, oa, oe, :] = w[:, :, i, j].T
    return out.reshape(P, K1 * P)


def _modes(w):
    n = np.roll(np.flip(w, (-2, -1)), (1, 1), (-2, -1))
    return [np.ascontiguousarray(v.transpose(2, 3, 1, 0)).reshape(2, P, C * C) for v in (w, n)]


def kernel(x, L0_conv_filters, L0_conv_w1, L0_conv_b1, L1_conv_weight, L2_conv_w1, L2_conv_b1, L2_conv_w2,
           L2_conv_b2, L3_conv_weights1):
    import concourse.bacc as bacc
    from concourse.bass_utils import run_bass_kernel_spmd

    x = np.asarray(x)
    parts = _shape_constants()
    parts["b1"] = np.tile(np.asarray(L0_conv_b1), 4)[:, None]
    parts["vb1"] = np.asarray(L2_conv_b1)[:, None]
    parts["vb2"] = np.tile(np.asarray(L2_conv_b2).reshape(C, TAPS), (4, 1))
    const = np.zeros((P, CONST_COLS), np.float32)
    for name, (at, n) in CONST_AT.items():
        const[:, at:at + n] = parts[name]
    basis, ibasis = _bases()
    w3, w3n = _modes(np.asarray(L3_conv_weights1))
    arrays = {
        "xt": _phases(x.transpose(0, 1, 3, 2)),
        "xn": _phases(x),
        "fw": _filters(np.asarray(L0_conv_filters)),
        "w1": _mix(np.asarray(L0_conv_w1)),
        "lw": _blocks(np.asarray(L1_conv_weight)),
        "v1": np.ascontiguousarray(L2_conv_w1),
        "v2": np.ascontiguousarray(np.tile(np.asarray(L2_conv_w2).reshape(P, C, TAPS).transpose(0, 2, 1),
                                           (1, 1, 4))).reshape(P, TAPS * P),
        "w3": w3,
        "w3n": w3n,
        "const": const,
        "basis": basis,
        "ibasis": ibasis,
    }
    nc = bacc.Bacc("TRN2", target_bir_lowering=False, num_devices=1)
    t = {n: nc.dram_tensor(n, a.shape, F16 if a.dtype == np.float16 else F32, kind="ExternalInput").ap() for n, a in arrays.items()}
    out = nc.dram_tensor("out", (P, B * NPIX), F32, kind="ExternalOutput").ap()
    build(nc, t["xt"], t["xn"], t["fw"], t["w1"], t["lw"], t["v1"], t["v2"], t["w3"], t["w3n"],
          t["const"], t["basis"], t["ibasis"], out)
    r = run_bass_kernel_spmd(nc, [arrays], core_ids=[0])
    got = r.results[0]["out"].reshape(2, 2, C, B, HR, WR).transpose(3, 2, 4, 0, 5, 1)
    return np.ascontiguousarray(got).reshape(B, C, H, W)
```

```python
import math
from contextlib import ExitStack

import numpy as np

import concourse.bass as bass
from concourse import mybir
from concourse.alu_op_type import AluOpType as ALU

F32 = mybir.dt.float32
F16 = mybir.dt.float16
ACT = mybir.ActivationFunctionType
AX = mybir.AxisListType
ABSMAX = bass.bass_isa.ReduceOp.absmax

B, C, H, W = 4, 32, 128, 128
P = 128
HR, WR = H // 2, W // 2
NPIX = HR * WR
SO = 24
KF = 15
M0 = 4 * SO
TINY = 1e-30
EPS = 1e-5

PADW = WR + 8
ROW = 2 * PADW
PROWS = HR + 7
IMG_RUN = HR * ROW
PLANE = PROWS * ROW + 8
QR = 16
QRUN = QR * ROW
NQ = HR // QR
NG = B * NQ
SLOTS = 4
CQ = C // SLOTS
CHUNK = 512
NCH = NPIX // CHUNK

K1 = 9
K2 = 6
TAPS = 9
TILES = {1: [(i, 7) for i in range(0, 63, 7)] + [(63, 2)],
         2: [(i, 8) for i in range(0, 64, 8)] + [(64, 1)]}
PR1, PC1 = HR + 3, WR + 4
MODES = 16
NPAIR = C // 2
STEPS = 3 * NPAIR
BODY = 3 * SLOTS // 2

OUTPUTS = [[[(0, 64)], [(64, 32)]],
           [[(0, 48), (72, 16)], [(88, 8), (48, 24)]]]
REACH = [[[0, 1, 2], [2, 3]],
         [[0, 1, 3], [2, 3]]]
UNITS = 16
ROUNDS = [(1, [(0, 0), (0, 1), (0, 2), (1, 2)]),
          (4, [(2, 0), (2, 1), (2, 2), (3, 2)]),
          (5, [(1, 0), (1, 1), (4, 0), (4, 1)]),
          (5, [(3, 0), (3, 1), (5, 0), (5, 1)])]
MAGS = 5
HALVES = 2
AHEAD = HALVES * BODY
FREE = 10
TT = NPIX // P
IBAS = 4
INVERSE = [(b, n) for n0, n1 in ((0, IBAS), (IBAS, NCH)) for b in range(B) for n in range(n0, n1)]


def build(nc, xt, xn, fw, w1, lw, v1, v2, w3, w3n, const, basis, ibasis, out):
    es = ExitStack()
    with es:
        def sb(name, shape, dt=F32, stack=es):
            return stack.enter_context(nc.sbuf_tensor(name, shape, dt))

        def sem(name):
            return es.enter_context(nc.semaphore(name))

        X = sb("X", [P, B * NPIX])
        cst = sb("cst", [P, CONST_COLS])
        yscale = sb("yscale", [P, 1])
        lwh = sb("lwh", [P, K1, P], F16)
        lwl = sb("lwl", [P, K1, P], F16)
        lscale = sb("lscale", [P, 1])
        bst = sb("bst", [P, B * NCH, 6])
        bstx = sb("bstx", [P, (B - 1) * NCH, 6])
        mv = sb("mv", [P, B, 2])
        mom = sb("mom", [P, B, 2])
        red = sb("red", [P, B, 2])
        var = sb("var", [P, B])
        std = sb("std", [P, B])
        rstd = sb("rstd", [P, B])
        shift = sb("shift", [P, B])
        fmax = sb("fmax", [P, SO])
        fall = sb("fall", [P, SO])
        frec = sb("frec", [P, SO])
        frow = sb("frow", [1, 4 * SO])
        frows = sb("frows", [1, 4, P])
        fcol = sb("fcol", [P, 4])
        wmax = sb("wmax", [P, 2])
        w1max = sb("w1max", [P, CQ, UNITS])
        w1col = sb("w1col", [P, 4])
        wall = sb("wall", [P, 2])
        wrec = sb("wrec", [P, 2])
        wload = sb("wload", [P, (IBAS - 1) * 4 * CHUNK])
        HL = sb("HL", [P, HR, 2, PADW], F16)
        mv3 = sb("mv3", [P, B, 2])
        zero16 = sb("zero16", [P, P], F16)
        s0 = ExitStack()
        norm0 = sb("norm0", [P, NPIX], F32, s0)
        s0.close()
        sq = sb("sq", [P, 2, 2, CHUNK], F32, s0)
        power = sb("power", [P, 2, CHUNK], F32, s0)
        mag = sb("mag", [P, 2, CHUNK], F32, s0)
        powc = sb("powc", [P, 2, CHUNK], F32, s0)
        mhl = sb("mhl", [P, 2, 6, CHUNK], F16, s0)
        patch = sb("patch", [P, SLOTS, QR, 2, PADW], F16, s0)
        fws = sb("fws", [P, 4, M0], F32, s0)
        fwx = sb("fwx", [P, 2, 2, 384], F16, s0)
        w1hl = sb("w1hl", [P, CQ, 2, UNITS * C], F16, s0)
        w1x = sb("w1x", [P, 2, UNITS, C], F16, s0)
        zpad = sb("zpad", [P, PLANE - IMG_RUN - 3 * ROW + 8], F16, s0)
        s0.close()
        s1 = ExitStack()
        t32 = sb("t32", [P, NPIX], F32, s1)
        PH = sb("PH", [P, 2, 2, PR1, PC1], F16, s1)
        s2 = ExitStack()
        v1s = sb("v1s", [C, P], F32, s2)
        v2s = sb("v2s", [P, TAPS, P], F32, s2)
        hid = sb("hid", [P, 1], F32, s2)
        pool = sb("pool", [P, 2], F32, s2)
        k9 = sb("k9", [P, TAPS], F32, s2)
        kk = sb("kk", [P, K2 * 4], F32, s2)
        krec = sb("krec", [P, 1], F32, s2)
        kscale = sb("kscale", [P, B], F32, s2)
        W2 = sb("W2", [P, K2 * 4, C], F32, s2)
        W2h = sb("W2h", [P, 2, K2, P], F16, s2)
        W2l = sb("W2l", [P, 2, K2, P], F16, s2)
        s2.close()
        s1.close()
        s3 = ExitStack()
        G = sb("G", [P, 2, B * C], F32, s3)
        XX = sb("XX", [P, 2, B, 2, C], F32, s3)
        WW = sb("WW", [P, 2, C, 2, C], F32, s3)
        R = sb("R", [P, 2, B, C], F32, s3)
        LL = sb("LL", [P, 2, 2, 4, C], F32, s3)
        LLhl = sb("LLhl", [P, B, 2, 4, 4 * C], F16, s3)
        w3max = sb("w3max", [P, 1], F32, s3)
        w3all = sb("w3all", [P, 1], F32, s3)
        w3rec = sb("w3rec", [P, 1], F32, s3)
        oscale = sb("oscale", [P, 1], F32, s3)
        ident16 = sb("ident16", [P, P], F16, s3)
        s4 = ExitStack()
        WL = sb("WL", [P, 2, 2, C * C], F32, s4)
        xg = sb("xg", [P, 2, B, P], F32, s4)
        xhl = sb("xhl", [P, 2, 2, B * P], F16, s4)
        xT = sb("xT", [P, 2, 2 * B * P], F16, s4)
        s4.close()
        prod = sb("prod", [P, B, C, 2 * C], F32, s3)
        prod0 = sb("prod0", [P, C, 2 * C], F32, s3)
        s3.close()

        def by_kind(v):
            n = v.shape[2] // UNITS
            return [v[:, :, u0 * n:u1 * n] for u0, u1 in ((0, 6), (6, 12), (12, 14), (14, 16))]

        hl_flat = HL[:, :, :, :].rearrange("p r h w -> p (r h w)").bitcast(F32)
        xin = [hl_flat[:, 0:NPIX], wload[:, 0:NPIX]]
        ibas = [v.bitcast(F16).rearrange("p (h m n) -> p h m n", h=2, m=4)
                for v in [hl_flat[:, 0:4 * CHUNK]]
                + [wload[:, i * 4 * CHUNK:(i + 1) * 4 * CHUNK] for i in range(IBAS - 1)]]
        bas = hl_flat[:, 4 * CHUNK:8 * CHUNK].bitcast(F16).rearrange("p (s h n) -> p s h n", s=4, h=2)

        pc = es.enter_context(nc.psum_tensor("pc", [P, 4, CHUNK], F32))
        py = es.enter_context(nc.psum_tensor("py", [P, 2, CHUNK], F32))
        pn = es.enter_context(nc.psum_tensor("pn", [P, CHUNK], F32))
        pw = es.enter_context(nc.psum_tensor("pw", [P, CHUNK], F32))

        w1s = wload[:, 0:CQ * UNITS * C].rearrange("p (q n) -> p q n", q=CQ)
        py16 = py[:, :, :].bitcast(F16)

        planes = nc.dram_tensor("planes", [P, 4, PLANE], F16)
        planes_ap = planes.ap()

        def bank(i):
            return pc[:, i % 4, :] if i < 8 else py[:, i - 8, :]

        def cc(name):
            at, n = CONST_AT[name]
            return cst[:, at:at + n]

        const_in = sem("const_in")
        xt0_in = [sem(f"xt0_in{h}") for h in range(2)]
        xt_in = sem("xt_in")
        fw_in = sem("fw_in")
        w1_in = sem("w1_in")
        lw_in = sem("lw_in")
        zeros_set = sem("zeros_set")
        zeros_out = sem("zeros_out")
        first_planes = [sem(f"first_planes{i}") for i in range(2)]
        planes_out = sem("planes_out")
        fmax_ready = sem("fmax_ready")
        fall_ready = sem("fall_ready")
        frow_ready = sem("frow_ready")
        fcol_ready = sem("fcol_ready")
        fw_split = sem("fw_split")
        wmax_ready = sem("wmax_ready")
        wall_ready = sem("wall_ready")
        wrec_ready = sem("wrec_ready")
        w1_hi = sem("w1_hi")
        w1_split = sem("w1_split")
        lw_split = sem("lw_split")
        first_hi = sem("first_hi")
        staged = sem("staged")
        patch_in = [sem(f"patch_in{i}") for i in range(SLOTS)]
        conv_done = sem("conv_done")
        square_done = sem("square_done")
        power_done = sem("power_done")
        mag_done = sem("mag_done")
        maghl_done = sem("maghl_done")
        w1x_ready = sem("w1x_ready")
        mixed = sem("mixed")
        group_stat = sem("group_stat")
        x_stat = sem("x_stat")
        mag_hi = sem("mag_hi")
        filters_ready = sem("filters_ready")
        y_out = sem("y_out")
        moments = sem("moments")
        group_sums = sem("group_sums")
        var_ready = sem("var_ready")
        std_ready = sem("std_ready")
        xn_in = [sem(f"xn_in{i}") for i in range(2)]
        in_done = sem("in_done")
        x1_done = sem("x1_done")
        norm_ready = sem("norm_ready")
        hi_done = sem("hi_done")
        bordered = sem("bordered")
        tile_done = sem("tile_done")
        tile_out = sem("tile_out")
        lo_done = sem("lo_done")
        lw_scale = sem("lw_scale")
        v_in = sem("v_in")
        pool_ready = sem("pool_ready")
        hid_sum = sem("hid_sum")
        hid_ready = sem("hid_ready")
        k_sum = sem("k_sum")
        w3_in = sem("w3_in")
        ww_ready = sem("ww_ready")
        bas_in = [sem(f"bas_in{i}") for i in range(4)]
        ibas_in = [sem(f"ibas_in{i}") for i in range(IBAS)]
        w3max_ready = sem("w3max_ready")
        w3all_ready = sem("w3all_ready")
        w3rec_ready = sem("w3rec_ready")
        ident_ready = sem("ident_ready")
        xg_norm = sem("xg_norm")
        xg_hi = sem("xg_hi")
        xg_ready = sem("xg_ready")
        xT_done = sem("xT_done")
        xT_out = sem("xT_out")
        spec_tile = sem("spec_tile")
        spec_done = sem("spec_done")
        G_ready = sem("G_ready")
        Gn_ready = sem("Gn_ready")
        XX_ready = sem("XX_ready")
        prod_ready = sem("prod_ready")
        LL_ready = sem("LL_ready")
        inv_done = sem("inv_done")
        inv_out = sem("inv_out")
        saved = sem("saved")
        v_chain = sem("v_chain")
        p_chain = sem("p_chain")

        INJOB = 4
        LASTJOB = INJOB + 2 * B

        def job(k):
            return INJOB - 1 if k == 0 else INJOB + k

        RUNS = [(0, 1), (1, 2), (2, 3), (3, NG - NQ), (NG - NQ, NG - NQ + 1), (NG - NQ + 1, NG - NQ + 2),
                (NG - NQ + 2, NG - 1)]
        XSUM = 3
        JOBS = [(1, b) for b in range(B)] + [(2, b) for b in range(B)]

        TILES_BEFORE = [sum(len(TILES[layer]) for layer, _ in JOBS[:k]) for k in range(2 * B + 1)]

        def reflect(engine, rows, link):
            link(engine.tensor_copy(rows[:, :, 0, 1:1 + WR], rows[:, :, 1, 1:1 + WR]))
            link(engine.tensor_copy(rows[0:64, :, HR + 1, 1:1 + WR], rows[0:64, :, HR, 1:1 + WR]))
            link(engine.tensor_copy(rows[64:128, :, HR + 1, 1:1 + WR], rows[64:128, :, HR - 1, 1:1 + WR]))
            link(engine.tensor_copy(rows[:, :, HR + 2, 1:1 + WR], rows[:, :, 2, 1:1 + WR]))
            link(engine.tensor_copy(rows[:, :, :, 0], rows[:, :, :, 1]))
            for g in range(4):
                q = rows[32 * g:32 * g + 32]
                link(engine.tensor_copy(q[:, :, :, WR + 1], q[:, :, :, WR - g % 2]))
            return engine.tensor_copy(rows[:, :, :, WR + 2], rows[:, :, :, 2])

        block = es.enter_context(nc.Block())

        @block.sync
        def _(sp):
            sp.dma_start(fws[:, :, :].rearrange("p g m -> p (g m)"), fw).then_inc(fw_in, 16)
            for h in range(2):
                part = slice(h * NPIX // 2, (h + 1) * NPIX // 2)
                sp.dma_start(X[:, part], xt[:, part]).then_inc(xt0_in[h], 16)
            sp.dma_start(cst[:, :], const).then_inc(const_in, 16)
            sp.dma_start(wload[:, 0:CQ * UNITS * C], w1).then_inc(w1_in, 16)
            sp.wait_ge(zeros_set, 2)
            for pr in range(2):
                for pcol in range(2):
                    plane = 2 * pr + pcol
                    top = (4 - pr) * ROW - pcol
                    end = top + IMG_RUN
                    sp.dma_start(planes_ap[:, plane, 0:top], zpad[:, 0:top]).then_inc(zeros_out, 16)
                    sp.dma_start(planes_ap[:, plane, end:PLANE], zpad[:, 0:PLANE - end]).then_inc(zeros_out, 16)
            for half in range(2):
                sp.wait_ge(staged, half + 1)
                rows = slice(half * HR // 2, (half + 1) * HR // 2)
                for a in range(2):
                    for e in range(2):
                        plane = 2 * (1 - a) + (1 - e)
                        at = (3 + a) * ROW - (1 - e) + half * IMG_RUN // 2
                        g = 2 * a + e
                        sp.dma_start(planes_ap[0:C, plane, at:at + IMG_RUN // 2],
                                     HL[32 * g:32 * g + 32, rows, :, :].rearrange("p r h w -> p (r h w)")
                                     ).then_inc(first_planes[half], 16)
            sp.wait_ge(zeros_out, 16 * 8)
            for b, q0, q1 in [(0, 0, 1), (0, 1, NQ)] + [(b, 0, NQ) for b in range(1, B)]:
                if b == 0:
                    sp.wait_ge(first_planes[q0], 64)
                else:
                    sp.wait_ge(planes_out, b * 64)
                if b == B - 1:
                    sp.dma_start(xin[0], xn[:, 0:NPIX]).then_inc(xn_in[0], 16)
                    sp.wait_ge(lw_split, 1)
                    sp.dma_start(xin[1], xn[:, NPIX:2 * NPIX]).then_inc(xn_in[1], 16)
                with sp.Fori(q0, q1) as q:
                    with sp.Fori(0, CQ) as cq:
                        for s in range(SLOTS):
                            sp.wait_ge(conv_done, q * (HALVES * STEPS) + cq * (HALVES * BODY)
                                       + (HALVES * (b * NQ * STEPS + 3 * (s // 2 - 1)) + AHEAD))
                            for plane in range(4):
                                src = bass.AP(planes, cq * (SLOTS * 4 * PLANE) + q * QRUN
                                              + ((b * C + s) * 4 * PLANE + plane * PLANE),
                                              [[ROW, 8], [1, 4], [1, QRUN]])
                                dst = patch[32 * plane:32 * plane + 32, s, :, :, :].rearrange("p r h w -> p (r h w)")
                                sp.dma_start(dst, src).then_inc(patch_in[s], 16)
                        if (b, q0) == (0, 0):
                            for later in range(1, B):
                                sp.dma_start(X[:, bass.ds(cq * CHUNK + later * NPIX, CHUNK)],
                                             xt[:, bass.ds(cq * CHUNK + later * NPIX, CHUNK)]).then_inc(xt_in, 16)
                if (b, q0) == (0, 0):
                    sp.wait_ge(w1_split, 1)
                    sp.dma_start(wload[:, 0:K1 * P], lw).then_inc(lw_in, 16)
            for b in range(2, B):
                sp.wait_ge(x1_done, b - 1)
                sp.dma_start(xin[b % 2], xn[:, b * NPIX:(b + 1) * NPIX]).then_inc(xn_in[b % 2], 16)
            sp.wait_ge(y_out, NG + 1)
            sp.dma_start(v1s[:, :], v1).then_inc(v_in, 16)
            sp.dma_start(v2s[:, :, :].rearrange("p t m -> p (t m)"), v2).then_inc(v_in, 16)
            sp.wait_ge(x1_done, B)
            for s in range(4):
                sp.dma_start(bas[:, s, :, :].rearrange("p h n -> p (h n)"), basis[s]).then_inc(bas_in[s], 16)
            for s in range(IBAS):
                sp.dma_start(ibas[s].rearrange("p h m n -> p (h m n)"), ibasis[s]).then_inc(ibas_in[s], 16)
            sp.wait_ge(tile_out, FREE + TILES_BEFORE[2 * B])
            for kt in range(2):
                sp.dma_start(WL[:, kt, 0, :], w3[kt]).then_inc(w3_in, 16)
                sp.dma_start(WL[:, kt, 1, :], w3n[kt]).then_inc(w3_in, 16)
            with sp.Fori(1, TT // 4) as t4:
                for s in range(4):
                    sp.wait_ge(spec_tile, 4 * t4 + (s - 3))
                    sp.dma_start(bas[:, s, :, :].rearrange("p h n -> p (h n)"),
                                 basis[bass.ds(4 * t4 + s, 1)].rearrange("o p n -> (o p) n")
                                 ).then_inc(bas_in[s], 16)
            for i, (b, n) in enumerate(INVERSE):
                sp.wait_ge(inv_out, i + 1)
                if b == B - 1 and n + IBAS < NCH:
                    sp.dma_start(ibas[n].rearrange("p h m n -> p (h m n)"), ibasis[n + IBAS]
                                 ).then_inc(ibas_in[n], 16)
                cols = slice(b * NPIX + n * CHUNK, b * NPIX + (n + 1) * CHUNK)
                sp.dma_start(out[:, cols], X[:, cols]).then_inc(saved, 16)
            sp.wait_ge(saved, 16 * len(INVERSE))

        @block.gpsimd
        def _(gp):
            steps = [0]

            def link(ins):
                steps[0] += 1
                ins.then_inc(p_chain, 1)
                gp.wait_ge(p_chain, steps[0])

            nc.gpsimd.memset(zero16[:, :], 0.0).then_inc(zeros_set, 1)
            gp.wait_ge(fmax_ready, 1)
            nc.gpsimd.partition_all_reduce(fall[:, :], fmax[:, :], P, ABSMAX).then_inc(fall_ready, 1)
            for i in range(2):
                gp.wait_ge(wmax_ready, i + 1)
                nc.gpsimd.partition_all_reduce(wall[:, i:i + 1], wmax[:, i:i + 1], P, ABSMAX).then_inc(wall_ready, 1)
            gp.wait_ge(norm_ready, 2)
            for b in range(1, B):
                xb = X[:, b * NPIX:(b + 1) * NPIX]
                xb3 = xb.rearrange("p (r w) -> p r w", w=WR)
                hi = HL[:, :, 0, 4:4 + WR]
                lo = HL[:, :, 1, 4:4 + WR]
                link(nc.gpsimd.tensor_scalar(xb, xb, rstd[:, b:b + 1], shift[:, b:b + 1], ALU.mult, ALU.add))
                if b == 1:
                    for half in range(2):
                        gp.wait_ge(first_planes[half], 64)
                else:
                    gp.wait_ge(planes_out, 64 * (b - 1))
                link(nc.gpsimd.tensor_copy(hi, xb3))
                link(nc.gpsimd.tensor_tensor(lo, xb3, hi, ALU.subtract))
                for a in range(2):
                    for e in range(2):
                        plane = 2 * (1 - a) + (1 - e)
                        at = (3 + a) * ROW - (1 - e)
                        g = 2 * a + e
                        gp.dma_start(planes_ap[b * C:(b + 1) * C, plane, at:at + IMG_RUN],
                                     HL[32 * g:32 * g + 32, :, :, :].rearrange("p r h w -> p (r h w)")
                                     ).then_inc(planes_out, 16)
            gp.wait_ge(lw_scale, 1)
            wl = wload[:, 0:K1 * P]
            flat_h = lwh[:, :, :].rearrange("p s m -> p (s m)")
            link(nc.gpsimd.tensor_scalar(wl, wl, wrec[:, 1:2], None, ALU.mult))
            link(nc.gpsimd.tensor_copy(flat_h, wl))
            nc.gpsimd.tensor_tensor(lwl[:, :, :].rearrange("p s m -> p (s m)"), wl, flat_h,
                                    ALU.subtract).then_inc(lw_split, 1)
            gp.wait_ge(norm_ready, 3)
            for b in range(2):
                xb = X[:, b * NPIX:(b + 1) * NPIX]
                gp.wait_ge(xn_in[b], 16)
                link(nc.gpsimd.tensor_scalar(xb, xb, rstd[:, b:b + 1], shift[:, b:b + 1], ALU.mult, ALU.add))
                nc.gpsimd.tensor_tensor(xb, xb, xin[b], ALU.add).then_inc(x1_done, 1)

            def low_part(k):
                layer, b = JOBS[k]
                s = k % 2
                if k > 0:
                    gp.wait_ge(hi_done, 2 * (k + 1))
                    nc.gpsimd.tensor_tensor(PH[:, s, 1, 1:1 + HR, 1:1 + WR],
                                            t32[:, :].rearrange("p (r w) -> p r w", w=WR),
                                            PH[:, s, 0, 1:1 + HR, 1:1 + WR], ALU.subtract).then_inc(lo_done, 1)
                rows = PH[:, s, :, :, :]
                if k == 0 or k >= B + 2:
                    return
                if layer == 2:
                    link(nc.gpsimd.memset(rows[:, :, 0:1, :], 0.0))
                    link(nc.gpsimd.memset(rows[:, :, 1 + HR:PR1, :], 0.0))
                    link(nc.gpsimd.memset(rows[:, :, :, 0:1], 0.0))
                    nc.gpsimd.memset(rows[:, :, :, 1 + WR:PC1], 0.0).then_inc(bordered, 1)
                    return
                gp.wait_ge(lo_done, k + 1)
                reflect(nc.gpsimd, rows, link).then_inc(bordered, 1)

            for k in range(2 * B):
                low_part(k)
            gp.wait_ge(w3_in, 64)
            for kt in range(2):
                a = WL[:, kt, 0, :].rearrange("p (o i) -> p o i", i=C)
                n = WL[:, kt, 1, :].rearrange("p (o i) -> p o i", i=C)
                link(nc.gpsimd.tensor_tensor(WW[:, kt, :, 0, :], a, n, ALU.add))
                link(nc.gpsimd.tensor_tensor(WW[:, kt, :, 1, :], a, n, ALU.subtract))
            gp.wait_ge(w3max_ready, 1)
            nc.gpsimd.partition_all_reduce(w3all[:, :], w3max[:, :], P, ABSMAX).then_inc(w3all_ready, 1)
            gp.wait_ge(w3rec_ready, 1)
            flat = WW[:, :, :, :, :].rearrange("p k o t i -> p (k o t i)")
            nc.gpsimd.tensor_scalar(flat, flat, w3rec[:, 0:1], 0.5, ALU.mult, ALU.mult).then_inc(ww_ready, 1)
            gp.wait_ge(ww_ready, 1)
            gp.wait_ge(XX_ready, 1)
            for b in range(B):
                nc.gpsimd.tensor_tensor(
                    prod[:, b, :, :], WW[:, 1, :, :, :].rearrange("p o t i -> p o (t i)"),
                    XX[:, 1, b, :, :].rearrange("p t i -> p (t i)").unsqueeze(1).broadcast_to([P, C, 2 * C]),
                    ALU.mult).then_inc(prod_ready, 1)

        @block.scalar
        def _(act):
            def root(j, n):
                act.wait_ge(var_ready, j + 1)
                nc.scalar.activation(std[:, 0:n], var[:, 0:n], ACT.Sqrt).then_inc(std_ready, 1)

            root(0, 1)
            act.wait_ge(norm_ready, 1)
            for half in range(2):
                rows = slice(half * HR // 2, (half + 1) * HR // 2)
                nc.scalar.activation(HL[:, rows, 0, 4:4 + WR],
                                     X[:, 0:NPIX].rearrange("p (r w) -> p r w", w=WR)[:, rows, :], ACT.Identity,
                                     bias=shift[:, 0:1], scale=rstd[:, 0:1]).then_inc(first_hi, 1)
            act.wait_ge(wrec_ready, 1)
            for i, (to, w) in enumerate(zip(by_kind(w1hl[:, :, 0, :]), by_kind(w1s))):
                nc.scalar.activation(to, w, ACT.Identity, scale=w1col[:, i:i + 1]).then_inc(w1_hi, 1)

            def square(t, k):
                for i in range(HALVES):
                    act.wait_ge(conv_done, t * HALVES + (i + 1 + AHEAD))
                    acc = pc[:, 2 * (k % 2) + i, :]
                    nc.scalar.activation(sq[:, k % 2, i, :], acc, ACT.Square)
                    nc.scalar.activation(acc, acc, ACT.Square).then_inc(square_done, 1)

            def root_of(t, k):
                if k % BODY == 2:
                    return
                act.wait_ge(power_done, t * HALVES + HALVES)
                if k % BODY == 5:
                    nc.scalar.activation(powc[:, :, :], powc[:, :, :], ACT.Sqrt).then_inc(mag_done, 1)
                else:
                    nc.scalar.activation(mag[:, k % 2, :], power[:, k % 2, :], ACT.Sqrt).then_inc(mag_done, 1)

            def group_out(g):
                act.wait_ge(mixed, g * CQ + (CQ + 1))
                nc.scalar.activation(X[:, bass.ds(g * (2 * CHUNK), 2 * CHUNK)],
                                     py[:, :, :].rearrange("p h n -> p (h n)"), ACT.Identity,
                                     bias=cc("b1"), scale=yscale[:, 0:1]).then_inc(y_out, 1)

            act.wait_ge(const_in, 16)
            square(0, 0)
            square(1, 1)
            root_of(0, 0)
            square(2, 2)
            for run, (g0, g1) in enumerate(RUNS):
                with act.Fori(g0, g1) as g:
                    with act.Fori(0, CQ) as cq:
                        for s in range(BODY):
                            root_of(g * STEPS + cq * BODY + (s + 1), s + 1)
                            square(g * STEPS + cq * BODY + (s + 3), s + 3)
                    group_out(g)
                if run == 2:
                    root(1, B - 1)
                elif run == XSUM + 1:
                    root(2, B - 1)
                elif run == XSUM + 3:
                    root(3, 1)
            g = NG - 1
            with act.Fori(0, CQ - 1) as cq:
                for s in range(BODY):
                    root_of(cq * BODY + (g * STEPS + s + 1), s + 1)
                    square(cq * BODY + (g * STEPS + s + 3), s + 3)
            for s in range(BODY - 1):
                root_of(g * STEPS + (CQ - 1) * BODY + s + 1, s + 1)
                if s < BODY - 3:
                    square(g * STEPS + (CQ - 1) * BODY + s + 3, s + 3)
            group_out(g)

            def high_part(k):
                b = JOBS[k][1]
                if k:
                    root(job(k), 1)
                act.wait_ge(norm_ready, job(k) + 1)
                if k >= 2:
                    act.wait_ge(tile_done, TILES_BEFORE[k - 1])
                if k >= 1:
                    act.wait_ge(lo_done, k)
                xb = X[:, b * NPIX:(b + 1) * NPIX]
                nc.scalar.activation(PH[:, k % 2, 0, 1:1 + HR, 1:1 + WR], xb.rearrange("p (r w) -> p r w", w=WR),
                                     ACT.Identity, bias=shift[:, 0:1], scale=rstd[:, 0:1]).then_inc(hi_done, 1)
                if k:
                    nc.scalar.activation(t32[:, :], xb, ACT.Identity, bias=shift[:, 0:1],
                                         scale=rstd[:, 0:1]).then_inc(hi_done, 1)

            high_part(0)
            root(INJOB, 1)
            act.wait_ge(norm_ready, INJOB + 1)
            for b in range(2, B):
                xb = X[:, b * NPIX:(b + 1) * NPIX]
                nc.scalar.activation(xb, xb, ACT.Identity, bias=shift[:, b:b + 1],
                                     scale=rstd[:, b:b + 1]).then_inc(in_done, 1)
            for k in range(1, 2 * B):
                high_part(k)
            root(LASTJOB, B)
            with act.Fori(0, TT // 2) as t2:
                for s in range(2):
                    act.wait_ge(xT_done, 2 * t2 + (s + 1 + 2))
                    nc.scalar.activation(xT[:, s, :], py16[:, s, :], ACT.Identity).then_inc(xT_out, 1)

        @block.vector
        def _(ve):
            steps = [0]

            def link(ins):
                steps[0] += 1
                ins.then_inc(v_chain, 1)
                ve.wait_ge(v_chain, steps[0])

            def batch_stats(b, loaded=None):
                for i in range(NCH):
                    if loaded is not None and i % (NCH // 2) == 0:
                        ve.wait_ge(loaded[i // (NCH // 2)], 16)
                    last = nc.vector.bn_stats(bst[:, i, :], X[:, b * NPIX + i * CHUNK:b * NPIX + (i + 1) * CHUNK])
                link(last)

            def aggregate(to, n, bst=bst):
                for i in range(n):
                    last = nc.vector.bn_aggr(to[:, i, :],
                                             bst[:, i * NCH:(i + 1) * NCH, :].rearrange("p n s -> p (n s)"))
                link(last)

            def moments_of(mv, n):
                nc.vector.tensor_copy(mom[:, 0:n, 0], mv[:, 0:n, 0])
                link(nc.vector.tensor_tensor(mom[:, 0:n, 1], mv[:, 0:n, 0], mv[:, 0:n, 0], ALU.mult))
                nc.vector.tensor_tensor(mom[:, 0:n, 1], mom[:, 0:n, 1], mv[:, 0:n, 1], ALU.add).then_inc(moments, 1)

            def finish_norm(j, n, done=None, first=0):
                r, sh = rstd[:, first:first + n], shift[:, first:first + n]
                ve.wait_ge(group_sums, j + 1)
                link(nc.vector.tensor_copy(red[:, 0:n, :].rearrange("p n s -> p (n s)"), pn[:, 0:2 * n]))
                link(nc.vector.tensor_tensor(var[:, 0:n], red[:, 0:n, 0], red[:, 0:n, 0], ALU.mult))
                link(nc.vector.tensor_tensor(var[:, 0:n], red[:, 0:n, 1], var[:, 0:n], ALU.subtract))
                nc.vector.tensor_scalar(var[:, 0:n], var[:, 0:n], 0.0, EPS, ALU.max, ALU.add).then_inc(var_ready, 1)
                ve.wait_ge(std_ready, j + 1)
                link(nc.vector.reciprocal(r, std[:, 0:n]))
                ins = nc.vector.scalar_tensor_tensor(sh, red[:, 0:n, 0], -1.0, r, ALU.mult, ALU.mult)
                if done is None:
                    link(ins)
                else:
                    ins.then_inc(done, 1)

            nc.vector.memset(zpad[:, :], 0.0).then_inc(zeros_set, 1)
            link(nc.vector.memset(HL[:, :, :, :].rearrange("p r h w -> p (r h w)").bitcast(F32), 0.0))
            ve.wait_ge(fw_in, 16)
            nc.vector.tensor_reduce(fmax[:, :], fws[:, :, :].rearrange("p g (x s) -> p s (g x)", s=SO),
                                    AX.X, ALU.max, apply_absolute_value=True).then_inc(fmax_ready, 1)
            batch_stats(0, xt0_in)
            aggregate(mv, 1)
            moments_of(mv, 1)
            finish_norm(0, 1, norm_ready)
            ve.wait_ge(norm_ready, 1)
            for half in range(2):
                rows = slice(half * HR // 2, (half + 1) * HR // 2)
                part = slice(half * NPIX // 2, (half + 1) * NPIX // 2)
                link(nc.vector.tensor_scalar(norm0[:, part], X[:, part], rstd[:, 0:1], shift[:, 0:1],
                                             ALU.mult, ALU.add))
                ve.wait_ge(first_hi, half + 1)
                nc.vector.tensor_tensor(HL[:, rows, 1, 4:4 + WR],
                                        norm0[:, part].rearrange("p (r w) -> p r w", w=WR),
                                        HL[:, rows, 0, 4:4 + WR], ALU.subtract).then_inc(staged, 1)

            ve.wait_ge(fall_ready, 1)
            link(nc.vector.tensor_scalar(fall[:, :], fall[:, :], TINY, None, ALU.max))
            link(nc.vector.reciprocal(frec[:, :], fall[:, :]))
            for i in range(4):
                last = nc.vector.tensor_copy(frow[0:1, i * SO:(i + 1) * SO], fall[0:1, :])
            link(last)
            for half in range(2):
                for c4 in range(2):
                    n = 32 if c4 else 64
                    to = frows[0:1, 2 * c4 + half, :].rearrange("o (c m) -> o c m", m=n)
                    at = 0
                    for first, run in OUTPUTS[half][c4]:
                        last = nc.vector.tensor_copy(
                            to[:, :, at:at + run],
                            frow[0:1, first:first + run].unsqueeze(1).broadcast_to([1, P // n, run]))
                        at += run
            last.then_inc(frow_ready, 1)
            link(nc.vector.tensor_tensor(
                fws[:, :, :].rearrange("p g (x s) -> p (g x) s", s=SO),
                fws[:, :, :].rearrange("p g (x s) -> p (g x) s", s=SO),
                frec[:, :].unsqueeze(1).broadcast_to([P, 16, SO]), ALU.mult))
            fw4 = fws[:, :, :].rearrange("p (k r) m -> p k r m", k=2)
            moves = []
            for at, (half, c4) in ((0, (0, 0)), (128, (1, 0)), (256, (0, 1)), (320, (1, 1))):
                n, off = 32 if c4 else 64, 0
                for first, run in OUTPUTS[half][c4]:
                    for kt in range(2):
                        hi, lo = [fwx[:, part, kt, at:at + 2 * n].rearrange("p (r m) -> p r m", r=2)
                                  [:, :, off:off + run] for part in range(2)]
                        moves.append((hi, lo, fw4[:, kt, :, first:first + run]))
                    off += run
            for hi, lo, src in moves:
                last = nc.vector.tensor_copy(hi, src)
            link(last)
            for hi, lo, src in moves:
                last = nc.vector.tensor_tensor(lo, src, hi, ALU.subtract)
            last.then_inc(fw_split, 1)

            ve.wait_ge(fcol_ready, 1)
            link(nc.vector.tensor_copy(fcol[:, :], pw[:, 0:4]))
            ve.wait_ge(w1_in, 16)
            link(nc.vector.tensor_reduce(w1max[:, :, :], w1s.rearrange("p q (u m) -> p q u m", m=C), AX.X, ALU.max,
                                         apply_absolute_value=True))
            for i, v in enumerate(by_kind(w1max[:, :, :])):
                last = nc.vector.tensor_scalar(v, v, fcol[:, i:i + 1], None, ALU.mult)
            link(last)
            nc.vector.tensor_reduce(wmax[:, 0:1], w1max[:, :, :].rearrange("p q u -> p (q u)"), AX.X,
                                    ALU.max).then_inc(wmax_ready, 1)
            ve.wait_ge(wall_ready, 1)
            link(nc.vector.tensor_scalar(yscale[:, :], wall[:, 0:1], TINY, None, ALU.max))
            link(nc.vector.reciprocal(wrec[:, 0:1], yscale[:, :]))
            nc.vector.tensor_scalar(w1col[:, :], fcol[:, :], wrec[:, 0:1], None, ALU.mult).then_inc(wrec_ready, 1)

            def powers(g, cq, k):
                for i in range(HALVES):
                    ve.wait_ge(square_done, g * (HALVES * STEPS) + cq * (HALVES * BODY) + (HALVES * k + i + 1))
                    acc = pc[:, 2 * (k % 2) + i, :]
                    squares = sq[:, k % 2, i, :]
                    if k % 3 < 2:
                        last = nc.vector.tensor_tensor(power[64 * i:64 * i + 64, k % 2, :], acc[0:64, :],
                                                       squares[64:128, :], ALU.add)
                    else:
                        for j in range(2):
                            ch = 2 * (k // 3 % 2) + j
                            last = nc.vector.tensor_tensor(powc[32 * ch:32 * ch + 32, i, :], acc[64 * j:64 * j + 32, :],
                                                           squares[64 * j + 32:64 * j + 64, :], ALU.add)
                    last.then_inc(power_done, 1)

            def split(g, cq, k):
                body = g * CQ + cq
                if k % BODY == 2:
                    ve.wait_ge(mixed, body + 1)
                    nc.vector.tensor_copy(w1x[:, :, :, :].rearrange("p h u m -> p (h u m)"),
                                          w1hl[:, bass.ds(cq, 1), :, :].rearrange("p o h n -> p (o h n)")
                                          ).then_inc(w1x_ready, 1)
                    return
                if k % BODY == 1:
                    ve.wait_ge(mixed, body + 1)
                if k % BODY == 5:
                    src, tile, n = powc[:, :, :], 4, 2
                else:
                    src, tile, n = mag[:, k % 2:k % 2 + 1, :], k % BODY // 3 * 2 + k % 3, 1
                done = body * MAGS + (k // BODY * MAGS + (1, 2, 0, 3, 4, 5)[k % BODY])
                ve.wait_ge(mag_done, done)
                nc.vector.tensor_copy(mhl[:, 0, tile:tile + n, :], src).then_inc(mag_hi, 1)
                ve.wait_ge(mag_hi, done)
                nc.vector.tensor_tensor(mhl[:, 1, tile:tile + n, :], src, mhl[:, 0, tile:tile + n, :],
                                        ALU.subtract).then_inc(maghl_done, 1)

            def group_stats(g):
                ve.wait_ge(y_out, g + 2)
                for i in range(2):
                    nc.vector.bn_stats(bst[:, bass.ds(g * 2 + i, 1), :].rearrange("p o s -> p (o s)"),
                                       X[:, bass.ds(g * (2 * CHUNK) + i * CHUNK, CHUNK)]).then_inc(group_stat, 1)

            ve.wait_ge(wrec_ready, 1)
            for i, (hi, lo, w) in enumerate(zip(by_kind(w1hl[:, :, 0, :]), by_kind(w1hl[:, :, 1, :]), by_kind(w1s))):
                ve.wait_ge(w1_hi, i + 1)
                last = nc.vector.scalar_tensor_tensor(lo, w, w1col[:, i:i + 1], hi, ALU.mult, ALU.subtract)
            last.then_inc(w1_split, 1)
            powers(0, 0, 0)
            powers(0, 0, 1)
            split(0, 0, 0)
            powers(0, 0, 2)
            for run, (g0, g1) in enumerate(RUNS):
                with ve.Fori(g0, g1) as g:
                    with ve.Fori(0, CQ) as cq:
                        for s in range(BODY):
                            split(g, cq, s + 1)
                            powers(g, cq, s + 3)
                        if run == 1:
                            for b in range(1, B):
                                nc.vector.bn_stats(
                                    bstx[:, bass.ds(cq + (b - 1) * NCH, 1), :].rearrange("p o s -> p (o s)"),
                                    X[:, bass.ds(cq * CHUNK + b * NPIX, CHUNK)]).then_inc(x_stat, 1)
                    group_stats(g)
                if run == 0:
                    ve.wait_ge(xt_in, 16 * (B - 1) * NCH)
                elif run == 1:
                    ve.wait_ge(x_stat, (B - 1) * NCH)
                    aggregate(mv, B - 1, bstx)
                    moments_of(mv, B - 1)
                    ve.wait_ge(lw_in, 16)
                    nc.vector.tensor_reduce(wmax[:, 1:2], wload[:, 0:K1 * P], AX.X, ALU.max,
                                            apply_absolute_value=True).then_inc(wmax_ready, 1)
                elif run == 2:
                    finish_norm(1, B - 1, norm_ready, first=1)
                    ve.wait_ge(wall_ready, 2)
                    link(nc.vector.tensor_scalar(lscale[:, :], wall[:, 1:2], TINY, None, ALU.max))
                    nc.vector.reciprocal(wrec[:, 1:2], lscale[:, :]).then_inc(lw_scale, 1)
                elif run == XSUM:
                    ve.wait_ge(group_stat, 2 * g1)
                    aggregate(mv, B - 1)
                    moments_of(mv, B - 1)
                elif run == XSUM + 1:
                    finish_norm(2, B - 1, norm_ready)
                elif run == XSUM + 2:
                    ve.wait_ge(x1_done, 1)
                    batch_stats(0)
                    aggregate(mv, 1)
                    moments_of(mv, 1)
                elif run == XSUM + 3:
                    finish_norm(job(0), 1, norm_ready)
            g = NG - 1
            with ve.Fori(0, CQ - 1) as cq:
                for s in range(BODY):
                    split(g, cq, s + 1)
                    powers(g, cq, s + 3)
            for s in range(BODY - 1):
                split(g, CQ - 1, s + 1)
                if s < BODY - 3:
                    powers(g, CQ - 1, s + 3)
            ve.wait_ge(y_out, NG + 1)
            ve.wait_ge(norm_ready, job(0) + 1)
            nc.vector.tensor_scalar(t32[:, :], X[:, 0:NPIX], rstd[:, 0:1], shift[:, 0:1],
                                    ALU.mult, ALU.add).then_inc(hi_done, 1)
            ve.wait_ge(hi_done, 2)
            nc.vector.tensor_tensor(PH[:, 0, 1, 1:1 + HR, 1:1 + WR], t32[:, :].rearrange("p (r w) -> p r w", w=WR),
                                    PH[:, 0, 0, 1:1 + HR, 1:1 + WR], ALU.subtract).then_inc(lo_done, 1)
            ve.wait_ge(lo_done, 1)
            reflect(nc.vector, PH[:, 0, :, :, :], link).then_inc(bordered, 1)
            group_stats(g)
            ve.wait_ge(group_stat, 2 * NG)
            link(nc.vector.bn_aggr(mv[:, 0, :], bst[:, (B - 1) * NCH:B * NCH, :].rearrange("p n s -> p (n s)")))
            moments_of(mv, 1)

            def x1(b):
                ve.wait_ge(xn_in[b % 2], 32)
                ve.wait_ge(in_done, b - 1)
                xb = X[:, b * NPIX:(b + 1) * NPIX]
                nc.vector.tensor_tensor(xb, xb, xin[b % 2], ALU.add).then_inc(x1_done, 1)

            def sums(k):
                layer, b = JOBS[k]
                if layer == 2:
                    ve.wait_ge(tile_out, FREE + TILES_BEFORE[b + 1])
                else:
                    ve.wait_ge(x1_done, b + 1)
                batch_stats(b)
                aggregate(mv, 1)
                moments_of(mv, 1)

            def normalise(k):
                ve.wait_ge(hi_done, 2 * k)
                finish_norm(job(k), 1, norm_ready)
                if JOBS[k][0] == 2:
                    ve.wait_ge(norm_ready, job(k) + 1)
                    nc.vector.tensor_scalar(pool[:, 0:1], pn[:, 2:3], rstd[:, 0:1], shift[:, 0:1],
                                            ALU.mult, ALU.add).then_inc(pool_ready, 1)

            def hidden(b):
                if b == 0:
                    ve.wait_ge(v_in, 32)
                ve.wait_ge(hid_sum, b + 1)
                nc.vector.tensor_scalar(hid[:, :], pw[:, 8:9], cc("vb1"), 0.0, ALU.add, ALU.max).then_inc(hid_ready, 1)

            def filters(b):
                ve.wait_ge(k_sum, b + 1)
                link(nc.vector.tensor_tensor(k9[:, :], pw[:, 16:16 + TAPS], cc("vb2"), ALU.add))
                scale = kscale[:, b:b + 1]
                link(nc.vector.tensor_reduce(scale, k9[:, :], AX.X, ALU.max, apply_absolute_value=True))
                link(nc.vector.tensor_scalar(scale, scale, TINY, None, ALU.max))
                link(nc.vector.reciprocal(krec[:, :], kscale[:, b:b + 1]))
                link(nc.vector.tensor_scalar(k9[:, :], k9[:, :], krec[:, 0:1], None, ALU.mult))
                masks = cc("taps").rearrange("p (t n) -> p t n", t=TAPS)
                link(nc.vector.tensor_scalar(kk[:, :], masks[:, 0, :], k9[:, 0:1], None, ALU.mult))
                for t in range(1, TAPS):
                    link(nc.vector.scalar_tensor_tensor(kk[:, :], masks[:, t, :], k9[:, t:t + 1], kk[:, :],
                                                        ALU.mult, ALU.add))
                link(nc.vector.tensor_tensor(
                    W2[:, :, :], kk[:, :].unsqueeze(2).broadcast_to([P, 4 * K2, C]),
                    cc("chan").unsqueeze(1).broadcast_to([P, 4 * K2, C]), ALU.mult))
                flat = W2[:, :, :].rearrange("p n c -> p (n c)")
                fh = W2h[:, b % 2, :, :].rearrange("p s m -> p (s m)")
                link(nc.vector.tensor_copy(fh, flat))
                nc.vector.tensor_tensor(W2l[:, b % 2, :, :].rearrange("p s m -> p (s m)"), flat, fh,
                                        ALU.subtract).then_inc(filters_ready, 1)

            def evict(k, i0, i1):
                layer, b = JOBS[k]
                scale = lscale[:, 0:1] if layer == 1 else kscale[:, b:b + 1]
                xb = X[:, b * NPIX:(b + 1) * NPIX].rearrange("p (r w) -> p r w", w=WR)
                for i in range(i0, i1):
                    w0, n = TILES[layer][i]
                    ve.wait_ge(tile_done, TILES_BEFORE[k] + i + 1)
                    parts = [(32 * g, 32, g // 2, g % 2) for g in range(4)] if layer == 1 else \
                        [(64 * a, 64, a, 0) for a in range(2)]
                    cols = WR + 1 if layer == 1 else WR
                    acc = bank(i)[:, 0:n * cols].rearrange("p (r w) -> p r w", w=cols)
                    todo = []
                    for at, size, a, e in parts:
                        lo, hi = max(w0 - a, 0), min(w0 + n - a, HR)
                        if lo < hi:
                            todo.append((slice(at, at + size), lo, hi, lo + a - w0, e))
                    for ps, lo, hi, r, e in todo:
                        last = nc.vector.scalar_tensor_tensor(xb[ps, lo:hi, :], acc[ps, r:r + hi - lo, e:e + WR],
                                                              scale[ps], xb[ps, lo:hi, :], ALU.mult, ALU.add)
                    last.then_inc(tile_out, 1)
                    if layer == 2 and i >= 2:
                        x3_stats(k, i - 2)

            def x3_stats(k, i):
                at = JOBS[k][1] * NPIX + i * CHUNK
                ve.wait_ge(tile_out, FREE + TILES_BEFORE[k] + i + 2)
                return nc.vector.bn_stats(bst[:, i, :], X[:, at:at + CHUNK])

            for k in range(2 * B):
                tiles = len(TILES[JOBS[k][0]])
                if k == 0:
                    evict(0, 0, 2)
                    finish_norm(INJOB, 1, norm_ready, first=B - 1)
                    sums(1)
                    evict(0, 2, 4)
                    normalise(1)
                    x1(2)
                    x1(3)
                    evict(0, 4, tiles)
                    continue
                following = k + 1 < 2 * B
                adaptive = following and JOBS[k + 1][0] == 2
                if following:
                    sums(k + 1)
                evict(k, 0, 2)
                if following:
                    normalise(k + 1)
                evict(k, 2, 4)
                if adaptive:
                    hidden(JOBS[k + 1][1])
                evict(k, 4, 5)
                if adaptive:
                    filters(JOBS[k + 1][1])
                evict(k, 5, tiles)
                if JOBS[k][0] == 2:
                    link(x3_stats(k, NCH - 1))
                    link(nc.vector.bn_aggr(mv3[:, JOBS[k][1], :], bst[:, 0:NCH, :].rearrange("p n s -> p (n s)")))

            moments_of(mv3, B)
            finish_norm(LASTJOB, B)
            nc.vector.tensor_copy(ident16[:, :], cc("ident")).then_inc(ident_ready, 1)
            for part, (t0, t1) in enumerate([(0, 4), (4, 8), (8, TT // 2)]):
                with ve.Fori(t0, t1) as t2:
                    for s in range(2):
                        ve.wait_ge(xT_done, 2 * t2 + (s + 1))
                        for b in range(B):
                            last = nc.vector.tensor_scalar(
                                xg[:, s, b, :], X[:, bass.ds(t2 * (2 * P) + (b * NPIX + s * P), P)],
                                rstd[:, b:b + 1], shift[:, b:b + 1], ALU.mult, ALU.add)
                        last.then_inc(xg_norm, 1)
                        ve.wait_ge(xg_norm, 2 * t2 + (s + 1))
                        tile = xg[:, s, :, :].rearrange("p b n -> p (b n)")
                        nc.vector.tensor_copy(xhl[:, s, 0, :], tile).then_inc(xg_hi, 1)
                        ve.wait_ge(xg_hi, 2 * t2 + (s + 1))
                        nc.vector.tensor_tensor(xhl[:, s, 1, :], tile, xhl[:, s, 0, :],
                                                ALU.subtract).then_inc(xg_ready, 1)
                if part == 0:
                    ve.wait_ge(w3_in, 64)
                    nc.vector.tensor_reduce(w3max[:, :], WL[:, :, :, :].rearrange("p k t n -> p (k t n)"), AX.X,
                                            ALU.max, apply_absolute_value=True).then_inc(w3max_ready, 1)
                elif part == 1:
                    ve.wait_ge(w3all_ready, 1)
                    link(nc.vector.tensor_scalar(w3all[:, :], w3all[:, :], TINY, None, ALU.max))
                    nc.vector.tensor_scalar(oscale[:, :], w3all[:, :], 1.0 / H, None, ALU.mult)
                    nc.vector.reciprocal(w3rec[:, :], w3all[:, :]).then_inc(w3rec_ready, 1)
            ve.wait_ge(spec_done, 1)
            cosw = cc("cosw").rearrange("p (k g) -> p k g", k=2)
            sinw = cc("sinw").rearrange("p (k g) -> p k g", k=2)
            for sgn in range(2):
                tab = sinw if sgn else cosw
                for g in range(4):
                    for kt in range(2):
                        gk = G[:, kt, :].rearrange("p (b c) -> p b c", b=B)
                        acc = pc[:, 2 * sgn + kt, :].rearrange("p (b g c) -> p b g c", b=B, g=4)
                        if sgn == 0 and g == 0:
                            ins = nc.vector.tensor_scalar(gk, acc[:, :, g, :], tab[:, kt, g:g + 1], None, ALU.mult)
                        else:
                            ins = nc.vector.scalar_tensor_tensor(gk, acc[:, :, g, :], tab[:, kt, g:g + 1], gk,
                                                                 ALU.mult, ALU.add)
                        if sgn == 1 and g == 3:
                            ins.then_inc(G_ready, 1)
                    if not (sgn == 1 and g == 3):
                        link(ins)
            ve.wait_ge(G_ready, 2)
            ve.wait_ge(Gn_ready, 1)
            for kt in (1, 0):
                nc.vector.tensor_copy(XX[:, kt, :, 0, :], G[:, kt, :].rearrange("p (b c) -> p b c", b=B))
                nc.vector.tensor_copy(XX[:, kt, :, 1, :],
                                      pn[:, kt * P:(kt + 1) * P].rearrange("p (b c) -> p b c", b=B)
                                      ).then_inc(XX_ready, 1)
            ve.wait_ge(XX_ready, 2)
            ve.wait_ge(ww_ready, 1)

            def mix_modes(b):
                ve.wait_ge(XX_ready, 2)
                link(nc.vector.tensor_tensor(
                    prod0[:, :, :], WW[:, 0, :, :, :].rearrange("p o t i -> p o (t i)"),
                    XX[:, 0, b, :, :].rearrange("p t i -> p (t i)").unsqueeze(1).broadcast_to([P, C, 2 * C]),
                    ALU.mult))
                link(nc.vector.tensor_reduce(R[:, 0, b, :], prod0[:, :, :], AX.X, ALU.add))
                ve.wait_ge(prod_ready, b + 1)
                link(nc.vector.tensor_reduce(R[:, 1, b, :], prod[:, b, :, :], AX.X, ALU.add))
                for sgn in range(2):
                    tab = cc("sin" if sgn else "cos").rearrange("p (k g) -> p k g", k=2)
                    for kt in range(2):
                        last = nc.vector.tensor_tensor(
                            LL[:, sgn, kt, :, :], R[:, kt, b, :].unsqueeze(1).broadcast_to([P, 4, C]),
                            tab[:, kt, :].unsqueeze(2).broadcast_to([P, 4, C]), ALU.mult)
                link(last)
                flat = LL[:, :, :, :, :].rearrange("p s k g o -> p (s k g o)")
                parts = LLhl[:, b, :, :, :].rearrange("p h m n -> p h (m n)")
                link(nc.vector.tensor_copy(parts[:, 0, :], flat))
                ins = nc.vector.tensor_tensor(parts[:, 1, :], flat, parts[:, 0, :], ALU.subtract)
                ins.then_inc(LL_ready, 1)

            def add(i):
                b, n = INVERSE[i]
                ve.wait_ge(inv_done, i + 1)
                xc = X[:, b * NPIX + n * CHUNK:b * NPIX + (n + 1) * CHUNK]
                nc.vector.scalar_tensor_tensor(xc, pc[:, i % 4, :], oscale[:, 0:1], xc,
                                               ALU.mult, ALU.add).then_inc(inv_out, 1)

            mix_modes(0)
            for b in range(1, B):
                mix_modes(b)
                for i in range((b - 1) * IBAS, b * IBAS):
                    add(i)
            for i in range((B - 1) * IBAS, len(INVERSE)):
                add(i)

        @block.tensor
        def _(pe):
            nc.tensor.sem_inc(conv_done, AHEAD)
            nc.tensor.sem_inc(tile_out, FREE)
            nc.tensor.sem_inc(mixed, 1)
            nc.tensor.sem_inc(y_out, 1)
            nc.tensor.sem_inc(xT_done, 2)

            def stats(j, n, pooled=False):
                pe.wait_ge(moments, j + 1)
                ins = nc.tensor.matmul(pn[:, 0:2 * n], cc("channel" if j in (2, INJOB) else "group"),
                                       mom[:, 0:n, :].rearrange("p n s -> p (n s)"), start=True, stop=True)
                if pooled:
                    ins = nc.tensor.matmul(pn[:, 2:4], cc("channel"), mom[:, 0:1, :].rearrange("p n s -> p (n s)"),
                                           start=True, stop=True)
                ins.then_inc(group_sums, 1)

            pe.wait_ge(const_in, 16)
            stats(0, 1)
            pe.wait_ge(frow_ready, 1)
            for i in range(4):
                last = nc.tensor.matmul(pw[:, i:i + 1], frows[0:1, i, :], cc("one")[0:1, :], start=True, stop=True)
            last.then_inc(fcol_ready, 1)
            pe.wait_ge(fw_split, 1)
            pe.wait_ge(zeros_set, 2)

            def reached(rounds):
                return {(t % 2, REACH[t % 2][t // 4][i]) for _, products in rounds for t, i in products}

            def conv(k, quad, freed=None):
                pair, kind = k // 3, k % 3
                slot = [(2 * pair + j) % SLOTS for j in range(2)]
                if kind == 0:
                    for j in range(2):
                        pe.wait_ge(patch_in[slot[j]], quad * 64 + 64)
                for i in range(HALVES):
                    if freed is not None:
                        pe.wait_ge(power_done, freed + (i + 1))
                    if kind < 2:
                        tiles = [(0, P, slot[i], kind, 128 * kind)]
                    else:
                        tiles = [(64 * j, 64, slot[j], i, 256 + 64 * i) for j in range(2)]
                    mm = 0
                    for kt in range(2):
                        for wt, h in ((0, 0), (0, 1), (1, 0)):
                            for at, n, sl, half, w in tiles:
                                last = nc.tensor.matmul(
                                    pc[at:at + n, 2 * (k % 2) + i, :], fwx[:, wt, kt, w:w + n],
                                    patch[:, sl, 8 * half:8 * half + 8, h, 4 * kt:4 * kt + WR],
                                    start=(mm == 0), stop=(mm == 5))
                            mm += 1
                    last.then_inc(conv_done, 1)

            def mix(g, cq, k, first=False, final=False):
                body = g * CQ + cq
                if first and k == 1:
                    pe.wait_ge(y_out, g + 1)
                if k == 1:
                    pe.wait_ge(w1x_ready, body + 1)
                if k in (1, 4, 5):
                    pe.wait_ge(maghl_done, body * MAGS + {1: 2, 4: 4, 5: 5}[k])
                for r, (step, products) in enumerate(ROUNDS):
                    if step != k:
                        continue
                    for wt, h in ((0, 0), (0, 1), (1, 0)):
                        for tile, i in products:
                            half, c4 = tile % 2, tile // 4
                            phase = REACH[half][c4][i]
                            unit = 12 + 2 * half + i if c4 else 6 * half + 3 * (tile // 2) + i
                            opens = first and (half, phase) not in reached(ROUNDS[:r])
                            closes = final and (half, phase) not in reached(ROUNDS[r + 1:])
                            last = nc.tensor.matmul(py[32 * phase:32 * phase + 32, half, :], w1x[:, wt, unit, :],
                                                    mhl[:, h, tile, :], start=opens and wt == h == 0,
                                                    stop=closes and wt == 1)
                if k == 5:
                    last.then_inc(mixed, 1)

            def zeros(to, start, stop):
                return nc.tensor.matmul(to, zero16[:, :], zero16[:, :].unsqueeze(1).broadcast_to([P, 4, P]),
                                        start=start, stop=stop)

            def step(g, cq, s, ahead=True, first=False, final=False):
                if ahead:
                    conv(s + 3, g * CQ + cq + (s + 3) // BODY,
                         g * (HALVES * STEPS) + cq * (HALVES * BODY) + HALVES * (s + 1))
                mix(g, cq, s, first, final)

            conv(0, 0)
            conv(1, 0)
            conv(2, 0, 0)
            pe.wait_ge(w1_split, 1)
            for run, (g0, g1) in enumerate(RUNS):
                with pe.Fori(g0, g1) as g:
                    for s in range(BODY):
                        step(g, 0, s, first=True)
                    with pe.Fori(1, CQ - 1) as cq:
                        for s in range(BODY):
                            step(g, cq, s)
                    for s in range(BODY):
                        step(g, CQ - 1, s, final=True)
                if run == 2:
                    stats(1, B - 1)
                elif run == XSUM + 1:
                    stats(2, B - 1)
                elif run == XSUM + 3:
                    stats(job(0), 1)
            g = NG - 1
            for s in range(BODY):
                step(g, 0, s, first=True)
            with pe.Fori(1, CQ - 1) as cq:
                for s in range(BODY):
                    step(g, cq, s)
            for s in range(BODY):
                step(g, CQ - 1, s, ahead=s < BODY - 3, final=True)

            pe.wait_ge(lw_split, 1)

            def window_sum(k, to, row, rows, done=True):
                layer, b = JOBS[k]
                nx, cols = (3, WR + 1) if layer == 1 else (3, WR)
                total, mm = 3 * (K1 if layer == 1 else K2), 0
                for s in range(total // 3):
                    sy, sx = s // nx, s % nx
                    if layer == 1:
                        hi, lo = lwh[:, s, :], lwl[:, s, :]
                    else:
                        hi, lo = W2h[:, b % 2, s, :], W2l[:, b % 2, s, :]
                    for wt, h in ((hi, 0), (hi, 1), (lo, 0)):
                        last = nc.tensor.matmul(to, wt, PH[:, k % 2, h, bass.ds(row + sy, rows), sx:sx + cols],
                                                start=(mm == 0), stop=(mm == total - 1))
                        mm += 1
                last.then_inc(tile_done, 1)

            def tiles(k, first, n):
                layer, b = JOBS[k]
                if first == 0:
                    pe.wait_ge(lo_done, k + 1)
                    pe.wait_ge(bordered, min(k + 1, B + 2))
                    if layer == 2:
                        pe.wait_ge(filters_ready, b + 1)
                rows, cols = (7, WR + 1) if layer == 1 else (8, WR)
                at = first % 4
                freed = FREE + at + 1 + ((TILES_BEFORE[k - 1] + 4 if k else -6) if first < 4 else TILES_BEFORE[k])
                with pe.Fori(0, n) as i:
                    pe.wait_ge(tile_out, i + freed)
                    window_sum(k, pc[:, bass.ds(i + at, 1), 0:rows * cols].rearrange("p o n -> p (o n)"),
                               i * rows + first * rows, rows)

            def leftover(k):
                layer = JOBS[k][0]
                for i in range(8, len(TILES[layer])):
                    row, n = TILES[layer][i]
                    if k:
                        pe.wait_ge(tile_out, FREE + TILES_BEFORE[k])
                    window_sum(k, bank(i)[:, 0:n * (WR + 1 if layer == 1 else WR)], row, n)

            def hidden_sum(b):
                if b == 0:
                    pe.wait_ge(v_in, 32)
                pe.wait_ge(pool_ready, b + 1)
                nc.tensor.matmul(pw[:, 8:9], v1s[:, :], pool[0:C, 0:1], start=True, stop=True).then_inc(hid_sum, 1)

            def taps_sum(b):
                pe.wait_ge(hid_ready, b + 1)
                for t in range(TAPS):
                    last = nc.tensor.matmul(pw[:, 16 + t:17 + t], v2s[:, t, :], hid[:, :], start=True, stop=True)
                last.then_inc(k_sum, 1)

            for k in range(2 * B):
                following = k + 1 < 2 * B
                adaptive = following and JOBS[k + 1][0] == 2
                tiles(k, 0, 2)
                if k == 0:
                    stats(INJOB, 1)
                elif following:
                    stats(job(k + 1), 1, pooled=adaptive)
                tiles(k, 2, 2)
                if k == 0:
                    stats(job(1), 1)
                elif adaptive:
                    hidden_sum(JOBS[k + 1][1])
                tiles(k, 4, 1)
                if adaptive:
                    taps_sum(JOBS[k + 1][1])
                tiles(k, 5, 3)
                leftover(k)
            stats(LASTJOB, B)

            pe.wait_ge(tile_out, FREE + TILES_BEFORE[2 * B])
            for m in range(4):
                zeros(pc[:, m, :], True, False)

            def transposes(t, s):
                pe.wait_ge(xg_ready, t + 1)
                for i in range(2 * B):
                    last = nc.tensor.transpose(py16[:, s % 2, i * P:(i + 1) * P],
                                               xhl[:, s % 2, i // B, i % B * P:(i % B + 1) * P], ident16[:, :])
                last.then_inc(xT_done, 1)

            def spectrum(t, s, t4):
                pe.wait_ge(xT_out, t + 1)
                pe.wait_ge(bas_in[s], t4 * 16 + 16)
                for m in range(4):
                    for wt, h in ((0, 0), (0, 1), (1, 0)):
                        last = nc.tensor.matmul(pc[:, m, :], bas[:, s, wt, m * P:(m + 1) * P],
                                                xT[:, s % 2, h * B * P:(h + 1) * B * P], start=False, stop=False)
                last.then_inc(spec_tile, 1)

            pe.wait_ge(ident_ready, 1)
            transposes(0, 0)
            with pe.Fori(0, TT // 4 - 1) as t4:
                for s in range(4):
                    transposes(t4 * 4 + (s + 1), (s + 1) % 4)
                    spectrum(t4 * 4 + s, s, t4)
            t4 = TT // 4 - 1
            for s in range(4):
                if s < 3:
                    transposes(t4 * 4 + s + 1, s + 1)
                spectrum(t4 * 4 + s, s, t4)
            for m in range(4):
                last = zeros(pc[:, m, :], False, True)
            last.then_inc(spec_done, 1)
            pe.wait_ge(G_ready, 2)
            perm = cc("mirror").rearrange("p (i o m) -> p i o m", i=2, o=2)
            for o in range(2):
                for i in range(2):
                    last = nc.tensor.matmul(pn[:, o * P:(o + 1) * P], perm[:, i, o, :], G[:, i, :],
                                            start=(i == 0), stop=(i == 1))
            last.then_inc(Gn_ready, 1)
            for i, (b, n) in enumerate(INVERSE):
                pe.wait_ge(LL_ready, b + 1)
                pe.wait_ge(ibas_in[n % IBAS], 16 * (n // IBAS + 1))
                if i >= 4:
                    pe.wait_ge(inv_out, i - 3)
                mm = 0
                for m in range(4):
                    for wt, h in ((0, 0), (0, 1), (1, 0)):
                        last = nc.tensor.matmul(pc[:, i % 4, :], LLhl[:, b, wt, m, :], ibas[n % IBAS][:, h, m, :],
                                                start=(mm == 0), stop=(mm == 11))
                        mm += 1
                last.then_inc(inv_done, 1)


def _const_columns():
    widths = [("group", P), ("channel", P), ("ident", P), ("mirror", 4 * P), ("taps", TAPS * 4 * K2), ("chan", C),
              ("cosw", 8), ("sinw", 8), ("cos", 8), ("sin", 8), ("one", 1), ("b1", 1), ("vb1", 1), ("vb2", TAPS)]
    at, where = 0, {}
    for name, n in widths:
        where[name] = (at, n)
        at += n
    return where, at


CONST_AT, CONST_COLS = _const_columns()


def _shape_constants():
    p = np.arange(P)
    chan, ph = p % C, p // C
    parts = {}
    parts["group"] = (chan[:, None] // 2 == chan[None, :] // 2) / 8.0
    parts["channel"] = (chan[:, None] == chan[None, :]) / 4.0
    parts["ident"] = np.eye(P)
    parts["chan"] = (chan[:, None] == np.arange(C)[None, :]) * 1.0
    parts["one"] = np.ones((P, 1))
    m = np.arange(MODES * MODES)
    minus = (-(m // MODES)) % MODES * MODES + (-(m % MODES)) % MODES
    full = np.zeros((2 * P, 2 * P))
    full[minus, m] = 1.0
    parts["mirror"] = full.reshape(2, P, 2, P).transpose(1, 0, 2, 3).reshape(P, 4 * P)
    taps = np.zeros((P, TAPS, K2, 2, 2))
    for q in range(4):
        for s in range(K2):
            for a in range(2):
                for e in range(2):
                    dy = 2 * (s // 3) + q // 2 - (2 - a) + 1
                    dx = 2 * (s % 3 - 1) + q % 2 - e + 1
                    if 0 <= dy < 3 and 0 <= dx < 3:
                        taps[ph == q, 3 * dy + dx, s, a, e] = 1.0
    parts["taps"] = taps.reshape(P, -1)
    k1, k2 = (m // MODES).reshape(2, P), (m % MODES).reshape(2, P)
    for name, f in (("cos", np.cos), ("sin", np.sin)):
        table = [[f(2 * math.pi * (k1[kt] * (g // 2) + k2[kt] * (g % 2)) / H) for g in range(4)] for kt in range(2)]
        parts[name] = np.array(table).transpose(2, 0, 1).reshape(P, 8)
        parts[name + "w"] = parts[name] / H
    return parts


def _bases():
    m = np.arange(MODES * MODES)
    pos = np.arange(NPIX)
    turns = (m[:, None] // MODES * (pos[None, :] // WR) + m[:, None] % MODES * (pos[None, :] % WR)) % HR
    angle = 2 * math.pi * turns / HR
    cas = np.stack([np.cos(angle) + np.sin(angle), np.cos(angle) - np.sin(angle)]).reshape(4, P, NPIX)
    high = cas.astype(np.float16)
    parts = np.stack([high, (cas - high).astype(np.float16)])
    basis = parts.reshape(2, 4 * P, TT, P).transpose(2, 3, 0, 1).reshape(TT, P, 2 * 4 * P)
    ibasis = parts.reshape(2, 4, P, NCH, CHUNK).transpose(3, 2, 0, 1, 4).reshape(NCH, P, 2 * 4 * CHUNK)
    return np.ascontiguousarray(basis), np.ascontiguousarray(ibasis)


def _phases(v):
    v = v.reshape(B, C, HR, 2, WR, 2).transpose(3, 5, 1, 0, 2, 4)
    return np.ascontiguousarray(v).reshape(P, B * NPIX)


def _filters(f):
    out = np.zeros((P, 2, 2, 2, 2, SO), f.dtype)
    for p in range(P):
        i2, plane, j2 = p // 4 % 8, p // 32, p % 4
        i, j = 2 * i2 + plane // 2, 2 * j2 + plane % 2
        for kt in range(2):
            for a in range(2):
                for e in range(2):
                    dx, dy = i - a, 8 * kt + j - e
                    if 0 <= dx < KF and 0 <= dy < KF:
                        out[p, kt, :, a, e, :] = f[:, :, dy, dx].T
    return out.reshape(P, 4 * M0)


def _mix(w):
    one = np.zeros((C, 4, SO, 4, C), w.dtype)
    for g in range(4):
        one[:, g, :, g, :] = w.reshape(C, C, SO).transpose(1, 2, 0)
    one = one.reshape(CQ, SLOTS, M0, 4, C)
    out = np.empty((P, CQ, UNITS, C), w.dtype)
    unit = 0
    for channels, half, c4 in [(slice(2 * p, 2 * p + 2), half, 0) for half in range(2) for p in range(2)] + \
            [(slice(0, 4), half, 1) for half in range(2)]:
        outputs = np.concatenate([np.arange(first, first + n) for first, n in OUTPUTS[half][c4]])
        rows = one[:, channels][:, :, outputs].reshape(CQ, P, 4, C)
        for phase in REACH[half][c4]:
            out[:, :, unit] = rows[:, :, phase].transpose(1, 0, 2)
            unit += 1
    return out.reshape(P, CQ * UNITS * C)


def _blocks(w):
    out = np.zeros((2, 2, C, 3, 3, 2, 2, C), w.dtype)
    for a in range(2):
        for e in range(2):
            for sy in range(3):
                for sx in range(3):
                    for oa in range(2):
                        for oe in range(2):
                            i = 3 - (2 * sy + a - (2 - oa))
                            j = 3 - (2 * sx + e - (2 - oe))
                            if 0 <= i < 5 and 0 <= j < 5:
                                out[a, e, :, sy, sx, oa, oe, :] = w[:, :, i, j].T
    return out.reshape(P, K1 * P)


def _modes(w):
    n = np.roll(np.flip(w, (-2, -1)), (1, 1), (-2, -1))
    return [np.ascontiguousarray(v.transpose(2, 3, 1, 0)).reshape(2, P, C * C) for v in (w, n)]


def kernel(x, L0_conv_filters, L0_conv_w1, L0_conv_b1, L1_conv_weight, L2_conv_w1, L2_conv_b1, L2_conv_w2,
           L2_conv_b2, L3_conv_weights1):
    import concourse.bacc as bacc
    from concourse.bass_utils import run_bass_kernel_spmd

    x = np.asarray(x)
    parts = _shape_constants()
    parts["b1"] = np.tile(np.asarray(L0_conv_b1), 4)[:, None]
    parts["vb1"] = np.asarray(L2_conv_b1)[:, None]
    parts["vb2"] = np.tile(np.asarray(L2_conv_b2).reshape(C, TAPS), (4, 1))
    const = np.zeros((P, CONST_COLS), np.float32)
    for name, (at, n) in CONST_AT.items():
        const[:, at:at + n] = parts[name]
    basis, ibasis = _bases()
    w3, w3n = _modes(np.asarray(L3_conv_weights1))
    arrays = {
        "xt": _phases(x.transpose(0, 1, 3, 2)),
        "xn": _phases(x),
        "fw": _filters(np.asarray(L0_conv_filters)),
        "w1": _mix(np.asarray(L0_conv_w1)),
        "lw": _blocks(np.asarray(L1_conv_weight)),
        "v1": np.ascontiguousarray(L2_conv_w1),
        "v2": np.ascontiguousarray(np.tile(np.asarray(L2_conv_w2).reshape(P, C, TAPS).transpose(0, 2, 1),
                                           (1, 1, 4))).reshape(P, TAPS * P),
        "w3": w3,
        "w3n": w3n,
        "const": const,
        "basis": basis,
        "ibasis": ibasis,
    }
    nc = bacc.Bacc("TRN2", target_bir_lowering=False, num_devices=1)
    t = {n: nc.dram_tensor(n, a.shape, F16 if a.dtype == np.float16 else F32, kind="ExternalInput").ap()
         for n, a in arrays.items()}
    out = nc.dram_tensor("out", (P, B * NPIX), F32, kind="ExternalOutput").ap()
    build(nc, t["xt"], t["xn"], t["fw"], t["w1"], t["lw"], t["v1"], t["v2"], t["w3"], t["w3n"],
          t["const"], t["basis"], t["ibasis"], out)
    r = run_bass_kernel_spmd(nc, [arrays], core_ids=[0])
    got = r.results[0]["out"].reshape(2, 2, C, B, HR, WR).transpose(3, 2, 4, 0, 5, 1)
    return np.ascontiguousarray(got).reshape(B, C, H, W)
```
